# Optimizing a Trainium2 kernel written in Bass

```python
import numpy as np
import jax
import jax.numpy as jnp

def _softmax(x, axis=-1):
    return jax.nn.softmax(x, axis=axis)

def _gelu(x):
    return jax.nn.gelu(x, approximate=True)

def _silu(x):
    return jax.nn.silu(x)

def _sigmoid(x):
    return jax.nn.sigmoid(x)

def _layernorm(x, axis=-1, eps=1e-05):
    m = jnp.mean(x, axis=axis, keepdims=True)
    v = jnp.var(x, axis=axis, keepdims=True)
    return (x - m) / jnp.sqrt(v + eps)

def _scatter_add(tgt, idx, src, axis=0):
    return tgt.at[idx].add(src)

def _segment_sum(src, seg, n):
    return jax.ops.segment_sum(src, seg, n)
kernel_name = 'mk_adj_preln_d4_adj_r2_351b7c'

def setup_inputs(seed: int=0):
    np.random.seed(seed)
    _w = jnp.asarray

    def _rec_inputs():
        import jax
        import jax.numpy as jnp
        _gk = jax.random.key(seed)
        x = -0.0005207 + 1.001 * jax.random.normal(jax.random.fold_in(_gk, 1), (3327, 256), jnp.float32)
        _a = jax.random.bernoulli(jax.random.fold_in(_gk, 2), 0.00480914, (3327, 3327))
        _a = jnp.logical_or(_a, jnp.swapaxes(_a, -1, -2))
        _a = jnp.logical_or(_a, jnp.eye(3327, dtype=bool))
        _af = _a.astype(jnp.float32)
        _af = _af * jax.random.uniform(jax.random.fold_in(_gk, 3), (3327, 3327), jnp.float32, 0.05, 5.41998)
        adj = _af
        return (x, adj)
    x, adj = _rec_inputs()

    def _L0_gnn_setup():
        import jax, jax.numpy as jnp
        import numpy as np
        N = 2048
        DIM_IN = 256
        DIM_Q = 256
        DIM_K = 256
        N_GRAPHS = 32
        key = jax.random.key(seed)
        ks = jax.random.split(key, 9)
        x = jax.random.normal(ks[0], (N, DIM_IN), dtype=jnp.float32)
        b = jax.random.normal(ks[1], (N, N), dtype=jnp.float32)
        edge_encoding = jax.random.normal(ks[2], (N, N), dtype=jnp.float32)
        ptr = jnp.arange(N_GRAPHS + 1, dtype=jnp.int64) * (N // N_GRAPHS)
        s_in = 1.0 / np.sqrt(DIM_IN)
        Wq = jax.random.normal(ks[3], (DIM_Q, DIM_IN), dtype=jnp.float32) * s_in
        bq = jnp.zeros((DIM_Q,), dtype=jnp.float32)
        Wk = jax.random.normal(ks[4], (DIM_K, DIM_IN), dtype=jnp.float32) * s_in
        bk = jnp.zeros((DIM_K,), dtype=jnp.float32)
        Wv = jax.random.normal(ks[5], (DIM_K, DIM_IN), dtype=jnp.float32) * s_in
        bv = jnp.zeros((DIM_K,), dtype=jnp.float32)
        return {'x': x, 'b': b, 'edge_encoding': edge_encoding, 'ptr': ptr, 'Wq': Wq, 'bq': bq, 'Wk': Wk, 'bk': bk, 'Wv': Wv, 'bv': bv}
    _L0_gnn_all = _L0_gnn_setup()
    _L0_gnn_in = {k: v for k, v in _L0_gnn_all.items() if k in ('ptr', 'Wq', 'bq', 'Wk', 'bk', 'Wv', 'bv')}
    del _L0_gnn_all

    def _L1_gnn_setup():
        import jax, jax.numpy as jnp
        import numpy as np
        N_HEADS = 4
        N_HIDDEN = 256
        SLOPE = 0.01
        NEG = -1000000000.0
        key = jax.random.key(seed)
        k1, k2, k3, k4 = jax.random.split(key, 4)
        N, F_IN = (4096, 256)
        h = jax.random.normal(k1, (N, F_IN), dtype=jnp.float32)
        W = jax.random.normal(k2, (F_IN, N_HIDDEN * N_HEADS), dtype=jnp.float32) * 0.05
        a = jax.random.normal(k3, (N_HEADS, 2 * N_HIDDEN, 1), dtype=jnp.float32) * 0.05
        adj_mat = jnp.where(jax.random.uniform(k4, (N, N)) < 0.01, 0.0, NEG).astype(jnp.float32)
        return {'h': h, 'adj_mat': adj_mat, 'W': W, 'a': a}
    _L1_gnn_all = _L1_gnn_setup()
    _L1_gnn_in = {k: v for k, v in _L1_gnn_all.items() if k in ('W', 'a')}
    del _L1_gnn_all

    def _L2_gnn_setup():
        import jax, jax.numpy as jnp
        import numpy as np
        N = 4096
        D = 256
        key = jax.random.key(seed)
        ks = jax.random.split(key, 6)
        s = 1.0 / np.sqrt(D)
        return {'x': jax.random.normal(ks[0], (N, D), jnp.float32), 'spatial_encoding': jax.random.normal(ks[1], (N, N), jnp.float32), 'edge_encoding': jax.random.normal(ks[2], (N, N), jnp.float32), 'Wq': jax.random.normal(ks[3], (D, D), jnp.float32) * s, 'bq': jnp.zeros((D,), jnp.float32), 'Wk': jax.random.normal(ks[4], (D, D), jnp.float32) * s, 'bk': jnp.zeros((D,), jnp.float32), 'Wv': jax.random.normal(ks[5], (D, D), jnp.float32) * s, 'bv': jnp.zeros((D,), jnp.float32)}
    _L2_gnn_all = _L2_gnn_setup()
    _L2_gnn_in = {k: v for k, v in _L2_gnn_all.items() if k in ('Wq', 'bq', 'Wk', 'bk', 'Wv', 'bv')}
    del _L2_gnn_all

    def _L3_gnn_setup():
        import jax, jax.numpy as jnp
        import numpy as np
        KAPPA = -1.0
        EPS = 1e-10
        N, D_IN, D_OUT = (4096, 256, 256)

        def _artan_k(x):
            sc = np.sqrt(-KAPPA)
            return jnp.arctanh(jnp.clip(sc * x, -1.0 + 1e-07, 1.0 - 1e-07)) / sc

        def _tan_k(x):
            sc = np.sqrt(-KAPPA)
            return jnp.tanh(sc * x) / sc

        def _clamp_abs(x, eps=EPS):
            return jnp.where(x >= 0, 1.0, -1.0) * jnp.maximum(jnp.abs(x), eps)

        def _norm(x):
            return jnp.sqrt(jnp.maximum(jnp.sum(x * x, axis=-1, keepdims=True), EPS * EPS))

        def mobius_matvec(W, x):
            x_norm = _norm(x)
            mx = x @ W
            mx_norm = _norm(mx)
            res = _tan_k(mx_norm / x_norm * _artan_k(x_norm)) * (mx / mx_norm)
            return jnp.where(mx_norm <= EPS, 0.0, res)

        def mobius_scalar_mul(r, x):
            x_norm = _norm(x)
            return _tan_k(r * _artan_k(x_norm)) * (x / x_norm)

        def weighted_midpoint_lincomb(A, X):
            gamma = jnp.maximum(2.0 / (1.0 + KAPPA * jnp.sum(X * X, axis=-1, keepdims=True)), 1e-15)
            denom = _clamp_abs(A @ (gamma - 1.0))
            nom = A @ (gamma * X)
            two_mean = nom / denom
            sq = jnp.sum(two_mean * two_mean, axis=-1, keepdims=True)
            a_mean = two_mean / (1.0 + jnp.sqrt(jnp.maximum(1.0 + KAPPA * sq, EPS)))
            alpha = jnp.sum(A, axis=-1, keepdims=True)
            return mobius_scalar_mul(alpha, a_mean)

        def logmap0(x):
            xn = _norm(x)
            return _artan_k(xn) * x / xn

        def expmap0(u):
            un = _norm(u)
            return _tan_k(un) * u / un
        key = jax.random.key(seed)
        k1, k2, k3 = jax.random.split(key, 3)
        X = jax.random.normal(k1, (N, D_IN), dtype=jnp.float32) * 0.001
        A_hat = jax.random.uniform(k2, (N, N), dtype=jnp.float32) / N
        W = jax.random.normal(k3, (D_IN, D_OUT), dtype=jnp.float32) * 0.01
        return {'X': X, 'A_hat': A_hat, 'W': W}
    _L3_gnn_all = _L3_gnn_setup()
    _L3_gnn_in = {k: v for k, v in _L3_gnn_all.items() if k in ('W',)}
    del _L3_gnn_all
    return {'x': x, 'adj': adj, 'L0_gnn_ptr': _L0_gnn_in['ptr'], 'L0_gnn_Wq': _L0_gnn_in['Wq'], 'L0_gnn_bq': _L0_gnn_in['bq'], 'L0_gnn_Wk': _L0_gnn_in['Wk'], 'L0_gnn_bk': _L0_gnn_in['bk'], 'L0_gnn_Wv': _L0_gnn_in['Wv'], 'L0_gnn_bv': _L0_gnn_in['bv'], 'L1_gnn_W': _L1_gnn_in['W'], 'L1_gnn_a': _L1_gnn_in['a'], 'L2_gnn_Wq': _L2_gnn_in['Wq'], 'L2_gnn_bq': _L2_gnn_in['bq'], 'L2_gnn_Wk': _L2_gnn_in['Wk'], 'L2_gnn_bk': _L2_gnn_in['bk'], 'L2_gnn_Wv': _L2_gnn_in['Wv'], 'L2_gnn_bv': _L2_gnn_in['bv'], 'L3_gnn_W': _L3_gnn_in['W']}

def reference(x, adj, L0_gnn_ptr, L0_gnn_Wq, L0_gnn_bq, L0_gnn_Wk, L0_gnn_bk, L0_gnn_Wv, L0_gnn_bv, L1_gnn_W, L1_gnn_a, L2_gnn_Wq, L2_gnn_bq, L2_gnn_Wk, L2_gnn_bk, L2_gnn_Wv, L2_gnn_bv, L3_gnn_W):
    import jax
    import jax.numpy as jnp

    def _L0_gnn_ref(x, b, edge_encoding, ptr, Wq, bq, Wk, bk, Wv, bv):
        import jax, jax.numpy as jnp
        import numpy as np
        N = 2048
        DIM_IN = 256
        DIM_Q = 256
        DIM_K = 256
        N_GRAPHS = 32
        n = x.shape[0]
        graph_id = jnp.searchsorted(ptr, jnp.arange(n), side='right') - 1
        mask = graph_id[:, None] == graph_id[None, :]
        query = x @ Wq.T + bq
        key = x @ Wk.T + bk
        value = x @ Wv.T + bv
        scale = 1.0 / jnp.sqrt(jnp.float32(query.shape[-1]))
        a = jnp.where(mask, query @ key.T * scale, 0.0)
        scores = (a + b + edge_encoding) * jnp.where(mask, 1.0, -1000000.0)
        softmax = jax.nn.softmax(scores, axis=-1) * mask
        return softmax @ value

    def _L1_gnn_ref(h, adj_mat, W, a):
        import jax, jax.numpy as jnp
        import numpy as np
        N_HEADS = 4
        N_HIDDEN = 256
        SLOPE = 0.01
        NEG = -1000000000.0
        N = h.shape[0]
        ht = (h @ W).reshape(N, N_HEADS, N_HIDDEN).transpose(1, 0, 2)
        a_src = a[:, :N_HIDDEN, 0]
        a_dst = a[:, N_HIDDEN:, 0]
        src = jnp.einsum('hnd,hd->hn', ht, a_src)
        dst = jnp.einsum('hnd,hd->hn', ht, a_dst)
        e = jax.nn.leaky_relu(src[:, :, None] + dst[:, None, :], SLOPE) + adj_mat[None]
        att = jax.nn.softmax(e, axis=-1)
        h_prime = jnp.einsum('hij,hjd->hid', att, ht)
        return h_prime.mean(axis=0)

    def _L2_gnn_ref(x, spatial_encoding, edge_encoding, Wq, bq, Wk, bk, Wv, bv):
        import jax, jax.numpy as jnp
        import numpy as np
        N = 4096
        D = 256
        q = x @ Wq.T + bq
        k = x @ Wk.T + bk
        v = x @ Wv.T + bv
        scale = 1.0 / jnp.sqrt(jnp.asarray(q.shape[-1], q.dtype))
        a = q @ k.T * scale + spatial_encoding + edge_encoding
        attn = jax.nn.softmax(a, axis=-1)
        return attn @ v

    def _L3_gnn_ref(X, A_hat, W):
        import jax, jax.numpy as jnp
        import numpy as np
        KAPPA = -1.0
        EPS = 1e-10
        N, D_IN, D_OUT = (4096, 256, 256)

        def _artan_k(x):
            sc = np.sqrt(-KAPPA)
            return jnp.arctanh(jnp.clip(sc * x, -1.0 + 1e-07, 1.0 - 1e-07)) / sc

        def _tan_k(x):
            sc = np.sqrt(-KAPPA)
            return jnp.tanh(sc * x) / sc

        def _clamp_abs(x, eps=EPS):
            return jnp.where(x >= 0, 1.0, -1.0) * jnp.maximum(jnp.abs(x), eps)

        def _norm(x):
            return jnp.sqrt(jnp.maximum(jnp.sum(x * x, axis=-1, keepdims=True), EPS * EPS))

        def mobius_matvec(W, x):
            x_norm = _norm(x)
            mx = x @ W
            mx_norm = _norm(mx)
            res = _tan_k(mx_norm / x_norm * _artan_k(x_norm)) * (mx / mx_norm)
            return jnp.where(mx_norm <= EPS, 0.0, res)

        def mobius_scalar_mul(r, x):
            x_norm = _norm(x)
            return _tan_k(r * _artan_k(x_norm)) * (x / x_norm)

        def weighted_midpoint_lincomb(A, X):
            gamma = jnp.maximum(2.0 / (1.0 + KAPPA * jnp.sum(X * X, axis=-1, keepdims=True)), 1e-15)
            denom = _clamp_abs(A @ (gamma - 1.0))
            nom = A @ (gamma * X)
            two_mean = nom / denom
            sq = jnp.sum(two_mean * two_mean, axis=-1, keepdims=True)
            a_mean = two_mean / (1.0 + jnp.sqrt(jnp.maximum(1.0 + KAPPA * sq, EPS)))
            alpha = jnp.sum(A, axis=-1, keepdims=True)
            return mobius_scalar_mul(alpha, a_mean)

        def logmap0(x):
            xn = _norm(x)
            return _artan_k(xn) * x / xn

        def expmap0(u):
            un = _norm(u)
            return _tan_k(un) * u / un
        XW = mobius_matvec(W, X)
        AXW = weighted_midpoint_lincomb(A_hat, XW)
        return expmap0(jax.nn.relu(logmap0(AXW)))
    h = jnp.maximum(_layernorm(x, axis=-1), 0.0)
    x = x + _L0_gnn_ref(h, adj, adj, L0_gnn_ptr, L0_gnn_Wq, L0_gnn_bq, L0_gnn_Wk, L0_gnn_bk, L0_gnn_Wv, L0_gnn_bv)
    h = jnp.maximum(_layernorm(x, axis=-1), 0.0)
    x = x + _L1_gnn_ref(h, adj, L1_gnn_W, L1_gnn_a)
    h = jnp.maximum(_layernorm(x, axis=-1), 0.0)
    x = x + _L2_gnn_ref(h, adj, adj, L2_gnn_Wq, L2_gnn_bq, L2_gnn_Wk, L2_gnn_bk, L2_gnn_Wv, L2_gnn_bv)
    h = jnp.maximum(_layernorm(x, axis=-1), 0.0)
    x = x + _L3_gnn_ref(h, adj, L3_gnn_W)
    return x

_drawn_inputs = setup_inputs


def setup_inputs(seed=0):
    import zlib

    import numpy as np

    out = dict(_drawn_inputs(seed))
    spreads = {'L0_gnn_bq': (0.0, 0.8),
     'L0_gnn_bk': (0.0, 0.8),
     'L0_gnn_bv': (0.0, 0.1),
     'L2_gnn_bq': (0.0, 0.8),
     'L2_gnn_bk': (0.0, 0.8),
     'L2_gnn_bv': (0.0, 0.1)}
    factors = {'L1_gnn_a': 8.0}
    for name, (base, spread) in spreads.items():
        noise = np.random.default_rng([zlib.crc32(name.encode()), seed]).standard_normal(out[name].shape)
        drawn = base * np.exp(spread * noise) if base else spread * noise
        out[name] = jnp.asarray(drawn.astype(out[name].dtype))
    for name, factor in factors.items():
        out[name] = (out[name] * factor).astype(out[name].dtype)
    return out
```

```python
from contextlib import ExitStack

import numpy as np
import concourse.bass as bass
from concourse import mybir

ALU = mybir.AluOpType
ACT = mybir.ActivationFunctionType
AX = mybir.AxisListType
F32 = mybir.dt.float32
F16 = mybir.dt.float16
BF16 = mybir.dt.bfloat16
I32 = mybir.dt.int32

P = 128
N = 3327
D = 256
NT = (N + P - 1) // P
NP = NT * P
HEADS = 4
NG = 33
W = 512
NB = NP // W
TAIL = NP - NB * W
NGRP = NT // 2
HALF = NP // 2
BIG = float(2.0 ** 100)
EPS = 1e-5
LOG_P = float(np.log(256.0))


class Mem:
    pass


def cols(start, size):
    return bass.ds(start, size)


def chunks(total, size):
    return [(a, min(size, total - a)) for a in range(0, total, size)]


def wait_apart(eng, sem, value, waited):
    eng.wait_ge(sem, value)
    eng.sem_inc(waited, 1)


def setup(nc, ctx, m, io):
    def sb(n, s, d=F32):
        return ctx.enter_context(nc.sbuf_tensor(n, s, d))

    m.x = sb("state", [P, NT * D])
    m.ident = sb("ident", [P, P])
    m.identb = sb("identb", [P, P], BF16)
    m.ones = sb("ones", [P, P])
    m.padneg = sb("padneg", [P, 1])
    m.rstd = sb("rstd", [P, NT])
    m.nbias = sb("nbias", [P, NT])
    x_cleared, x_body, x_last, set_steps, pool_steps = (
        nc.alloc_semaphore(n) for n in ("x_cleared", "x_body", "x_last", "set_steps", "pool_steps"))
    with nc.sbuf_tensor("pidx", [P, 1], F32) as pidx, nc.Block() as block:
        xt = m.x[:].rearrange("p (t d) -> p t d", t=NT)

        @block.sync
        def _(sp):
            sp.dma_start(xt[:, 0:NT - 1, :],
                         io.x[0:(NT - 1) * P, :].rearrange("(t p) d -> p t d", p=P)).then_inc(x_body, 16)
            sp.wait_ge(x_cleared, 1)
            sp.dma_start(xt[0:N - (NT - 1) * P, NT - 1, :], io.x[(NT - 1) * P:N, :]).then_inc(x_last, 16)
            sp.wait_ge(x_body, 16)
            sp.wait_ge(x_last, 16)

        @block.gpsimd
        def _(pool):
            pool.iota(pidx[:], pattern=[[0, 1]], base=0, channel_multiplier=1,
                      allow_small_or_imprecise_dtypes=True).then_inc(pool_steps, 1)
            pool.memset(m.ident[:], 0.0).then_inc(pool_steps, 1)
            pool.wait_ge(pool_steps, 2)
            pool.affine_select(out=m.ident[:], in_=m.ident[:], compare_op=ALU.not_equal, fill=1.0,
                               base=0, pattern=[[-1, P]], channel_multiplier=1).then_inc(pool_steps, 1)

        @block.vector
        def _(dve):
            dve.memset(xt[:, NT - 1, :], 0.0).then_inc(x_cleared, 1)
            dve.memset(m.ones[:], 1.0).then_inc(set_steps, 1)
            dve.wait_ge(pool_steps, 3)
            dve.tensor_copy(m.identb[:], m.ident[:]).then_inc(set_steps, 1)
            dve.tensor_scalar(m.padneg[:], pidx[:], float(P - 1), -1e30, ALU.is_ge,
                              ALU.mult).then_inc(set_steps, 1)


def norm(nc, m, name, split, haug, hlow):
    width = D + 2
    with ExitStack() as ctx:
        def sb(n, s, d=F32):
            return ctx.enter_context(nc.sbuf_tensor(f"{name}_{n}", s, d))

        def sem(n):
            return nc.alloc_semaphore(f"{name}_{n}")

        stat = sb("stat", [P, 2 * 6])
        mv = sb("mv", [P, 2 * 2])
        mvall = sb("mvall", [P, NT, 2])
        std = sb("std", [P, NT])
        stage = sb("stage", [P, 2, D])
        psT = ctx.enter_context(nc.psum_tensor(f"{name}_psT", [P, 2, W], F32))
        stat_steps, waited = sem("stat_steps"), sem("waited")
        var_ready, std_ready, scale_ready = sem("var_ready"), sem("std_ready"), sem("scale_ready")
        row_steps = sem("row_steps")
        h_ready, transposed, h_split, hT_stored = sem("h_ready"), sem("transposed"), sem("h_split"), sem("hT_stored")
        block = ctx.enter_context(nc.Block())
        hT3 = m.hT[:].rearrange("p (c n) -> p c n", c=2)
        ha = haug[:].rearrange("p (t w) -> p t w", t=NT)

        @block.vector
        def _(dve):
            with dve.Fori(0, NT // 2) as i:
                for u in range(2):
                    dve.bn_stats(stat[:, 6 * u:6 * u + 6], m.x[:, cols(i * 2 * D + u * D, D)]).then_inc(stat_steps, 1)
                for u in range(2):
                    wait_apart(dve, stat_steps, i * 4 + 1 + u, waited)
                    dve.bn_aggr(mv[:, 2 * u:2 * u + 2], stat[:, 6 * u:6 * u + 6]).then_inc(stat_steps, 1)
                dve.wait_ge(stat_steps, i * 4 + 4)
                dve.tensor_copy(mvall[:].rearrange("p t k -> p (t k)")[:, cols(i * 4, 4)], mv[:]).then_inc(row_steps, 1)
            dve.wait_ge(row_steps, NT // 2)
            dve.tensor_scalar(std[:], mvall[:, :, 1], EPS, None, ALU.add).then_inc(var_ready, 1)
            dve.wait_ge(std_ready, 1)
            dve.reciprocal(m.rstd[:], std[:]).then_inc(row_steps, 1)
            dve.wait_ge(row_steps, NT // 2 + 1)
            dve.scalar_tensor_tensor(out=m.nbias[:], in0=mvall[:, :, 0], scalar=-1.0, in1=m.rstd[:],
                                     op0=ALU.mult, op1=ALU.mult).then_inc(scale_ready, 1)
            dve.memset(ha[:, :, D:D + 2], 1.0).then_inc(row_steps, 1)
            if split:
                dve.memset(hlow[:].rearrange("p (t w) -> p t w", t=NT)[:, :, D:D + 2], 0.0).then_inc(row_steps, 1)
            with dve.Fori(0, NT // 2) as i:
                for u in range(2):
                    at = i * 2 * width + u * width
                    dve.wait_ge(h_ready, i * 2 + u + 1)
                    if split:
                        dve.tensor_copy(haug[:, cols(at, D)], stage[:, u, :]).then_inc(row_steps, 1)
                        dve.wait_ge(row_steps, i * 2 + u + NT // 2 + 4)
                        dve.tensor_tensor(hlow[:, cols(at, D)], stage[:, u, :], haug[:, cols(at, D)],
                                          ALU.subtract).then_inc(h_split, 1)
                    else:
                        dve.tensor_copy(haug[:, cols(at, D)], stage[:, u, :]).then_inc(h_split, 1)
                    dve.wait_ge(transposed, i * 2 + u + 1)
                    dve.tensor_copy(hT3[:, :, cols(i * 2 * P + u * P, P)],
                                    psT[:, u, 0:2 * P].rearrange("p (c n) -> p c n", c=2)).then_inc(hT_stored, 1)

        @block.scalar
        def _(act):
            act.preload_act_table(ACT.Sqrt)
            act.wait_ge(var_ready, 1)
            act.activation(std[:], std[:], ACT.Sqrt).then_inc(std_ready, 1)
            act.preload_act_table(ACT.Exp)
            act.wait_ge(scale_ready, 1)
            for u in range(2):
                act.activation(stage[:, u, :], m.x[:, u * D:(u + 1) * D], ACT.Relu,
                               scale=m.rstd[:, u:u + 1], bias=m.nbias[:, u:u + 1]).then_inc(h_ready, 1)
            with act.Fori(1, NT // 2) as i:
                for u in range(2):
                    act.wait_ge(h_split, i * 2 + u - 1)
                    act.wait_ge(transposed, i * 2 + u - 1)
                    act.activation(stage[:, u, :], m.x[:, cols(i * 2 * D + u * D, D)], ACT.Relu,
                                   scale=m.rstd[:, cols(i * 2 + u, 1)],
                                   bias=m.nbias[:, cols(i * 2 + u, 1)]).then_inc(h_ready, 1)

        @block.tensor
        def _(pe):
            pe.wait_ge(h_ready, 1)
            for u in range(2):
                pe.wait_ge(h_ready, u + 1)
                for c in range(2):
                    mm = pe.transpose(psT[:, u, c * P:(c + 1) * P], stage[:, u, c * P:(c + 1) * P], m.ident[:])
                mm.then_inc(transposed, 1)
            with pe.Fori(1, NT // 2) as i:
                for u in range(2):
                    pe.wait_ge(h_ready, i * 2 + u + 1)
                    pe.wait_ge(hT_stored, i * 2 + u - 1)
                    for c in range(2):
                        mm = pe.transpose(psT[:, u, c * P:(c + 1) * P], stage[:, u, c * P:(c + 1) * P], m.ident[:])
                    mm.then_inc(transposed, 1)


def queries_keys(nc, m, name, io_q, io_k, bq, bk, q_parts, k_parts):
    with ExitStack() as ctx:
        def sb(n, s, d=F32):
            return ctx.enter_context(nc.sbuf_tensor(f"{name}_{n}", s, d))

        def sem(n):
            return nc.alloc_semaphore(f"{name}_{n}")

        wt = [sb(f"w{k}", [P, 2, D]) for k in "qk"]
        bias = [sb(f"b{k}", [P, 2]) for k in "qk"]
        whole = sb("whole", [P, 4, W])
        ps = ctx.enter_context(nc.psum_tensor(f"{name}_ps", [P, 4, W], F32))
        weights_in = [sem(f"weights_in{k}") for k in range(4)]
        bias_scaled = sem("bias_scaled")
        product_done, whole_ready, high_ready, low_ready = sem("product_done"), sem("whole_ready"), sem("high_ready"), sem("low_ready")
        block = ctx.enter_context(nc.Block())
        parts = [q_parts, k_parts]

        @block.sync
        def _(sp):
            for k, src in enumerate((io_q, io_k)):
                sp.dma_start(wt[k][:], src.rearrange("(c p) d -> p c d", p=P)).then_inc(weights_in[k], 16)
            for k, src in enumerate((bq, bk)):
                sp.dma_start(bias[k][:], src).then_inc(weights_in[2 + k], 16)

        def each_block(eng, body):
            with eng.Fori(0, NB) as b:
                body(b, W, b * 4)
            body(NB, TAIL, NB * 4)

        @block.tensor
        def _(pe):
            for s in weights_in[0:2]:
                pe.wait_ge(s, 16)

            def body(b, w, done):
                for k in range(4):
                    pe.wait_ge(whole_ready, done + k + 1)
                    for c in range(2):
                        mm = pe.matmul(ps[:, k, 0:w], wt[k // 2][:, c, (k % 2) * P:(k % 2 + 1) * P],
                                       m.hT[:, cols(b * W + c * NP, w)], start=(c == 0), stop=(c == 1))
                    mm.then_inc(product_done, 1)
            each_block(pe, body)

        @block.scalar
        def _(act):
            act.preload_act_table(ACT.Exp)
            for s in weights_in[2:4]:
                act.wait_ge(s, 16)
            act.mul(bias[0][:], bias[0][:], 1.0 / 32).then_inc(bias_scaled, 1)
            act.sem_inc(whole_ready, 4)
            act.wait_ge(bias_scaled, 1)

            def body(b, w, done):
                for k in range(4):
                    act.wait_ge(product_done, done + k + 1)
                    act.wait_ge(low_ready, done + k + 1)
                    act.activation(whole[:, k, 0:w], ps[:, k, 0:w], ACT.Identity, bias=bias[k // 2][:, k % 2:k % 2 + 1],
                                   scale=1.0 / 32 if k < 2 else 1.0).then_inc(whole_ready, 1)
            each_block(act, body)

        @block.vector
        def _(dve):
            dve.sem_inc(low_ready, 4)

            def body(b, w, done):
                for k in range(4):
                    high, low = parts[k // 2]
                    at = cols(b * W + (k % 2) * (NQ if k < 2 else NP), w)
                    dve.wait_ge(whole_ready, done + k + 5)
                    dve.tensor_copy(high[:, at], whole[:, k, 0:w]).then_inc(high_ready, 1)
                    dve.wait_ge(high_ready, done + k + 1)
                    dve.tensor_tensor(low[:, at], whole[:, k, 0:w], high[:, at], ALU.subtract).then_inc(low_ready, 1)
            each_block(dve, body)


NQ = (NB + 1) * W


def aug_plain(nc, name, augI, augJ, q_parts):
    aug_steps = nc.alloc_semaphore(f"{name}_aug_steps")
    with nc.Block() as block:
        @block.vector
        def _(dve):
            dve.memset(augI[:], 0.0).then_inc(aug_steps, 1)
            dve.memset(augJ[:], 0.0).then_inc(aug_steps, 1)
            for q in q_parts:
                for c in range(2):
                    dve.memset(q[:, c * NQ + NP:(c + 1) * NQ], 0.0).then_inc(aug_steps, 1)
            dve.wait_ge(aug_steps, 6)
            dve.memset(augI[0:1, :], 1.0).then_inc(aug_steps, 1)
            dve.memset(augJ[0:1, N:NP], -BIG).then_inc(aug_steps, 1)
            dve.memset(augJ[64:67, :], 1.0).then_inc(aug_steps, 1)


def aug_graphs(nc, name, ptr, augI, augJ, notJ, q_parts):
    with ExitStack() as ctx:
        def sb(n, s, d=F32):
            return ctx.enter_context(nc.sbuf_tensor(f"{name}_{n}", s, d))

        def sem(n):
            return nc.alloc_semaphore(f"{name}_{n}")

        G = NG + 1
        bounds = sb("bounds", [G, 2], I32)
        edges = sb("edges", [G, 2])
        node = sb("node", [G, NP])
        hot = sb("hot", [G, NP])
        bounds_cleared, low_in, high_in, node_ready, dve_steps = (
            sem("bounds_cleared"), sem("low_in"), sem("high_in"), sem("node_ready"), sem("dve_steps"))
        block = ctx.enter_context(nc.Block())

        @block.sync
        def _(sp):
            sp.wait_ge(bounds_cleared, 1)
            sp.dma_start(bounds[1:G, 0:1], ptr).then_inc(low_in, 16)
            sp.dma_start(bounds[0:G - 1, 1:2], ptr).then_inc(high_in, 16)

        @block.gpsimd
        def _(pool):
            pool.iota(node[:], pattern=[[1, NP]], base=0, channel_multiplier=0,
                      allow_small_or_imprecise_dtypes=True).then_inc(node_ready, 1)

        @block.vector
        def _(dve):
            steps = 0

            def done(ins):
                nonlocal steps
                steps += 1
                ins.then_inc(dve_steps, 1)
                return steps

            done(dve.memset(bounds[:, 0:1], -1))
            dve.memset(bounds[:, 1:2], 1 << 30).then_inc(dve_steps, 1)
            steps += 1
            dve.wait_ge(dve_steps, 2)
            dve.memset(edges[:], 0.0).then_inc(bounds_cleared, 1)
            done(dve.memset(augI[:], 0.0))
            done(dve.memset(augJ[:], 0.0))
            done(dve.memset(notJ[:], 0.0))
            for q in q_parts:
                for c in range(2):
                    done(dve.memset(q[:, c * NQ + NP:(c + 1) * NQ], 0.0))
            dve.wait_ge(low_in, 16)
            dve.wait_ge(high_in, 16)
            dve.wait_ge(bounds_cleared, 1)
            n = done(dve.tensor_copy(edges[:], bounds[:]))
            dve.wait_ge(dve_steps, n)
            dve.wait_ge(node_ready, 1)
            n = done(dve.tensor_scalar(hot[:], node[:], edges[:, 0:1], None, ALU.is_ge))
            dve.wait_ge(dve_steps, n)
            n = done(dve.scalar_tensor_tensor(out=hot[:], in0=node[:], scalar=edges[:, 1:2], in1=hot[:],
                                              op0=ALU.is_lt, op1=ALU.mult))
            dve.wait_ge(dve_steps, n)
            done(dve.tensor_scalar(augI[0:G, 0:NP], hot[:], -BIG, None, ALU.mult))
            done(dve.tensor_scalar(augJ[0:G, :], hot[:], -1.0, 1.0, ALU.mult, ALU.add))
            n = done(dve.tensor_scalar(notJ[0:G, :], hot[:], -1.0, None, ALU.mult))
            dve.wait_ge(dve_steps, n)
            done(dve.memset(augJ[0:G, N:NP], 1.0))
            done(dve.memset(notJ[0:G, N:NP], -1.0))
            done(dve.memset(augJ[64:67, :], 1.0))


def row_max(nc, name, adj, qh, kh, graphs, augI, augJ, notJ, negm, zoff):
    with ExitStack() as ctx:
        def sb(n, s, d=F32):
            return ctx.enter_context(nc.sbuf_tensor(f"{name}_{n}", s, d))

        def sem(n):
            return nc.alloc_semaphore(f"{name}_{n}")

        rows = sb("rows", [P, 2, NP])
        junk = sb("junk", [P, 2, HALF], BF16)
        best = sb("best", [P, 2, 2])
        least = sb("least", [P, 2, 2])
        top = sb("top", [P, 2])
        low = sb("low", [P, 2])
        if graphs:
            masked = sb("masked", [P, 2, NP])
            junk2 = sb("junk2", [P, NP], BF16)
            shift = sb("shift", [P, 2])
            zt = sb("zt", [P, 2])
        ps = [ctx.enter_context(nc.psum_tensor(f"{name}_ps{k}", [P, 4 * W], F32)) for k in range(2)]
        rows_in = [sem(f"rows_in{k}") for k in range(2)]
        rows_used, products, bank_free, max_steps = sem("rows_used"), sem("products"), sem("bank_free"), sem("max_steps")
        shift_ready, sums_ready, waited = sem("shift_ready"), sem("sums_ready"), sem("waited")
        block = ctx.enter_context(nc.Block())

        @block.sync
        def _(sp):
            with sp.Fori(0, NT // 2) as i:
                for u in range(2):
                    sp.wait_ge(rows_used, i * 2 + u + 1)
                    sp.dma_start(rows[:, u, :], adj[cols(i * 2 * P + u * P, P), :]).then_inc(rows_in[u], 16)

        @block.tensor
        def _(pe):
            with pe.Fori(0, NT // 2) as i:
                for u in range(2):
                    at = i * 2 * P + u * P
                    for half in range(2):
                        kinds = ("scores", "graphs") if graphs else ("scores",)
                        for kind in kinds:
                            bank = kinds.index(kind) if graphs else half
                            n = len(kinds) * half + kinds.index(kind)
                            pe.wait_ge(bank_free, i * 4 * len(kinds) + u * 2 * len(kinds) + n + 1)
                            for a, w in chunks(HALF, W):
                                key = half * HALF + a
                                out = ps[bank][:, a:a + w]
                                if kind == "scores":
                                    for c in range(2):
                                        mm = pe.matmul(out, qh[:, cols(at + c * NQ, P)], kh[:, c * NP + key:c * NP + key + w],
                                                       start=(c == 0), stop=(c == 1 and not graphs))
                                    if graphs:
                                        mm = pe.matmul(out, augI[:, cols(at, P)], augJ[:, key:key + w],
                                                       start=False, stop=True)
                                else:
                                    mm = pe.matmul(out, augI[:, cols(at, P)], notJ[:, key:key + w], start=True, stop=True)
                            mm.then_inc(products, 1)

        per_half = 2 if graphs else 1

        @block.vector
        def _(dve):
            dve.sem_inc(bank_free, 2)
            dve.sem_inc(rows_used, 2)
            per_tile = 5 if graphs else 2
            with dve.Fori(0, NT // 2) as i:
                for u in range(2):
                    dve.wait_ge(rows_in[u], i * 16 + 16)
                    if graphs:
                        dve.wait_ge(sums_ready, i * 2 + u + 1)
                    for half in range(2):
                        a = half * HALF
                        w = HALF if half == 0 else N - HALF
                        done = i * 4 * per_half + (u * 2 + half) * per_half
                        wait_apart(dve, products, done + 1, waited)
                        dve.tensor_tensor_reduce(junk[:, half, 0:w], rows[:, u, a:a + w], ps[0 if graphs else half][:, 0:w], 1.0, -3e38,
                                                 ALU.add, ALU.max, best[:, u, half:half + 1]).then_inc(bank_free, 1)
                        if graphs:
                            wait_apart(dve, products, done + 2, waited)
                            dve.tensor_tensor_reduce(masked[:, u, a:a + HALF], rows[:, u, a:a + HALF], ps[1][:, 0:HALF], 1.0, 3e38,
                                                     ALU.add, ALU.min, least[:, u, half:half + 1]).then_inc(bank_free, 1)
                    dve.wait_ge(bank_free, i * 4 * per_half + (u + 1) * 2 * per_half + 2)
                    base = i * 2 * per_tile + u * per_tile
                    dve.tensor_tensor(top[:, u:u + 1], best[:, u, 0:1], best[:, u, 1:2], ALU.max).then_inc(max_steps, 1)
                    if graphs:
                        dve.tensor_tensor(low[:, u:u + 1], least[:, u, 0:1], least[:, u, 1:2], ALU.min).then_inc(max_steps, 1)
                        dve.wait_ge(max_steps, base + 2)
                        dve.scalar_tensor_tensor(out=top[:, u:u + 1], in0=low[:, u:u + 1], scalar=-1e6, in1=top[:, u:u + 1],
                                                 op0=ALU.mult, op1=ALU.max).then_inc(max_steps, 1)
                        dve.wait_ge(max_steps, base + 3)
                        dve.tensor_scalar(shift[:, u:u + 1], top[:, u:u + 1], -2.0, LOG_P, ALU.mult, ALU.add).then_inc(shift_ready, 1)
                        dve.tensor_scalar(negm[:, cols(i * 2 + u, 1)], top[:, u:u + 1], -1.0, LOG_P / 2, ALU.mult,
                                          ALU.add).then_inc(max_steps, 1)
                        dve.sem_inc(max_steps, 1)
                    else:
                        dve.wait_ge(max_steps, base + 1)
                        dve.tensor_scalar(negm[:, cols(i * 2 + u, 1)], top[:, u:u + 1], -1.0, LOG_P / 2, ALU.mult,
                                          ALU.add).then_inc(max_steps, 1)
                    dve.sem_inc(rows_used, 1)

        if graphs:
            @block.scalar
            def _(act):
                act.preload_act_table(ACT.Exp)
                act.sem_inc(sums_ready, 2)
                with act.Fori(0, NT // 2) as i:
                    for u in range(2):
                        act.wait_ge(shift_ready, i * 2 + u + 1)
                        act.activation(junk2[:], masked[:, u, :], ACT.Exp, bias=shift[:, u:u + 1], scale=-2e6,
                                       accum_out=zt[:, u:u + 1]).then_inc(sums_ready, 1)
                        act.wait_ge(sums_ready, i * 2 + u + 3)
                        act.copy(zoff[:, cols(i * 2 + u, 1)], zt[:, u:u + 1])


def shift_rows(nc, m, name, negm, augI):
    with ExitStack() as ctx:
        def sb(n, s, d=F32):
            return ctx.enter_context(nc.sbuf_tensor(f"{name}_{n}", s, d))

        def sem(n):
            return nc.alloc_semaphore(f"{name}_{n}")

        part = sb("part", [P, 3, NT], BF16)
        part32 = sb("part32", [P, NT, 3])
        rest = sb("rest", [P, 2, NT])
        diag = sb("diag", [P, 2, 3, P], BF16)
        pick = sb("pick", [P, 3, P], BF16)
        ps = ctx.enter_context(nc.psum_tensor(f"{name}_ps", [P, 2, W], F32))
        dve_steps, diag_ready, row_ready, row_stored = sem("dve_steps"), sem("diag_ready"), sem("row_ready"), sem("row_stored")
        block = ctx.enter_context(nc.Block())

        @block.vector
        def _(dve):
            dve.sem_inc(row_ready, 2)
            dve.memset(pick[:], 0.0).then_inc(dve_steps, 1)
            dve.tensor_copy(part[:, 0, :], negm[:]).then_inc(dve_steps, 1)
            dve.wait_ge(dve_steps, 2)
            for k in range(3):
                dve.memset(pick[:, k, 64 + k:65 + k], 1.0).then_inc(dve_steps, 1)
            dve.tensor_tensor(rest[:, 0, :], negm[:], part[:, 0, :], ALU.subtract).then_inc(dve_steps, 1)
            dve.wait_ge(dve_steps, 6)
            dve.tensor_copy(part[:, 1, :], rest[:, 0, :]).then_inc(dve_steps, 1)
            dve.wait_ge(dve_steps, 7)
            dve.tensor_tensor(rest[:, 1, :], rest[:, 0, :], part[:, 1, :], ALU.subtract).then_inc(dve_steps, 1)
            dve.wait_ge(dve_steps, 8)
            dve.tensor_copy(part[:, 2, :], rest[:, 1, :]).then_inc(dve_steps, 1)
            dve.wait_ge(dve_steps, 9)
            dve.tensor_copy(part32[:].rearrange("p t k -> p k t"), part[:]).then_inc(dve_steps, 1)
            dve.wait_ge(dve_steps, 10)
            scal = part32[:].rearrange("p t k -> p (t k)")
            with dve.Fori(0, NT // 2) as i:
                for u in range(2):
                    dve.wait_ge(row_ready, i * 2 + u + 1)
                    for k in range(3):
                        dve.tensor_scalar(diag[:, u, k, :], m.ident[:], scal[:, cols(i * 6 + u * 3 + k, 1)], None,
                                          ALU.mult).then_inc(diag_ready, 1)
                for u in range(2):
                    dve.wait_ge(row_ready, i * 2 + u + 3)
                    dve.tensor_copy(augI[64:67, cols(i * 2 * P + u * P, P)], ps[64:67, u, 0:P]).then_inc(row_stored, 1)

        @block.tensor
        def _(pe):
            with pe.Fori(0, NT // 2) as i:
                for u in range(2):
                    pe.wait_ge(diag_ready, i * 6 + u * 3 + 3)
                    for k in range(3):
                        mm = pe.matmul(ps[:, u, 0:P], pick[:, k, :], diag[:, u, k, :], start=(k == 0), stop=(k == 2))
                    mm.then_inc(row_ready, 1)


def over_blocks(eng, one):
    with eng.Fori(0, NB) as b:
        one(b, W, W)
    one(NB, TAIL, None)


def later_groups(eng, step, b, w, n0, begin=0):
    def four(i):
        for u in range(4):
            g = i * 4 + u + 1
            step(b, w, g, u, n0 + g)
    with eng.Fori(begin, NGRP // 4) as i:
        four(i)


FIRST = 4


def pslot(slot):
    return 2 if slot == FIRST else slot % 2


def bslot(slot):
    return 1 if slot == FIRST else slot % 2


def load_blocks(sp, adjT, ring, adj_in, used, n0):
    def step(b, w, g, slot, n):
        sp.wait_ge(used, n + (1 if slot == FIRST else 2))
        sp.dma_start(ring[:, slot, :, 0:w],
                     adjT[cols(g * 2 * P, 2 * P), cols(b * W, w)].rearrange("(u p) i -> p u i", p=P)
                     ).then_inc(adj_in[slot], 16)

    def one(b, w, next_w):
        n = n0 + b * NGRP
        step(b, w, 0, FIRST, n)
        later_groups(sp, step, b, w, n)
    over_blocks(sp, one)


def arrived(dve, adj_in, b, g, slot, before=0):
    if slot == FIRST:
        dve.wait_ge(adj_in[slot], (b + before) * 16 + 16)
    else:
        dve.wait_ge(adj_in[slot], (b + before) * 48 + (g - 1 - slot) * 4 + 16)


def attend(nc, name, adjT, q_parts, k_parts, augI, augJ, hh, hl, U):
    width = D + 2
    with ExitStack() as ctx:
        def sb(n, s, d=F32):
            return ctx.enter_context(nc.sbuf_tensor(f"{name}_{n}", s, d))

        def sem(n):
            return nc.alloc_semaphore(f"{name}_{n}")

        ring = sb("ring", [P, 5, 2, W])
        t = sb("t", [P, 3, 2, W])
        p32 = sb("p32", [P, 3, 2, W])
        ph = sb("ph", [P, 3, 2, W], F16)
        pl = sb("pl", [P, 3, 2, W], F16)
        psS = [ctx.enter_context(nc.psum_tensor(f"{name}_psS{k}", [P, 2, W], F32)) for k in range(2)]
        acc = [ctx.enter_context(nc.psum_tensor(f"{name}_acc{k}", [P, W], F32)) for k in range(4)]
        adj_in = [sem(f"adj_in{k}") for k in range(5)]
        scores_ready, added, exp_ready, probs_ready, summed, stored = (
            sem("scores_ready"), sem("added"), sem("exp_ready"), sem("probs_ready"), sem("summed"), sem("stored"))
        block = ctx.enter_context(nc.Block())

        @block.sync
        def _(sp):
            load_blocks(sp, adjT, ring, adj_in, added, 0)

        @block.tensor
        def _(pe):
            kh, kl = k_parts
            qh, ql = q_parts

            def scores(b, w, g, slot, need):
                pe.wait_ge(added, need)
                for u in range(2):
                    key = g * 2 * P + u * P
                    out = psS[bslot(slot)][:, u, 0:w]
                    pe.matmul(out, augJ[:, cols(key, P)], augI[:, cols(b * W, w)], start=True, stop=False)
                    for c in range(2):
                        high = kh[:, cols(key + c * NP, P)]
                        pe.matmul(out, high, qh[:, cols(b * W + c * NQ, w)], start=False, stop=False)
                        pe.matmul(out, high, ql[:, cols(b * W + c * NQ, w)], start=False, stop=False)
                        mm = pe.matmul(out, kl[:, cols(key + c * NP, P)], qh[:, cols(b * W + c * NQ, w)],
                                       start=False, stop=(c == 1))
                mm.then_inc(scores_ready, 1)

            def sums(b, w, g, slot, n, first, last):
                pe.wait_ge(probs_ready, n + 3)
                for u in range(2):
                    row = cols(g * 2 * width + u * width, width - 1)
                    for q in range(w // P):
                        if first and u == 0:
                            pe.wait_ge(stored, b * 4 + q + 1)
                        out = acc[q][:, 0:width - 1]
                        high = ph[:, pslot(slot), u, q * P:(q + 1) * P]
                        low = pl[:, pslot(slot), u, q * P:(q + 1) * P]
                        pe.matmul(out, high, hh[:, row], start=(first and u == 0), stop=False)
                        pe.matmul(out, high, hl[:, row], start=False, stop=False)
                        mm = pe.matmul(out, low, hh[:, row], start=False, stop=(last and u == 1))
                mm.then_inc(summed, 1)

            def one(b, w, next_w):
                n0 = b * NGRP

                def step(b, w, g, slot, n):
                    nxt = (slot + 1) % 4
                    scores(b, w, g + 1, nxt, n + 5)
                    sums(b, w, g, slot, n, False, False)

                scores(b, w, 1, 0, n0 + 5)
                sums(b, w, 0, FIRST, n0, True, False)
                later = NGRP // 4
                with pe.Fori(0, later - 1) as i:
                    for u in range(4):
                        step(b, w, i * 4 + u + 1, u, n0 + i * 4 + u + 1)
                for u in range(3):
                    g = (later - 1) * 4 + u + 1
                    step(b, w, g, u, n0 + g)
                n = n0 + NGRP - 1
                if next_w:
                    scores(b + 1, next_w, 0, FIRST, n + 6)
                sums(b, w, NGRP - 1, 3, n, False, True)

            scores(0, W, 0, FIRST, 5)
            over_blocks(pe, one)

        @block.vector
        def _(dve):
            dve.sem_inc(added, 5)
            dve.sem_inc(probs_ready, 2)

            def add(b, w, g, slot, n):
                s = pslot(slot)
                arrived(dve, adj_in, b, g, slot)
                dve.wait_ge(scores_ready, n + 1)
                dve.wait_ge(exp_ready, n * 2 + 2)
                dve.tensor_tensor(t[:, s, :, 0:w], ring[:, slot, :, 0:w], psS[bslot(slot)][:, :, 0:w],
                                  ALU.add).then_inc(added, 1)

            def low_half(w, slot, n):
                s = pslot(slot)
                dve.wait_ge(exp_ready, n * 2 + 6)
                dve.wait_ge(summed, n + 1)
                dve.tensor_tensor(pl[:, s, :, 0:w], p32[:, s, :, 0:w], ph[:, s, :, 0:w], ALU.subtract).then_inc(probs_ready, 1)

            def one(b, w, next_w):
                n0 = b * NGRP

                def step(b, w, g, slot, n):
                    low_half(w, (slot - 1) % 4, n - 1)
                    add(b, w, g, slot, n)

                low_half(w, FIRST, n0)
                add(b, w, 1, 0, n0 + 1)
                for u in range(1, 4):
                    step(b, w, u + 1, u, n0 + u + 1)
                later_groups(dve, step, b, w, n0, begin=1)
                if next_w:
                    add(b + 1, next_w, 0, FIRST, n0 + NGRP)
                low_half(w, 3, n0 + NGRP - 1)

            add(0, W, 0, FIRST, 0)
            over_blocks(dve, one)

        @block.scalar
        def _(act):
            act.preload_act_table(ACT.Exp)
            act.sem_inc(exp_ready, 4)
            act.sem_inc(stored, 4)
            act.sem_inc(summed, 2)

            def exps(b, w, g, slot, n):
                s = pslot(slot)
                act.wait_ge(added, n + 6)
                act.wait_ge(summed, n + 1)
                act.wait_ge(probs_ready, n + 1)
                act.activation(p32[:, s, :, 0:w], t[:, s, :, 0:w], ACT.Exp, scale=2.0).then_inc(exp_ready, 1)
                act.activation(ph[:, s, :, 0:w], t[:, s, :, 0:w], ACT.Exp, scale=2.0).then_inc(exp_ready, 1)

            def one(b, w, next_w):
                n0 = b * NGRP
                later_groups(act, exps, b, w, n0)
                if next_w:
                    exps(b + 1, next_w, 0, FIRST, n0 + NGRP)
                act.wait_ge(summed, n0 + NGRP + 2)
                for q in range(w // P):
                    act.copy(U[:, cols(b * 4 * width + q * width, width - 1)], acc[q][:, 0:width - 1]).then_inc(stored, 1)

            exps(0, W, 0, FIRST, 0)
            over_blocks(act, one)


class Chain:

    def __init__(self, eng, sem):
        self.eng, self.sem, self.count = eng, sem, 0

    def __call__(self, ins):
        self.count += 1
        ins.then_inc(self.sem, 1)
        self.eng.wait_ge(self.sem, self.count)


class RowProduct:

    def __init__(self, ctx, nc, m, name, src, src_width, scale, dst, plus, ps, pso):
        def sb(n, s, d=F32):
            return ctx.enter_context(nc.sbuf_tensor(f"{name}_{n}", s, d))

        def sem(n):
            return nc.alloc_semaphore(f"{name}_{n}")

        self.m, self.src, self.src_width, self.scale, self.dst, self.plus = m, src, src_width, scale, dst, plus
        self.w = sb("w", [P, 2, D])
        self.stage = sb("stage", [P, 2, D])
        self.turned = sb("turned", [P, 2, D])
        self.ps, self.pso = ps, pso
        self.staged, self.transposed, self.turned_ready, self.product_done, self.dst_done, self.biased = (
            sem("staged"), sem("transposed"), sem("turned_ready"), sem("product_done"), sem("dst_done"), sem("biased"))

    def start_vector(self, dve):
        dve.sem_inc(self.turned_ready, 2)

    def start_scalar(self, act):
        act.sem_inc(self.transposed, 2)
        act.sem_inc(self.dst_done, 2)

    def scalar(self, act, n0=0, scale0=0):
        with act.Fori(0, NT // 2) as i:
            for u in range(2):
                act.wait_ge(self.transposed, i * 2 + u + 1 + n0)
                act.activation(self.stage[:, u, :], self.src[:, cols(i * 2 * self.src_width + u * self.src_width, D)],
                               ACT.Copy, scale=self.scale[:, cols(i * 2 + u + scale0, 1)]).then_inc(self.staged, 1)

    def tensor(self, pe, n0=0):
        m, ps, pso = self.m, self.ps, self.pso
        with pe.Fori(0, NT // 2) as i:
            for u in range(2):
                pe.wait_ge(self.staged, i * 2 + u + 1 + n0)
                pe.wait_ge(self.turned_ready, i * 2 + u + 1 + n0)
                for c in range(2):
                    mm = pe.transpose(ps[u][:, c * P:(c + 1) * P], self.stage[:, u, c * P:(c + 1) * P], m.ident[:])
                mm.then_inc(self.transposed, 1)
            for u in range(2):
                pe.wait_ge(self.turned_ready, i * 2 + u + 3 + n0)
                pe.wait_ge(self.dst_done, i * 2 + u + 1 + n0)
                for c in range(2):
                    mm = pe.matmul(pso[u][:, 0:D], self.turned[:, u, c * P:(c + 1) * P], self.w[:, c, :],
                                   start=(c == 0), stop=(c == 1))
                mm.then_inc(self.product_done, 1)

    def vector(self, dve, n0=0, bias=None, share=None):
        with dve.Fori(0, NT // 2) as i:
            for u in range(2):
                dve.wait_ge(self.transposed, i * 2 + u + 3 + n0)
                dve.tensor_copy(self.turned[:, u, :], self.ps[u][:, 0:D]).then_inc(self.turned_ready, 1)
            for u in range(2):
                at = cols(i * 2 * D + u * D, D)
                if bias is not None:
                    dve.scalar_tensor_tensor(out=self.dst[:, at], in0=bias[:], scalar=share[:, cols(i * 2 + u, 1)],
                                             in1=self.dst[:, at], op0=ALU.mult, op1=ALU.add).then_inc(self.biased, 1)
                    dve.wait_ge(self.biased, i * 2 + u + 1)
                dve.wait_ge(self.product_done, i * 2 + u + 1 + n0)
                if self.plus:
                    dve.tensor_tensor(self.dst[:, at], self.dst[:, at], self.pso[u][:, 0:D], ALU.add).then_inc(self.dst_done, 1)
                else:
                    dve.tensor_copy(self.dst[:, at], self.pso[u][:, 0:D]).then_inc(self.dst_done, 1)


def project(nc, m, name, U, weight, bias, zoff):
    with ExitStack() as ctx:
        def sb(n, s, d=F32):
            return ctx.enter_context(nc.sbuf_tensor(f"{name}_{n}", s, d))

        def sem(n):
            return nc.alloc_semaphore(f"{name}_{n}")

        z = sb("z", [P, NT])
        rz = sb("rz", [P, NT])
        share = sb("share", [P, NT])
        b = sb("b", [P, D])
        ps = [ctx.enter_context(nc.psum_tensor(f"{name}_ps{k}", [P, W], F32)) for k in range(4)]
        weight_in, bias_in, z_steps = sem("weight_in"), sem("bias_in"), sem("z_steps")
        rp = RowProduct(ctx, nc, m, name, U, D + 2, rz, m.x, True, ps[0:2], ps[2:4])
        block = ctx.enter_context(nc.Block())
        Z = U[:].rearrange("p (t w) -> p t w", t=NT)[:, :, D]

        @block.sync
        def _(sp):
            sp.dma_start(rp.w[:], weight.rearrange("(c p) d -> p c d", p=P)).then_inc(weight_in, 16)
            sp.dma_start(b[:], bias.partition_broadcast(P)).then_inc(bias_in, 16)

        @block.vector
        def _(dve):
            chain = Chain(dve, z_steps)
            if zoff is not None:
                chain(dve.tensor_tensor(z[:], Z, zoff[:], ALU.add))
            else:
                chain(dve.tensor_copy(z[:], Z))
            chain(dve.reciprocal(rz[:], z[:]))
            chain(dve.tensor_tensor(share[:], Z, rz[:], ALU.mult))
            rp.start_vector(dve)
            dve.wait_ge(bias_in, 16)
            rp.vector(dve, bias=b, share=share)

        @block.scalar
        def _(act):
            act.wait_ge(z_steps, 3)
            rp.start_scalar(act)
            rp.scalar(act)

        @block.tensor
        def _(pe):
            pe.wait_ge(weight_in, 16)
            rp.tensor(pe)


def gat_vectors(nc, m, name, io, wa, scol, dcol, d01, dbc):
    with ExitStack() as ctx:
        def sb(n, s, d=F32):
            return ctx.enter_context(nc.sbuf_tensor(f"{name}_{n}", s, d))

        def sem(n):
            return nc.alloc_semaphore(f"{name}_{n}")

        wT = sb("wT", [P, 2 * HEADS, D])
        a = sb("a", [P, HEADS, 2, 2])
        spread = sb("spread", [P, 2, HEADS, P])
        psw = ctx.enter_context(nc.psum_tensor(f"{name}_psw", [P, W], F32))
        psc = ctx.enter_context(nc.psum_tensor(f"{name}_psc", [P, W], F32))
        psd = ctx.enter_context(nc.psum_tensor(f"{name}_psd", [P, HEADS, W], F32))
        w_in, a_in, wa_done, wa_ready, spread_ready, cols_done, d_done, d_stored, dve_steps = (
            sem("w_in"), sem("a_in"), sem("wa_done"), sem("wa_ready"), sem("spread_ready"), sem("cols_done"),
            sem("d_done"), sem("d_stored"), sem("dve_steps"))
        block = ctx.enter_context(nc.Block())

        @block.sync
        def _(sp):
            sp.dma_start(wT[:], io.w["L1T"].rearrange("(k p) c -> p k c", p=P)).then_inc(w_in, 16)
            sp.dma_start(a[:], io.a).then_inc(a_in, 16)

        def each_block(eng, body):
            with eng.Fori(0, NB) as b:
                body(b, W)
            body(NB, TAIL)

        @block.tensor
        def _(pe):
            pe.wait_ge(w_in, 16)
            pe.wait_ge(a_in, 16)
            for c in range(2):
                for h in range(HEADS):
                    at = c * 2 * HEADS + h * 2
                    for k in range(2):
                        mm = pe.matmul(psw[:, at:at + 2], wT[:, h * 2 + k, c * P:(c + 1) * P], a[:, h, k, :],
                                       start=(k == 0), stop=(k == 1))
            mm.then_inc(wa_done, 1)
            pe.wait_ge(wa_ready, 1)
            for t in range(NT):
                for c in range(2):
                    mm = pe.matmul(psc[:, t * 8:t * 8 + 8], m.hT[:, c * NP + t * P:c * NP + (t + 1) * P], wa[:, c, :],
                                   start=(c == 0), stop=(c == 1))
            mm.then_inc(cols_done, 1)
            pe.wait_ge(spread_ready, 8)

            def body(b, w):
                for h in range(HEADS):
                    pe.wait_ge(d_stored, b * HEADS + h + 1)
                    for c in range(2):
                        mm = pe.matmul(psd[:, h, 0:w], spread[:, c, h, :], m.hT[:, cols(b * W + c * NP, w)],
                                       start=(c == 0), stop=(c == 1))
                    mm.then_inc(d_done, 1)
            each_block(pe, body)

        @block.scalar
        def _(act):
            act.preload_act_table(ACT.Exp)
            act.sem_inc(d_stored, HEADS)

            def body(b, w):
                for h in range(HEADS):
                    act.wait_ge(d_done, b * HEADS + h + 1)
                    act.copy(dbc[:, cols(b * W + h * NP, w)], psd[:, h, 0:w]).then_inc(d_stored, 1)
            each_block(act, body)

        @block.vector
        def _(dve):
            dve.wait_ge(wa_done, 1)
            dve.tensor_copy(wa[:].rearrange("p c k -> p (c k)"), psw[:, 0:4 * HEADS]).then_inc(wa_ready, 1)
            dve.wait_ge(wa_ready, 1)
            for c in range(2):
                for h in range(HEADS):
                    dve.tensor_scalar(spread[:, c, h, :], m.ones[:], wa[:, c, 2 * h + 1:2 * h + 2], None,
                                      ALU.mult).then_inc(spread_ready, 1)
            dve.wait_ge(cols_done, 1)
            both = psc[:, 0:NT * 8].rearrange("p (t h s) -> p s h t", h=HEADS, s=2)
            dve.tensor_copy(scol[:], both[:, 0]).then_inc(dve_steps, 1)
            dve.tensor_copy(dcol[:], both[:, 1]).then_inc(dve_steps, 1)
            dve.wait_ge(dve_steps, 2)
            dve.tensor_scalar(dcol[:, :, NT - 1], dcol[:, :, NT - 1], m.padneg[:, 0:1], None, ALU.add).then_inc(dve_steps, 1)
            dve.wait_ge(dve_steps, 3)
            dve.tensor_scalar(d01[:], dcol[:], 0.01, None, ALU.mult).then_inc(dve_steps, 1)
            dve.wait_ge(d_stored, HEADS * (NB + 2))
            dve.memset(dbc[:].rearrange("p (h n) -> p h n", h=HEADS)[:, :, N:NP], -1e30).then_inc(dve_steps, 1)


def gat_max(nc, name, adj, scol, dbc, negm):
    with ExitStack() as ctx:
        def sb(n, s, d=F32):
            return ctx.enter_context(nc.sbuf_tensor(f"{name}_{n}", s, d))

        def sem(n):
            return nc.alloc_semaphore(f"{name}_{n}")

        rows = sb("rows", [P, 2, NP])
        junk = sb("junk", [P, 2, NP], BF16)
        best = sb("best", [P, 2, HEADS + 1])
        steep = sb("steep", [P, HEADS + 1, NT])
        flat = sb("flat", [P, HEADS, NT])
        dtop = sb("dtop", [P, HEADS])
        rows_in = [sem(f"rows_in{k}") for k in range(2)]
        rows_used, reduced, steps, waited = sem("rows_used"), sem("reduced"), sem("steps"), sem("waited")
        block = ctx.enter_context(nc.Block())

        @block.sync
        def _(sp):
            with sp.Fori(0, NT // 2) as i:
                for u in range(2):
                    sp.wait_ge(rows_used, i * 2 + u + 1)
                    sp.dma_start(rows[:, u, :], adj[cols(i * 2 * P + u * P, P), :]).then_inc(rows_in[u], 16)

        @block.vector
        def _(dve):
            dve.sem_inc(rows_used, 2)
            dve.sem_inc(reduced, 2)
            with dve.Fori(0, NT // 2) as i:
                for u in range(2):
                    wait_apart(dve, rows_in[u], i * 16 + 16, waited)
                    for h in range(HEADS):
                        wait_apart(dve, reduced, i * 2 * (HEADS + 1) + u * (HEADS + 1) + h + 1, waited)
                        dve.tensor_tensor_reduce(junk[:, h % 2, 0:N], dbc[:, h * NP:h * NP + N], rows[:, u, 0:N], 1.0, -3e38,
                                                 ALU.add, ALU.max, best[:, u, h:h + 1]).then_inc(reduced, 1)
                    dve.tensor_reduce(best[:, u, HEADS:HEADS + 1], rows[:, u, 0:N], AX.X, ALU.max).then_inc(reduced, 1)
                    dve.wait_ge(reduced, i * 2 * (HEADS + 1) + (u + 1) * (HEADS + 1) + 2)
                    dve.tensor_copy(steep[:, :, cols(i * 2 + u, 1)],
                                    best[:, u, :].rearrange("p (h o) -> p h o", o=1)).then_inc(rows_used, 1)
            chain = Chain(dve, steps)
            chain(dve.tensor_reduce(dtop[:], dbc[:].rearrange("p (h n) -> p h n", h=HEADS)[:, :, 0:N], AX.X, ALU.max))
            chain(dve.tensor_scalar(dtop[:], dtop[:], 0.01, None, ALU.mult))
            dve.wait_ge(rows_used, NT + 2)
            for h in range(HEADS):
                chain(dve.tensor_scalar(flat[:, h, :], scol[:, h, :], 0.01, dtop[:, h:h + 1], ALU.mult, ALU.add))
                chain(dve.tensor_tensor(flat[:, h, :], flat[:, h, :], steep[:, HEADS, :], ALU.add))
            chain(dve.tensor_tensor(steep[:, 0:HEADS, :], steep[:, 0:HEADS, :], scol[:], ALU.add))
            chain(dve.tensor_tensor(flat[:], flat[:], steep[:, 0:HEADS, :], ALU.max))
            chain(dve.tensor_scalar(negm[:], flat[:], -1.0, None, ALU.mult))


def gat(nc, m, name, io, wa, dcol, d01, negm, haug):
    width = D + 2
    with ExitStack() as ctx:
        def sb(n, s, d=F32):
            return ctx.enter_context(nc.sbuf_tensor(f"{name}_{n}", s, d))

        def sem(n):
            return nc.alloc_semaphore(f"{name}_{n}")

        U = sb("U", [P, NT * width])
        A = sb("A", [P, NQ])
        B = sb("B", [P, NQ])
        spread = sb("spread", [P, 2, P])
        diag = sb("diag", [P, W])
        s32 = sb("s32", [P, W])
        rz = sb("rz", [P, NT])
        ring = sb("ring", [P, 5, 2, W])
        slope = sb("slope", [P, 3, 2, W])
        t = sb("t", [P, 3, 2, W])
        p32 = sb("p32", [P, 3, 2, W])
        acc = [ctx.enter_context(nc.psum_tensor(f"{name}_acc{k}", [P, W], F32)) for k in range(4)]
        spare = [ctx.enter_context(nc.psum_tensor(f"{name}_spare{k}", [P, W], F32)) for k in range(4)]
        adj_in = [sem(f"adj_in{k}") for k in range(5)]
        w_in, spread_ready, diag_ready, sm_done, s_ready, ab_ready = (
            sem("w_in"), sem("spread_ready"), sem("diag_ready"), sem("sm_done"), sem("s_ready"), sem("ab_ready"))
        slope_ready, maxed, added, exp_ready, summed, stored, z_steps, head_done = (
            sem("slope_ready"), sem("maxed"), sem("added"), sem("exp_ready"), sem("summed"), sem("stored"),
            sem("z_steps"), sem("head_done"))
        waited = sem("waited")
        rp = RowProduct(ctx, nc, m, name, U, width, rz, m.x, True, spare[0:2], spare[2:4])
        block = ctx.enter_context(nc.Block())
        GROUPS = (NB + 1) * NGRP
        BLOCKS = NB + 1
        Z = U[:].rearrange("p (t w) -> p t w", t=NT)[:, :, D]
        dflat = dcol[:].rearrange("p h t -> p (h t)")
        d01flat = d01[:].rearrange("p h t -> p (h t)")
        negflat = negm[:].rearrange("p h t -> p (h t)")
        waflat = wa[:].rearrange("p c k -> p (c k)")

        @block.sync
        def _(sp):
            with sp.Fori(0, HEADS) as h:
                sp.wait_ge(head_done, h + 1)
                sp.dma_start(rp.w[:], io.w["L1"][:, cols(h * D, D)].rearrange("(c p) d -> p c d", p=P)).then_inc(w_in, 16)

                load_blocks(sp, io.adjT, ring, adj_in, added, h * GROUPS)

        @block.tensor
        def _(pe):
            def sm(h, b, w):
                n = h * BLOCKS + b
                pe.wait_ge(s_ready, n + 1)
                for c in range(2):
                    mm = pe.matmul(spare[0][:, 0:w], spread[:, c, :], m.hT[:, cols(b * W + c * NP, w)], start=(c == 0), stop=(c == 1))
                mm.then_inc(sm_done, 1)
                pe.wait_ge(diag_ready, n + 1)
                pe.wait_ge(ab_ready, n * 2 + 2)
                pe.matmul(spare[1][:, 0:w], m.ones[:], diag[:, 0:w], start=True, stop=True).then_inc(sm_done, 1)

            def sums(b, w, g, slot, n, stored_n, first, last):
                pe.wait_ge(exp_ready, n + 3)
                for u in range(2):
                    row = cols(g * 2 * width + u * width, width - 1)
                    for q in range(w // P):
                        if first and u == 0:
                            pe.wait_ge(stored, stored_n + q + 1)
                        mm = pe.matmul(acc[q][:, 0:width - 1], p32[:, pslot(slot), u, q * P:(q + 1) * P], haug[:, row],
                                       start=(first and u == 0), stop=(last and u == 1))
                mm.then_inc(summed, 1)

            with pe.Fori(0, HEADS) as h:
                wait_apart(pe, spread_ready, h * 2 + 2, waited)
                with pe.Fori(0, NB) as b:
                    sm(h, b, W)
                sm(h, NB, TAIL)

                def one(b, w, next_w):
                    n0 = h * GROUPS + b * NGRP
                    sums(b, w, 0, FIRST, n0, h * NT + b * 4, True, False)
                    later = NGRP // 4
                    with pe.Fori(0, later - 1) as i:
                        for u in range(4):
                            sums(b, w, i * 4 + u + 1, u, n0 + i * 4 + u + 1, 0, False, False)
                    for u in range(4):
                        g = (later - 1) * 4 + u + 1
                        sums(b, w, g, u, n0 + g, 0, False, g == NGRP - 1)
                over_blocks(pe, one)
                wait_apart(pe, w_in, h * 16 + 16, waited)
                rp.tensor(pe, h * NT)

        @block.vector
        def _(dve):
            for ab_tile in (A, B):
                dve.memset(ab_tile[:, NP:NQ], 0.0).then_inc(ab_ready, 1)
            dve.sem_inc(added, 5)
            dve.sem_inc(maxed, 2)
            dve.sem_inc(head_done, 1)
            rp.start_vector(dve)

            def ab(h, b, w):
                n = h * BLOCKS + b
                dve.wait_ge(sm_done, n * 2 + 1)
                for q in range(w // P):
                    ins = dve.tensor_scalar(diag[:, q * P:(q + 1) * P], m.ident[:], negflat[:, cols(h * NT + b * 4 + q, 1)], None, ALU.mult)
                ins.then_inc(diag_ready, 1)
                dve.wait_ge(sm_done, n * 2 + 2)
                dve.wait_ge(s_ready, n + 2)
                dve.tensor_tensor(A[:, cols(b * W, w)], s32[:, 0:w], spare[1][:, 0:w], ALU.add).then_inc(ab_ready, 1)
                dve.scalar_tensor_tensor(out=B[:, cols(b * W, w)], in0=s32[:, 0:w], scalar=0.01, in1=spare[1][:, 0:w],
                                         op0=ALU.mult, op1=ALU.add).then_inc(ab_ready, 1)
    
            with dve.Fori(0, HEADS) as h:
                for c in range(2):
                    dve.tensor_scalar(spread[:, c, :], m.ones[:], waflat[:, cols(h * 2 + c * 2 * HEADS, 1)], None,
                                      ALU.mult).then_inc(spread_ready, 1)
                with dve.Fori(0, NB) as b:
                    ab(h, b, W)
                ab(h, NB, TAIL)
                wait_apart(dve, ab_ready, h * 2 * BLOCKS + 2 * BLOCKS + 2, waited)

                def step(b, w, g, slot, n):
                    s = pslot(slot)
                    dve.wait_ge(slope_ready, n + 1)
                    dve.wait_ge(exp_ready, n + 1)
                    for u in range(2):
                        ins = dve.scalar_tensor_tensor(out=t[:, s, u, 0:w], in0=A[:, cols(b * W, w)],
                                                       scalar=dflat[:, cols(h * NT + g * 2 + u, 1)], in1=slope[:, s, u, 0:w],
                                                       op0=ALU.add, op1=ALU.max)
                    ins.then_inc(maxed, 1)
                    arrived(dve, adj_in, b, g, slot, h * BLOCKS)
                    dve.wait_ge(maxed, n + 3)
                    dve.tensor_tensor(t[:, s, :, 0:w], t[:, s, :, 0:w], ring[:, slot, :, 0:w], ALU.add).then_inc(added, 1)

                def one(b, w, next_w):
                    n0 = h * GROUPS + b * NGRP
                    step(b, w, 0, FIRST, n0)
                    later_groups(dve, step, b, w, n0)
                over_blocks(dve, one)
                dve.wait_ge(stored, h * NT + NT + 4)
                dve.reciprocal(rz[:], Z).then_inc(z_steps, 1)
                dve.wait_ge(z_steps, h * 2 + 1)
                dve.tensor_scalar(rz[:], rz[:], 1.0 / HEADS, None, ALU.mult).then_inc(z_steps, 1)
                rp.vector(dve, h * NT)
                dve.wait_ge(rp.dst_done, h * NT + NT + 2)
                dve.sem_inc(head_done, 1)

        @block.scalar
        def _(act):
            act.preload_act_table(ACT.Exp)
            act.sem_inc(exp_ready, 2)
            act.sem_inc(summed, 2)
            act.sem_inc(stored, 4)
            act.sem_inc(s_ready, 1)
            rp.start_scalar(act)

            def s_row(h, b, w):
                n = h * BLOCKS + b
                act.wait_ge(sm_done, n * 2 + 1)
                act.wait_ge(ab_ready, n * 2 + 2)
                act.copy(s32[:, 0:w], spare[0][:, 0:w]).then_inc(s_ready, 1)

            with act.Fori(0, HEADS) as h:
                with act.Fori(0, NB) as b:
                    s_row(h, b, W)
                s_row(h, NB, TAIL)
                act.wait_ge(ab_ready, h * 2 * BLOCKS + 2 * BLOCKS + 2)

                def slopes(b, w, g, slot, n):
                    s = pslot(slot)
                    act.wait_ge(maxed, n + 1)
                    for u in range(2):
                        ins = act.activation(slope[:, s, u, 0:w], B[:, cols(b * W, w)], ACT.Identity,
                                             bias=d01flat[:, cols(h * NT + g * 2 + u, 1)])
                    ins.then_inc(slope_ready, 1)

                def exps(w, slot, n):
                    s = pslot(slot)
                    act.wait_ge(added, n + 6)
                    act.wait_ge(summed, n + 1)
                    act.activation(p32[:, s, :, 0:w], t[:, s, :, 0:w], ACT.Exp).then_inc(exp_ready, 1)

                def one(b, w, next_w):
                    n0 = h * GROUPS + b * NGRP

                    def step(b, w, g, slot, n):
                        slopes(b, w, g, slot, n)
                        exps(w, (slot - 1) % 4, n - 1)
                    slopes(b, w, 1, 0, n0 + 1)
                    exps(w, FIRST, n0)
                    for u in range(1, 4):
                        step(b, w, u + 1, u, n0 + u + 1)
                    later_groups(act, step, b, w, n0, begin=1)
                    if next_w:
                        slopes(b + 1, next_w, 0, FIRST, n0 + NGRP)
                    exps(w, 3, n0 + NGRP - 1)
                    act.wait_ge(summed, n0 + NGRP + 2)
                    for q in range(w // P):
                        act.copy(U[:, cols(b * 4 * width + q * width, width - 1)], acc[q][:, 0:width - 1]).then_inc(stored, 1)
                slopes(0, W, 0, FIRST, h * GROUPS)
                over_blocks(act, one)
                act.wait_ge(z_steps, h * 2 + 2)
                rp.scalar(act, h * NT)


TOP = float(np.float32(1.0 - 1e-7))
EPS3 = 1e-10


def artanh_before(chain, dve, y, v, w):
    chain(dve.tensor_scalar(y, y, TOP, -TOP, ALU.min, ALU.max))
    chain(dve.tensor_scalar(w, y, -1.0, 1.0, ALU.mult, ALU.add))
    chain(dve.reciprocal(w, w))
    chain(dve.tensor_scalar(v, y, 1.0, None, ALU.add))
    chain(dve.tensor_tensor(v, v, w, ALU.mult))


def artanh_after(chain, dve, y, v, w, z):
    chain(dve.tensor_tensor(w, y, y, ALU.mult))
    chain(dve.tensor_scalar(z, w, 1.0 / 11, 1.0 / 9, ALU.mult, ALU.add))
    for k in (7, 5, 3, 1):
        chain(dve.tensor_tensor(z, z, w, ALU.mult))
        chain(dve.tensor_scalar(z, z, 1.0 / k, None, ALU.add))
    chain(dve.tensor_tensor(z, z, y, ALU.mult))
    chain(dve.scalar_tensor_tensor(out=v, in0=v, scalar=0.5, in1=z, op0=ALU.mult, op1=ALU.subtract))
    chain(dve.scalar_tensor_tensor(out=v, in0=y, scalar=0.125, in1=v, op0=ALU.is_ge, op1=ALU.mult))
    chain(dve.tensor_tensor(v, v, z, ALU.add))


def row_product(nc, m, name, src, src_width, ones, dst, weight):
    with ExitStack() as ctx:
        ps = [ctx.enter_context(nc.psum_tensor(f"{name}_ps{k}", [P, W], F32)) for k in range(4)]
        weight_in = nc.alloc_semaphore(f"{name}_weight_in")
        rp = RowProduct(ctx, nc, m, name, src, src_width, ones, dst, False, ps[0:2], ps[2:4])
        block = ctx.enter_context(nc.Block())

        @block.sync
        def _(sp):
            sp.dma_start(rp.w[:], weight.rearrange("(c p) d -> p c d", p=P)).then_inc(weight_in, 16)

        @block.vector
        def _(dve):
            rp.start_vector(dve)
            rp.vector(dve)

        @block.scalar
        def _(act):
            rp.start_scalar(act)
            rp.scalar(act)

        @block.tensor
        def _(pe):
            pe.wait_ge(weight_in, 16)
            rp.tensor(pe)


def square_sums(chain, dve, src, big, out):
    chain(dve.tensor_tensor(big, src, src, ALU.mult))
    chain(dve.tensor_reduce(out, big, AX.X, ALU.add))


def hyper_points(nc, name, haug, mx, gaug):
    with ExitStack() as ctx:
        def col(n):
            return ctx.enter_context(nc.sbuf_tensor(f"{name}_{n}", [P, NT], F32))[:]

        def sem(n):
            return nc.alloc_semaphore(f"{name}_{n}")

        hh, mm, xn, mn, live, v, w, z, f = (col(n) for n in ("hh", "mm", "xn", "mn", "live", "v", "w", "z", "f"))
        steps, sums_ready, roots_ready, log_in, log_out, tanh_in, tanh_out = (
            sem("steps"), sem("sums_ready"), sem("roots_ready"), sem("log_in"), sem("log_out"), sem("tanh_in"), sem("tanh_out"))
        h3 = haug[:].rearrange("p (t w) -> p t w", t=NT)
        g3 = gaug[:].rearrange("p (t w) -> p t w", t=NT)
        mx3 = mx[:].rearrange("p (t d) -> p t d", t=NT)
        block = ctx.enter_context(nc.Block())

        @block.vector
        def _(dve):
            chain = Chain(dve, steps)
            square_sums(chain, dve, h3[:, :, 0:D], g3[:, :, 0:D], hh)
            square_sums(chain, dve, mx3, g3[:, :, 0:D], mm)
            chain(dve.tensor_scalar(live, mm, EPS3 * EPS3, None, ALU.is_gt))
            chain(dve.tensor_scalar(hh, hh, EPS3 * EPS3, None, ALU.max))
            dve.tensor_scalar(mm, mm, EPS3 * EPS3, None, ALU.max).then_inc(sums_ready, 1)
            dve.wait_ge(roots_ready, 2)
            chain(dve.reciprocal(f, xn))
            chain(dve.tensor_tensor(f, f, mn, ALU.mult))
            artanh_before(chain, dve, xn, v, w)
            dve.sem_inc(log_in, 1)
            dve.wait_ge(log_out, 1)
            artanh_after(chain, dve, xn, v, w, z)
            chain(dve.tensor_tensor(v, v, f, ALU.mult))
            dve.sem_inc(tanh_in, 1)
            dve.wait_ge(tanh_out, 1)
            chain(dve.tensor_tensor(v, v, live, ALU.mult))
            chain(dve.tensor_tensor(w, v, v, ALU.mult))
            chain(dve.tensor_scalar(w, w, -1.0, 1.0, ALU.mult, ALU.add))
            chain(dve.reciprocal(w, w))
            chain(dve.tensor_scalar(w, w, 2.0, 1e-15, ALU.mult, ALU.max))
            chain(dve.tensor_scalar(g3[:, :, D], w, -1.0, None, ALU.add))
            chain(dve.memset(g3[:, :, D + 1], 1.0))
            chain(dve.reciprocal(f, mn))
            chain(dve.tensor_tensor(f, f, v, ALU.mult))
            chain(dve.tensor_tensor(f, f, w, ALU.mult))
            chain(dve.tensor_tensor(g3[:, :, 0:D], mx3, f.rearrange("p (t o) -> p t o", o=1).to_broadcast([P, NT, D]), ALU.mult))

        @block.scalar
        def _(act):
            act.wait_ge(sums_ready, 1)
            act.activation(xn, hh, ACT.Sqrt).then_inc(roots_ready, 1)
            act.activation(mn, mm, ACT.Sqrt).then_inc(roots_ready, 1)
            act.wait_ge(log_in, 1)
            act.activation(v, v, ACT.Ln).then_inc(log_out, 1)
            act.wait_ge(tanh_in, 1)
            act.activation(v, v, ACT.Tanh).then_inc(tanh_out, 1)


def mean_sums(nc, name, adjT, gaug, U):
    width = D + 2
    with ExitStack() as ctx:
        def sem(n):
            return nc.alloc_semaphore(f"{name}_{n}")

        ring = ctx.enter_context(nc.sbuf_tensor(f"{name}_ring", [P, 5, 2, W], F32))
        acc = [ctx.enter_context(nc.psum_tensor(f"{name}_acc{k}", [P, W], F32)) for k in range(8)]
        adj_in = [sem(f"adj_in{k}") for k in range(5)]
        summed, stored = sem("summed"), sem("stored")
        block = ctx.enter_context(nc.Block())

        @block.sync
        def _(sp):
            load_blocks(sp, adjT, ring, adj_in, summed, 0)

        @block.tensor
        def _(pe):
            def sums(b, w, g, slot, first, last):
                arrived(pe, adj_in, b, g, slot)
                for u in range(2):
                    for q in range(w // P):
                        if first and u == 0:
                            pe.wait_ge(stored, b * 4 + q + 1)
                        mm = pe.matmul(acc[q][:, 0:width], ring[:, slot, u, q * P:(q + 1) * P],
                                       gaug[:, cols(g * 2 * width + u * width, width)],
                                       start=(first and u == 0), stop=(last and u == 1))
                mm.then_inc(summed, 1)

            def one(b, w, next_w):
                sums(b, w, 0, FIRST, True, False)
                later = NGRP // 4
                with pe.Fori(0, later - 1) as i:
                    for u in range(4):
                        sums(b, w, i * 4 + u + 1, u, False, False)
                for u in range(4):
                    g = (later - 1) * 4 + u + 1
                    sums(b, w, g, u, False, g == NGRP - 1)
            over_blocks(pe, one)

        @block.vector
        def _(dve):
            dve.sem_inc(summed, 5)
            dve.sem_inc(stored, 4)

            def one(b, w, next_w):
                dve.wait_ge(summed, b * NGRP + NGRP + 5)
                for q in range(w // P):
                    dve.tensor_copy(U[:, cols(b * 4 * width + q * width, width)], acc[q][:, 0:width]).then_inc(stored, 1)
            over_blocks(dve, one)


def hyper_mean(nc, m, name, U, big):
    with ExitStack() as ctx:
        def col(n):
            return ctx.enter_context(nc.sbuf_tensor(f"{name}_{n}", [P, NT], F32))[:]

        def sem(n):
            return nc.alloc_semaphore(f"{name}_{n}")

        ss, d, k, q, y, v, w, z = (col(n) for n in ("ss", "d", "k", "q", "y", "v", "w", "z"))
        steps, root_in, root_out, log_in, log_out, tanh_in, tanh_out = (
            sem("steps"), sem("root_in"), sem("root_out"), sem("log_in"), sem("log_out"), sem("tanh_in"), sem("tanh_out"))
        U3 = U[:].rearrange("p (t w) -> p t w", t=NT)
        big3 = big[:].rearrange("p (t d) -> p t d", t=NT)
        x3 = m.x[:].rearrange("p (t d) -> p t d", t=NT)
        nom, den, alpha = U3[:, :, 0:D], U3[:, :, D], U3[:, :, D + 1]

        def wide(c):
            return c.rearrange("p (t o) -> p t o", o=1).to_broadcast([P, NT, D])
        block = ctx.enter_context(nc.Block())

        @block.vector
        def _(dve):
            chain = Chain(dve, steps)

            def norm_of(factor, squares, number):
                if factor is not None:
                    chain(dve.tensor_tensor(y, factor, factor, ALU.mult))
                    chain(dve.tensor_tensor(y, y, squares, ALU.mult))
                    chain(dve.tensor_scalar(y, y, EPS3 * EPS3, None, ALU.max))
                else:
                    chain(dve.tensor_scalar(y, squares, EPS3 * EPS3, None, ALU.max))
                dve.sem_inc(root_in, 1)
                dve.wait_ge(root_out, number)

            square_sums(chain, dve, nom, big3, ss)
            chain(dve.tensor_scalar(d, den, 0.0, 2.0, ALU.is_ge, ALU.mult))
            chain(dve.tensor_scalar(d, d, -1.0, None, ALU.add))
            chain(dve.tensor_tensor(v, d, den, ALU.mult))
            chain(dve.tensor_scalar(v, v, EPS3, None, ALU.max))
            chain(dve.tensor_tensor(d, d, v, ALU.mult))
            chain(dve.reciprocal(d, d))
            chain(dve.tensor_tensor(y, d, d, ALU.mult))
            chain(dve.tensor_tensor(y, y, ss, ALU.mult))
            chain(dve.tensor_scalar(y, y, -1.0, 1.0, ALU.mult, ALU.add))
            chain(dve.tensor_scalar(y, y, EPS3, None, ALU.max))
            dve.sem_inc(root_in, 1)
            dve.wait_ge(root_out, 1)
            chain(dve.tensor_scalar(y, y, 1.0, None, ALU.add))
            chain(dve.reciprocal(y, y))
            chain(dve.tensor_tensor(k, d, y, ALU.mult))
            norm_of(k, ss, 2)
            chain(dve.reciprocal(q, y))
            chain(dve.tensor_tensor(k, k, q, ALU.mult))
            artanh_before(chain, dve, y, v, w)
            dve.sem_inc(log_in, 1)
            dve.wait_ge(log_out, 1)
            artanh_after(chain, dve, y, v, w, z)
            chain(dve.tensor_tensor(v, v, alpha, ALU.mult))
            dve.sem_inc(tanh_in, 1)
            dve.wait_ge(tanh_out, 1)
            chain(dve.tensor_tensor(k, k, v, ALU.mult))
            norm_of(k, ss, 3)
            chain(dve.reciprocal(q, y))
            chain(dve.tensor_tensor(k, k, q, ALU.mult))
            artanh_before(chain, dve, y, v, w)
            dve.sem_inc(log_in, 1)
            dve.wait_ge(log_out, 2)
            artanh_after(chain, dve, y, v, w, z)
            chain(dve.tensor_tensor(k, k, v, ALU.mult))
            chain(dve.tensor_tensor(nom, nom, wide(k), ALU.mult))
            chain(dve.tensor_scalar(nom, nom, 0.0, None, ALU.max))
            square_sums(chain, dve, nom, big3, ss)
            norm_of(None, ss, 4)
            chain(dve.reciprocal(q, y))
            chain(dve.tensor_copy(v, y))
            dve.sem_inc(tanh_in, 1)
            dve.wait_ge(tanh_out, 2)
            chain(dve.tensor_tensor(q, q, v, ALU.mult))
            chain(dve.tensor_tensor(nom, nom, wide(q), ALU.mult))
            chain(dve.tensor_tensor(x3, x3, nom, ALU.add))

        @block.scalar
        def _(act):
            def root(n):
                act.wait_ge(root_in, n)
                act.activation(y, y, ACT.Sqrt).then_inc(root_out, 1)

            def log(n):
                act.wait_ge(log_in, n)
                act.activation(v, v, ACT.Ln).then_inc(log_out, 1)

            def tanh(n):
                act.wait_ge(tanh_in, n)
                act.activation(v, v, ACT.Tanh).then_inc(tanh_out, 1)

            root(1)
            root(2)
            log(1)
            tanh(1)
            root(3)
            log(2)
            root(4)
            tanh(2)


def store(nc, m, out):
    body_out, last_out = nc.alloc_semaphore("body_out"), nc.alloc_semaphore("last_out")
    with nc.Block() as block:
        @block.sync
        def _(sp):
            xt = m.x[:].rearrange("p (t d) -> p t d", t=NT)
            sp.dma_start(out[0:(NT - 1) * P, :].rearrange("(t p) d -> p t d", p=P), xt[:, 0:NT - 1, :]).then_inc(body_out, 16)
            sp.dma_start(out[(NT - 1) * P:N, :], xt[0:N - (NT - 1) * P, NT - 1, :]).then_inc(last_out, 16)
            sp.wait_ge(body_out, 16)
            sp.wait_ge(last_out, 16)


class Io:
    pass


def attention_layer(nc, m, io, name, graphs):
    with nc.cleanup_on_exit(), ExitStack() as layer:
        def sb(n, s, d=F32):
            return layer.enter_context(nc.sbuf_tensor(f"{name}_{n}", s, d))

        hh = sb("hh", [P, NT * (D + 2)], F16)
        hl = sb("hl", [P, NT * (D + 2)], F16)
        negm = sb("negm", [P, NT])
        zoff = sb("zoff", [P, NT]) if graphs else None
        q_parts = (sb("qh", [P, 2 * NQ], F16), sb("ql", [P, 2 * NQ], F16))
        k_parts = (sb("kh", [P, 2 * NP], F16), sb("kl", [P, 2 * NP], F16))
        augI = sb("augI", [P, NQ], BF16)
        augJ = sb("augJ", [P, NP], BF16)
        with nc.sbuf_tensor(f"{name}_hT", [P, 2 * NP], F32) as m.hT:
            norm(nc, m, f"{name}_norm", True, hh, hl)
            queries_keys(nc, m, f"{name}_qk", io.w[name + "q"], io.w[name + "k"], io.b[name + "q"],
                         io.b[name + "k"], q_parts, k_parts)
        with nc.sbuf_tensor(f"{name}_notJ", [P, NP], BF16) as notJ:
            if graphs:
                aug_graphs(nc, name, io.ptr, augI, augJ, notJ, q_parts)
            else:
                aug_plain(nc, name, augI, augJ, q_parts)
            row_max(nc, f"{name}_max", io.adj, q_parts[0], k_parts[0], graphs, augI, augJ, notJ, negm, zoff)
        shift_rows(nc, m, f"{name}_shift", negm, augI)
        U = sb("U", [P, NT * (D + 2)])
        attend(nc, f"{name}_att", io.adjT, q_parts, k_parts, augI, augJ, hh, hl, U)
        project(nc, m, f"{name}_out", U, io.w[name + "v"], io.b[name + "v"], zoff)


def gat_layer(nc, m, io):
    with nc.cleanup_on_exit(), ExitStack() as layer:
        def sb(n, s, d=F32):
            return layer.enter_context(nc.sbuf_tensor(f"L1_{n}", s, d))

        haug = sb("haug", [P, NT * (D + 2)])
        m.hT = sb("hT", [P, 2 * NP])
        wa = sb("wa", [P, 2, 2 * HEADS])
        scol, dcol, d01, negm = (sb(n, [P, HEADS, NT]) for n in ("scol", "dcol", "d01", "negm"))
        norm(nc, m, "L1_norm", False, haug, None)
        with nc.sbuf_tensor("L1_dbc", [P, HEADS * NP], F32) as dbc:
            gat_vectors(nc, m, "L1_vec", io, wa, scol, dcol, d01, dbc)
            gat_max(nc, "L1_max", io.adj, scol, dbc, negm)
        gat(nc, m, "L1_gat", io, wa, dcol, d01, negm, haug)


def hyper_layer(nc, m, io):
    with nc.cleanup_on_exit(), ExitStack() as layer:
        def sb(n, s, d=F32):
            return layer.enter_context(nc.sbuf_tensor(f"L3_{n}", s, d))

        gaug = sb("gaug", [P, NT * (D + 2)])
        with nc.sbuf_tensor("L3_haug", [P, NT * (D + 2)], F32) as haug, \
                nc.sbuf_tensor("L3_mx", [P, NT * D], F32) as mx:
            with nc.sbuf_tensor("L3_hT", [P, 2 * NP], F32) as m.hT:
                norm(nc, m, "L3_norm", False, haug, None)
            row_product(nc, m, "L3_mx", haug, D + 2, m.ones, mx, io.w["L3"])
            hyper_points(nc, "L3_points", haug, mx, gaug)
        U = sb("U", [P, NT * (D + 2)])
        big = sb("big", [P, NT * D])
        mean_sums(nc, "L3_mean", io.adjT, gaug, U)
        hyper_mean(nc, m, "L3_out", U, big)


def program(nc, io, layers):
    with ExitStack() as ctx:
        m = Mem()
        setup(nc, ctx, m, io)
        if "L0" in layers:
            attention_layer(nc, m, io, "L0", True)
        if "L1" in layers:
            gat_layer(nc, m, io)
        if "L2" in layers:
            attention_layer(nc, m, io, "L2", False)
        if "L3" in layers:
            hyper_layer(nc, m, io)
        store(nc, m, io.out)


LAYERS = ("L0", "L1", "L2", "L3")


def kernel(**inputs):
    import concourse.bacc as bacc
    from concourse.bass_utils import run_bass_kernel_spmd as run

    nc = bacc.Bacc("TRN2", target_bir_lowering=False, num_devices=1)
    arrays = {}

    def given(name, array):
        array = np.ascontiguousarray(array)
        arrays[name] = array
        return nc.dram_tensor(name, array.shape, mybir.dt.from_np(array.dtype), kind="ExternalInput").ap()

    adj = np.asarray(inputs["adj"])
    pad = ((0, NP - N), (0, NP - N))
    io = Io()
    io.x = given("x", inputs["x"])
    io.adj = given("adj_padded", np.pad(adj, pad))
    io.adjT = given("adj_transposed", np.pad(adj.T, pad))
    io.ptr = given("ptr", np.asarray(inputs["L0_gnn_ptr"]).reshape(NG, 1))
    io.w, io.b = {}, {}
    for layer in ("L0", "L2"):
        for k in "qkv":
            io.w[layer + k] = given(f"{layer}_W{k}_transposed", np.asarray(inputs[f"{layer}_gnn_W{k}"]).T)
            b = np.asarray(inputs[f"{layer}_gnn_b{k}"])
            io.b[layer + k] = given(f"{layer}_b{k}", b if k == "v" else b.reshape(2, P).T)
    io.w["L1"] = given("L1_W", inputs["L1_gnn_W"])
    io.w["L1T"] = given("L1_W_transposed", np.asarray(inputs["L1_gnn_W"]).T)
    io.a = given("L1_a", np.asarray(inputs["L1_gnn_a"]).reshape(HEADS, 2, 2, P).transpose(3, 0, 2, 1))
    io.w["L3"] = given("L3_W", inputs["L3_gnn_W"])
    io.out = nc.dram_tensor("out", (N, D), F32, kind="ExternalOutput").ap()
    program(nc, io, LAYERS)
    return run(nc, [arrays], core_ids=[0]).results[0]["out"]
```

```python
from contextlib import ExitStack

import numpy as np
import concourse.bass as bass
from concourse import mybir

ALU = mybir.AluOpType
ACT = mybir.ActivationFunctionType
AX = mybir.AxisListType
F32 = mybir.dt.float32
F16 = mybir.dt.float16
BF16 = mybir.dt.bfloat16
I32 = mybir.dt.int32

P = 128
N = 3327
D = 256
NT = (N + P - 1) // P
NP = NT * P
HEADS = 4
NG = 33
W = 512
NB = NP // W
TAIL = NP - NB * W
NGRP = NT // 2
HALF = NP // 2
BIG = float(2.0 ** 100)
EPS = 1e-5
LOG_P = float(np.log(256.0))


class Mem:
    pass


def cols(start, size):
    return bass.ds(start, size)


def chunks(total, size):
    return [(a, min(size, total - a)) for a in range(0, total, size)]


def wait_apart(eng, sem, value, waited):
    eng.wait_ge(sem, value)
    eng.sem_inc(waited, 1)


def setup(nc, ctx, m, io):
    def sb(n, s, d=F32):
        return ctx.enter_context(nc.sbuf_tensor(n, s, d))

    m.x = sb("state", [P, NT * D])
    m.ident = sb("ident", [P, P])
    m.identb = sb("identb", [P, P], BF16)
    m.ones = sb("ones", [P, P])
    m.padneg = sb("padneg", [P, 1])
    m.rstd = sb("rstd", [P, NT])
    m.nbias = sb("nbias", [P, NT])
    x_cleared, x_body, x_last, set_steps, pool_steps = (
        nc.alloc_semaphore(n) for n in ("x_cleared", "x_body", "x_last", "set_steps", "pool_steps"))
    with nc.sbuf_tensor("pidx", [P, 1], F32) as pidx, nc.Block() as block:
        xt = m.x[:].rearrange("p (t d) -> p t d", t=NT)

        @block.sync
        def _(sp):
            sp.dma_start(xt[:, 0:NT - 1, :],
                         io.x[0:(NT - 1) * P, :].rearrange("(t p) d -> p t d", p=P)).then_inc(x_body, 16)
            sp.wait_ge(x_cleared, 1)
            sp.dma_start(xt[0:N - (NT - 1) * P, NT - 1, :], io.x[(NT - 1) * P:N, :]).then_inc(x_last, 16)
            sp.wait_ge(x_body, 16)
            sp.wait_ge(x_last, 16)

        @block.gpsimd
        def _(pool):
            pool.iota(pidx[:], pattern=[[0, 1]], base=0, channel_multiplier=1,
                      allow_small_or_imprecise_dtypes=True).then_inc(pool_steps, 1)
            pool.memset(m.ident[:], 0.0).then_inc(pool_steps, 1)
            pool.wait_ge(pool_steps, 2)
            pool.affine_select(out=m.ident[:], in_=m.ident[:], compare_op=ALU.not_equal, fill=1.0,
                               base=0, pattern=[[-1, P]], channel_multiplier=1).then_inc(pool_steps, 1)

        @block.vector
        def _(dve):
            dve.memset(xt[:, NT - 1, :], 0.0).then_inc(x_cleared, 1)
            dve.memset(m.ones[:], 1.0).then_inc(set_steps, 1)
            dve.wait_ge(pool_steps, 3)
            dve.tensor_copy(m.identb[:], m.ident[:]).then_inc(set_steps, 1)
            dve.tensor_scalar(m.padneg[:], pidx[:], float(P - 1), -1e30, ALU.is_ge,
                              ALU.mult).then_inc(set_steps, 1)


def norm(nc, m, name, split, haug, hlow):
    width = D + 2
    with ExitStack() as ctx:
        def sb(n, s, d=F32):
            return ctx.enter_context(nc.sbuf_tensor(f"{name}_{n}", s, d))

        def sem(n):
            return nc.alloc_semaphore(f"{name}_{n}")

        stat = sb("stat", [P, 2 * 6])
        mv = sb("mv", [P, 2 * 2])
        mvall = sb("mvall", [P, NT, 2])
        std = sb("std", [P, NT])
        stage = sb("stage", [P, 2, D])
        psT = ctx.enter_context(nc.psum_tensor(f"{name}_psT", [P, 2, W], F32))
        stat_steps, waited = sem("stat_steps"), sem("waited")
        var_ready, std_ready, scale_ready = sem("var_ready"), sem("std_ready"), sem("scale_ready")
        row_steps = sem("row_steps")
        h_ready, transposed, h_split, hT_stored = sem("h_ready"), sem("transposed"), sem("h_split"), sem("hT_stored")
        block = ctx.enter_context(nc.Block())
        hT3 = m.hT[:].rearrange("p (c n) -> p c n", c=2)
        ha = haug[:].rearrange("p (t w) -> p t w", t=NT)

        @block.vector
        def _(dve):
            with dve.Fori(0, NT // 2) as i:
                for u in range(2):
                    dve.bn_stats(stat[:, 6 * u:6 * u + 6], m.x[:, cols(i * 2 * D + u * D, D)]).then_inc(stat_steps, 1)
                for u in range(2):
                    wait_apart(dve, stat_steps, i * 4 + 1 + u, waited)
                    dve.bn_aggr(mv[:, 2 * u:2 * u + 2], stat[:, 6 * u:6 * u + 6]).then_inc(stat_steps, 1)
                dve.wait_ge(stat_steps, i * 4 + 4)
                dve.tensor_copy(mvall[:].rearrange("p t k -> p (t k)")[:, cols(i * 4, 4)], mv[:]).then_inc(row_steps, 1)
            dve.wait_ge(row_steps, NT // 2)
            dve.tensor_scalar(std[:], mvall[:, :, 1], EPS, None, ALU.add).then_inc(var_ready, 1)
            dve.wait_ge(std_ready, 1)
            dve.reciprocal(m.rstd[:], std[:]).then_inc(row_steps, 1)
            dve.wait_ge(row_steps, NT // 2 + 1)
            dve.scalar_tensor_tensor(out=m.nbias[:], in0=mvall[:, :, 0], scalar=-1.0, in1=m.rstd[:],
                                     op0=ALU.mult, op1=ALU.mult).then_inc(scale_ready, 1)
            dve.memset(ha[:, :, D:D + 2], 1.0).then_inc(row_steps, 1)
            if split:
                dve.memset(hlow[:].rearrange("p (t w) -> p t w", t=NT)[:, :, D:D + 2], 0.0).then_inc(row_steps, 1)
            with dve.Fori(0, NT // 2) as i:
                for u in range(2):
                    at = i * 2 * width + u * width
                    dve.wait_ge(h_ready, i * 2 + u + 1)
                    if split:
                        dve.tensor_copy(haug[:, cols(at, D)], stage[:, u, :]).then_inc(row_steps, 1)
                        dve.wait_ge(row_steps, i * 2 + u + NT // 2 + 4)
                        dve.tensor_tensor(hlow[:, cols(at, D)], stage[:, u, :], haug[:, cols(at, D)],
                                          ALU.subtract).then_inc(h_split, 1)
                    else:
                        dve.tensor_copy(haug[:, cols(at, D)], stage[:, u, :]).then_inc(h_split, 1)
                    dve.wait_ge(transposed, i * 2 + u + 1)
                    dve.tensor_copy(hT3[:, :, cols(i * 2 * P + u * P, P)],
                                    psT[:, u, 0:2 * P].rearrange("p (c n) -> p c n", c=2)).then_inc(hT_stored, 1)

        @block.scalar
        def _(act):
            act.preload_act_table(ACT.Sqrt)
            act.wait_ge(var_ready, 1)
            act.activation(std[:], std[:], ACT.Sqrt).then_inc(std_ready, 1)
            act.preload_act_table(ACT.Exp)
            act.wait_ge(scale_ready, 1)
            for u in range(2):
                act.activation(stage[:, u, :], m.x[:, u * D:(u + 1) * D], ACT.Relu,
                               scale=m.rstd[:, u:u + 1], bias=m.nbias[:, u:u + 1]).then_inc(h_ready, 1)
            with act.Fori(1, NT // 2) as i:
                for u in range(2):
                    act.wait_ge(h_split, i * 2 + u - 1)
                    act.wait_ge(transposed, i * 2 + u - 1)
                    act.activation(stage[:, u, :], m.x[:, cols(i * 2 * D + u * D, D)], ACT.Relu,
                                   scale=m.rstd[:, cols(i * 2 + u, 1)],
                                   bias=m.nbias[:, cols(i * 2 + u, 1)]).then_inc(h_ready, 1)

        @block.tensor
        def _(pe):
            pe.wait_ge(h_ready, 1)
            for u in range(2):
                pe.wait_ge(h_ready, u + 1)
                for c in range(2):
                    mm = pe.transpose(psT[:, u, c * P:(c + 1) * P], stage[:, u, c * P:(c + 1) * P], m.ident[:])
                mm.then_inc(transposed, 1)
            with pe.Fori(1, NT // 2) as i:
                for u in range(2):
                    pe.wait_ge(h_ready, i * 2 + u + 1)
                    pe.wait_ge(hT_stored, i * 2 + u - 1)
                    for c in range(2):
                        mm = pe.transpose(psT[:, u, c * P:(c + 1) * P], stage[:, u, c * P:(c + 1) * P], m.ident[:])
                    mm.then_inc(transposed, 1)


def queries_keys(nc, m, name, io_q, io_k, bq, bk, q_parts, k_parts):
    with ExitStack() as ctx:
        def sb(n, s, d=F32):
            return ctx.enter_context(nc.sbuf_tensor(f"{name}_{n}", s, d))

        def sem(n):
            return nc.alloc_semaphore(f"{name}_{n}")

        wt = [sb(f"w{k}", [P, 2, D]) for k in "qk"]
        bias = [sb(f"b{k}", [P, 2]) for k in "qk"]
        whole = sb("whole", [P, 4, W])
        ps = ctx.enter_context(nc.psum_tensor(f"{name}_ps", [P, 4, W], F32))
        weights_in = [sem(f"weights_in{k}") for k in range(4)]
        bias_scaled = sem("bias_scaled")
        product_done, whole_ready, high_ready, low_ready = sem("product_done"), sem("whole_ready"), sem("high_ready"), sem("low_ready")
        block = ctx.enter_context(nc.Block())
        parts = [q_parts, k_parts]

        @block.sync
        def _(sp):
            for k, src in enumerate((io_q, io_k)):
                sp.dma_start(wt[k][:], src.rearrange("(c p) d -> p c d", p=P)).then_inc(weights_in[k], 16)
            for k, src in enumerate((bq, bk)):
                sp.dma_start(bias[k][:], src).then_inc(weights_in[2 + k], 16)

        def each_block(eng, body):
            with eng.Fori(0, NB) as b:
                body(b, W, b * 4)
            body(NB, TAIL, NB * 4)

        @block.tensor
        def _(pe):
            for s in weights_in[0:2]:
                pe.wait_ge(s, 16)

            def body(b, w, done):
                for k in range(4):
                    pe.wait_ge(whole_ready, done + k + 1)
                    for c in range(2):
                        mm = pe.matmul(ps[:, k, 0:w], wt[k // 2][:, c, (k % 2) * P:(k % 2 + 1) * P],
                                       m.hT[:, cols(b * W + c * NP, w)], start=(c == 0), stop=(c == 1))
                    mm.then_inc(product_done, 1)
            each_block(pe, body)

        @block.scalar
        def _(act):
            act.preload_act_table(ACT.Exp)
            for s in weights_in[2:4]:
                act.wait_ge(s, 16)
            act.mul(bias[0][:], bias[0][:], 1.0 / 32).then_inc(bias_scaled, 1)
            act.sem_inc(whole_ready, 4)
            act.wait_ge(bias_scaled, 1)

            def body(b, w, done):
                for k in range(4):
                    act.wait_ge(product_done, done + k + 1)
                    act.wait_ge(low_ready, done + k + 1)
                    act.activation(whole[:, k, 0:w], ps[:, k, 0:w], ACT.Identity, bias=bias[k // 2][:, k % 2:k % 2 + 1],
                                   scale=1.0 / 32 if k < 2 else 1.0).then_inc(whole_ready, 1)
            each_block(act, body)

        @block.vector
        def _(dve):
            dve.sem_inc(low_ready, 4)

            def body(b, w, done):
                for k in range(4):
                    high, low = parts[k // 2]
                    at = cols(b * W + (k % 2) * (NQ if k < 2 else NP), w)
                    dve.wait_ge(whole_ready, done + k + 5)
                    dve.tensor_copy(high[:, at], whole[:, k, 0:w]).then_inc(high_ready, 1)
                    dve.wait_ge(high_ready, done + k + 1)
                    dve.tensor_tensor(low[:, at], whole[:, k, 0:w], high[:, at], ALU.subtract).then_inc(low_ready, 1)
            each_block(dve, body)


NQ = (NB + 1) * W


def aug_plain(nc, name, augI, augJ, q_parts):
    aug_steps = nc.alloc_semaphore(f"{name}_aug_steps")
    with nc.Block() as block:
        @block.vector
        def _(dve):
            dve.memset(augI[:], 0.0).then_inc(aug_steps, 1)
            dve.memset(augJ[:], 0.0).then_inc(aug_steps, 1)
            for q in q_parts:
                for c in range(2):
                    dve.memset(q[:, c * NQ + NP:(c + 1) * NQ], 0.0).then_inc(aug_steps, 1)
            dve.wait_ge(aug_steps, 6)
            dve.memset(augI[0:1, :], 1.0).then_inc(aug_steps, 1)
            dve.memset(augJ[0:1, N:NP], -BIG).then_inc(aug_steps, 1)
            dve.memset(augJ[64:67, :], 1.0).then_inc(aug_steps, 1)


def aug_graphs(nc, name, ptr, augI, augJ, notJ, q_parts):
    with ExitStack() as ctx:
        def sb(n, s, d=F32):
            return ctx.enter_context(nc.sbuf_tensor(f"{name}_{n}", s, d))

        def sem(n):
            return nc.alloc_semaphore(f"{name}_{n}")

        G = NG + 1
        bounds = sb("bounds", [G, 2], I32)
        edges = sb("edges", [G, 2])
        node = sb("node", [G, NP])
        hot = sb("hot", [G, NP])
        bounds_cleared, low_in, high_in, node_ready, dve_steps = (
            sem("bounds_cleared"), sem("low_in"), sem("high_in"), sem("node_ready"), sem("dve_steps"))
        block = ctx.enter_context(nc.Block())

        @block.sync
        def _(sp):
            sp.wait_ge(bounds_cleared, 1)
            sp.dma_start(bounds[1:G, 0:1], ptr).then_inc(low_in, 16)
            sp.dma_start(bounds[0:G - 1, 1:2], ptr).then_inc(high_in, 16)

        @block.gpsimd
        def _(pool):
            pool.iota(node[:], pattern=[[1, NP]], base=0, channel_multiplier=0,
                      allow_small_or_imprecise_dtypes=True).then_inc(node_ready, 1)

        @block.vector
        def _(dve):
            steps = 0

            def done(ins):
                nonlocal steps
                steps += 1
                ins.then_inc(dve_steps, 1)
                return steps

            done(dve.memset(bounds[:, 0:1], -1))
            dve.memset(bounds[:, 1:2], 1 << 30).then_inc(dve_steps, 1)
            steps += 1
            dve.wait_ge(dve_steps, 2)
            dve.memset(edges[:], 0.0).then_inc(bounds_cleared, 1)
            done(dve.memset(augI[:], 0.0))
            done(dve.memset(augJ[:], 0.0))
            done(dve.memset(notJ[:], 0.0))
            for q in q_parts:
                for c in range(2):
                    done(dve.memset(q[:, c * NQ + NP:(c + 1) * NQ], 0.0))
            dve.wait_ge(low_in, 16)
            dve.wait_ge(high_in, 16)
            dve.wait_ge(bounds_cleared, 1)
            n = done(dve.tensor_copy(edges[:], bounds[:]))
            dve.wait_ge(dve_steps, n)
            dve.wait_ge(node_ready, 1)
            n = done(dve.tensor_scalar(hot[:], node[:], edges[:, 0:1], None, ALU.is_ge))
            dve.wait_ge(dve_steps, n)
            n = done(dve.scalar_tensor_tensor(out=hot[:], in0=node[:], scalar=edges[:, 1:2], in1=hot[:],
                                              op0=ALU.is_lt, op1=ALU.mult))
            dve.wait_ge(dve_steps, n)
            done(dve.tensor_scalar(augI[0:G, 0:NP], hot[:], -BIG, None, ALU.mult))
            done(dve.tensor_scalar(augJ[0:G, :], hot[:], -1.0, 1.0, ALU.mult, ALU.add))
            n = done(dve.tensor_scalar(notJ[0:G, :], hot[:], -1.0, None, ALU.mult))
            dve.wait_ge(dve_steps, n)
            done(dve.memset(augJ[0:G, N:NP], 1.0))
            done(dve.memset(notJ[0:G, N:NP], -1.0))
            done(dve.memset(augJ[64:67, :], 1.0))


def row_max(nc, name, adj, qh, kh, graphs, augI, augJ, notJ, negm, zoff):
    with ExitStack() as ctx:
        def sb(n, s, d=F32):
            return ctx.enter_context(nc.sbuf_tensor(f"{name}_{n}", s, d))

        def sem(n):
            return nc.alloc_semaphore(f"{name}_{n}")

        rows = sb("rows", [P, 2, NP])
        junk = sb("junk", [P, 2, HALF], BF16)
        best = sb("best", [P, 2, 2])
        least = sb("least", [P, 2, 2])
        top = sb("top", [P, 2])
        low = sb("low", [P, 2])
        if graphs:
            masked = sb("masked", [P, 2, NP])
            junk2 = sb("junk2", [P, NP], BF16)
            shift = sb("shift", [P, 2])
            zt = sb("zt", [P, 2])
        ps = [ctx.enter_context(nc.psum_tensor(f"{name}_ps{k}", [P, 4 * W], F32)) for k in range(2)]
        rows_in = [sem(f"rows_in{k}") for k in range(2)]
        rows_used, products, bank_free, max_steps = sem("rows_used"), sem("products"), sem("bank_free"), sem("max_steps")
        shift_ready, sums_ready, waited = sem("shift_ready"), sem("sums_ready"), sem("waited")
        block = ctx.enter_context(nc.Block())

        @block.sync
        def _(sp):
            with sp.Fori(0, NT // 2) as i:
                for u in range(2):
                    sp.wait_ge(rows_used, i * 2 + u + 1)
                    sp.dma_start(rows[:, u, :], adj[cols(i * 2 * P + u * P, P), :]).then_inc(rows_in[u], 16)

        @block.tensor
        def _(pe):
            with pe.Fori(0, NT // 2) as i:
                for u in range(2):
                    at = i * 2 * P + u * P
                    for half in range(2):
                        kinds = ("scores", "graphs") if graphs else ("scores",)
                        for kind in kinds:
                            bank = kinds.index(kind) if graphs else half
                            n = len(kinds) * half + kinds.index(kind)
                            pe.wait_ge(bank_free, i * 4 * len(kinds) + u * 2 * len(kinds) + n + 1)
                            for a, w in chunks(HALF, W):
                                key = half * HALF + a
                                out = ps[bank][:, a:a + w]
                                if kind == "scores":
                                    for c in range(2):
                                        mm = pe.matmul(out, qh[:, cols(at + c * NQ, P)], kh[:, c * NP + key:c * NP + key + w],
                                                       start=(c == 0), stop=(c == 1 and not graphs))
                                    if graphs:
                                        mm = pe.matmul(out, augI[:, cols(at, P)], augJ[:, key:key + w],
                                                       start=False, stop=True)
                                else:
                                    mm = pe.matmul(out, augI[:, cols(at, P)], notJ[:, key:key + w], start=True, stop=True)
                            mm.then_inc(products, 1)

        per_half = 2 if graphs else 1

        @block.vector
        def _(dve):
            dve.sem_inc(bank_free, 2)
            dve.sem_inc(rows_used, 2)
            per_tile = 5 if graphs else 2
            with dve.Fori(0, NT // 2) as i:
                for u in range(2):
                    dve.wait_ge(rows_in[u], i * 16 + 16)
                    if graphs:
                        dve.wait_ge(sums_ready, i * 2 + u + 1)
                    for half in range(2):
                        a = half * HALF
                        w = HALF if half == 0 else N - HALF
                        done = i * 4 * per_half + (u * 2 + half) * per_half
                        wait_apart(dve, products, done + 1, waited)
                        dve.tensor_tensor_reduce(junk[:, half, 0:w], rows[:, u, a:a + w], ps[0 if graphs else half][:, 0:w], 1.0, -3e38,
                                                 ALU.add, ALU.max, best[:, u, half:half + 1]).then_inc(bank_free, 1)
                        if graphs:
                            wait_apart(dve, products, done + 2, waited)
                            dve.tensor_tensor_reduce(masked[:, u, a:a + HALF], rows[:, u, a:a + HALF], ps[1][:, 0:HALF], 1.0, 3e38,
                                                     ALU.add, ALU.min, least[:, u, half:half + 1]).then_inc(bank_free, 1)
                    dve.wait_ge(bank_free, i * 4 * per_half + (u + 1) * 2 * per_half + 2)
                    base = i * 2 * per_tile + u * per_tile
                    dve.tensor_tensor(top[:, u:u + 1], best[:, u, 0:1], best[:, u, 1:2], ALU.max).then_inc(max_steps, 1)
                    if graphs:
                        dve.tensor_tensor(low[:, u:u + 1], least[:, u, 0:1], least[:, u, 1:2], ALU.min).then_inc(max_steps, 1)
                        dve.wait_ge(max_steps, base + 2)
                        dve.scalar_tensor_tensor(out=top[:, u:u + 1], in0=low[:, u:u + 1], scalar=-1e6, in1=top[:, u:u + 1],
                                                 op0=ALU.mult, op1=ALU.max).then_inc(max_steps, 1)
                        dve.wait_ge(max_steps, base + 3)
                        dve.tensor_scalar(shift[:, u:u + 1], top[:, u:u + 1], -2.0, LOG_P, ALU.mult, ALU.add).then_inc(shift_ready, 1)
                        dve.tensor_scalar(negm[:, cols(i * 2 + u, 1)], top[:, u:u + 1], -1.0, LOG_P / 2, ALU.mult,
                                          ALU.add).then_inc(max_steps, 1)
                        dve.sem_inc(max_steps, 1)
                    else:
                        dve.wait_ge(max_steps, base + 1)
                        dve.tensor_scalar(negm[:, cols(i * 2 + u, 1)], top[:, u:u + 1], -1.0, LOG_P / 2, ALU.mult,
                                          ALU.add).then_inc(max_steps, 1)
                    dve.sem_inc(rows_used, 1)

        if graphs:
            @block.scalar
            def _(act):
                act.preload_act_table(ACT.Exp)
                act.sem_inc(sums_ready, 2)
                with act.Fori(0, NT // 2) as i:
                    for u in range(2):
                        act.wait_ge(shift_ready, i * 2 + u + 1)
                        act.activation(junk2[:], masked[:, u, :], ACT.Exp, bias=shift[:, u:u + 1], scale=-2e6,
                                       accum_out=zt[:, u:u + 1]).then_inc(sums_ready, 1)
                        act.wait_ge(sums_ready, i * 2 + u + 3)
                        act.copy(zoff[:, cols(i * 2 + u, 1)], zt[:, u:u + 1])


def shift_rows(nc, m, name, negm, augI):
    with ExitStack() as ctx:
        def sb(n, s, d=F32):
            return ctx.enter_context(nc.sbuf_tensor(f"{name}_{n}", s, d))

        def sem(n):
            return nc.alloc_semaphore(f"{name}_{n}")

        part = sb("part", [P, 3, NT], BF16)
        part32 = sb("part32", [P, NT, 3])
        rest = sb("rest", [P, 2, NT])
        diag = sb("diag", [P, 2, 3, P], BF16)
        pick = sb("pick", [P, 3, P], BF16)
        ps = ctx.enter_context(nc.psum_tensor(f"{name}_ps", [P, 2, W], F32))
        dve_steps, diag_ready, row_ready, row_stored = sem("dve_steps"), sem("diag_ready"), sem("row_ready"), sem("row_stored")
        block = ctx.enter_context(nc.Block())

        @block.vector
        def _(dve):
            dve.sem_inc(row_ready, 2)
            dve.memset(pick[:], 0.0).then_inc(dve_steps, 1)
            dve.tensor_copy(part[:, 0, :], negm[:]).then_inc(dve_steps, 1)
            dve.wait_ge(dve_steps, 2)
            for k in range(3):
                dve.memset(pick[:, k, 64 + k:65 + k], 1.0).then_inc(dve_steps, 1)
            dve.tensor_tensor(rest[:, 0, :], negm[:], part[:, 0, :], ALU.subtract).then_inc(dve_steps, 1)
            dve.wait_ge(dve_steps, 6)
            dve.tensor_copy(part[:, 1, :], rest[:, 0, :]).then_inc(dve_steps, 1)
            dve.wait_ge(dve_steps, 7)
            dve.tensor_tensor(rest[:, 1, :], rest[:, 0, :], part[:, 1, :], ALU.subtract).then_inc(dve_steps, 1)
            dve.wait_ge(dve_steps, 8)
            dve.tensor_copy(part[:, 2, :], rest[:, 1, :]).then_inc(dve_steps, 1)
            dve.wait_ge(dve_steps, 9)
            dve.tensor_copy(part32[:].rearrange("p t k -> p k t"), part[:]).then_inc(dve_steps, 1)
            dve.wait_ge(dve_steps, 10)
            scal = part32[:].rearrange("p t k -> p (t k)")
            with dve.Fori(0, NT // 2) as i:
                for u in range(2):
                    dve.wait_ge(row_ready, i * 2 + u + 1)
                    for k in range(3):
                        dve.tensor_scalar(diag[:, u, k, :], m.ident[:], scal[:, cols(i * 6 + u * 3 + k, 1)], None,
                                          ALU.mult).then_inc(diag_ready, 1)
                for u in range(2):
                    dve.wait_ge(row_ready, i * 2 + u + 3)
                    dve.tensor_copy(augI[64:67, cols(i * 2 * P + u * P, P)], ps[64:67, u, 0:P]).then_inc(row_stored, 1)

        @block.tensor
        def _(pe):
            with pe.Fori(0, NT // 2) as i:
                for u in range(2):
                    pe.wait_ge(diag_ready, i * 6 + u * 3 + 3)
                    for k in range(3):
                        mm = pe.matmul(ps[:, u, 0:P], pick[:, k, :], diag[:, u, k, :], start=(k == 0), stop=(k == 2))
                    mm.then_inc(row_ready, 1)


def over_blocks(eng, one):
    with eng.Fori(0, NB) as b:
        one(b, W, W)
    one(NB, TAIL, None)


def later_groups(eng, step, b, w, n0, begin=0):
    def four(i):
        for u in range(4):
            g = i * 4 + u + 1
            step(b, w, g, u, n0 + g)
    with eng.Fori(begin, NGRP // 4) as i:
        four(i)


FIRST = 4


def pslot(slot):
    return 2 if slot == FIRST else slot % 2


def bslot(slot):
    return 1 if slot == FIRST else slot % 2


def load_blocks(sp, adjT, ring, adj_in, used, n0):
    def step(b, w, g, slot, n):
        sp.wait_ge(used, n + (1 if slot == FIRST else 2))
        sp.dma_start(ring[:, slot, :, 0:w],
                     adjT[cols(g * 2 * P, 2 * P), cols(b * W, w)].rearrange("(u p) i -> p u i", p=P)
                     ).then_inc(adj_in[slot], 16)

    def one(b, w, next_w):
        n = n0 + b * NGRP
        step(b, w, 0, FIRST, n)
        later_groups(sp, step, b, w, n)
    over_blocks(sp, one)


def arrived(dve, adj_in, b, g, slot, before=0):
    if slot == FIRST:
        dve.wait_ge(adj_in[slot], (b + before) * 16 + 16)
    else:
        dve.wait_ge(adj_in[slot], (b + before) * 48 + (g - 1 - slot) * 4 + 16)


def attend(nc, name, adjT, q_parts, k_parts, augI, augJ, hh, hl, U):
    width = D + 2
    with ExitStack() as ctx:
        def sb(n, s, d=F32):
            return ctx.enter_context(nc.sbuf_tensor(f"{name}_{n}", s, d))

        def sem(n):
            return nc.alloc_semaphore(f"{name}_{n}")

        ring = sb("ring", [P, 5, 2, W])
        t = sb("t", [P, 3, 2, W])
        p32 = sb("p32", [P, 3, 2, W])
        ph = sb("ph", [P, 3, 2, W], F16)
        pl = sb("pl", [P, 3, 2, W], F16)
        psS = [ctx.enter_context(nc.psum_tensor(f"{name}_psS{k}", [P, 2, W], F32)) for k in range(2)]
        acc = [ctx.enter_context(nc.psum_tensor(f"{name}_acc{k}", [P, W], F32)) for k in range(4)]
        adj_in = [sem(f"adj_in{k}") for k in range(5)]
        scores_ready, added, exp_ready, probs_ready, summed, stored = (
            sem("scores_ready"), sem("added"), sem("exp_ready"), sem("probs_ready"), sem("summed"), sem("stored"))
        block = ctx.enter_context(nc.Block())

        @block.sync
        def _(sp):
            load_blocks(sp, adjT, ring, adj_in, added, 0)

        @block.tensor
        def _(pe):
            kh, kl = k_parts
            qh, ql = q_parts

            def scores(b, w, g, slot, need):
                pe.wait_ge(added, need)
                for u in range(2):
                    key = g * 2 * P + u * P
                    out = psS[bslot(slot)][:, u, 0:w]
                    pe.matmul(out, augJ[:, cols(key, P)], augI[:, cols(b * W, w)], start=True, stop=False)
                    for c in range(2):
                        high = kh[:, cols(key + c * NP, P)]
                        pe.matmul(out, high, qh[:, cols(b * W + c * NQ, w)], start=False, stop=False)
                        pe.matmul(out, high, ql[:, cols(b * W + c * NQ, w)], start=False, stop=False)
                        mm = pe.matmul(out, kl[:, cols(key + c * NP, P)], qh[:, cols(b * W + c * NQ, w)],
                                       start=False, stop=(c == 1))
                mm.then_inc(scores_ready, 1)

            def sums(b, w, g, slot, n, first, last):
                pe.wait_ge(probs_ready, n + 3)
                for u in range(2):
                    row = cols(g * 2 * width + u * width, width - 1)
                    for q in range(w // P):
                        if first and u == 0:
                            pe.wait_ge(stored, b * 4 + q + 1)
                        out = acc[q][:, 0:width - 1]
                        high = ph[:, pslot(slot), u, q * P:(q + 1) * P]
                        low = pl[:, pslot(slot), u, q * P:(q + 1) * P]
                        pe.matmul(out, high, hh[:, row], start=(first and u == 0), stop=False)
                        pe.matmul(out, high, hl[:, row], start=False, stop=False)
                        mm = pe.matmul(out, low, hh[:, row], start=False, stop=(last and u == 1))
                mm.then_inc(summed, 1)

            def one(b, w, next_w):
                n0 = b * NGRP

                def step(b, w, g, slot, n):
                    nxt = (slot + 1) % 4
                    scores(b, w, g + 1, nxt, n + 5)
                    sums(b, w, g, slot, n, False, False)

                scores(b, w, 1, 0, n0 + 5)
                sums(b, w, 0, FIRST, n0, True, False)
                later = NGRP // 4
                with pe.Fori(0, later - 1) as i:
                    for u in range(4):
                        step(b, w, i * 4 + u + 1, u, n0 + i * 4 + u + 1)
                for u in range(3):
                    g = (later - 1) * 4 + u + 1
                    step(b, w, g, u, n0 + g)
                n = n0 + NGRP - 1
                if next_w:
                    scores(b + 1, next_w, 0, FIRST, n + 6)
                sums(b, w, NGRP - 1, 3, n, False, True)

            scores(0, W, 0, FIRST, 5)
            over_blocks(pe, one)

        @block.vector
        def _(dve):
            dve.sem_inc(added, 5)
            dve.sem_inc(probs_ready, 2)

            def add(b, w, g, slot, n):
                s = pslot(slot)
                arrived(dve, adj_in, b, g, slot)
                dve.wait_ge(scores_ready, n + 1)
                dve.wait_ge(exp_ready, n * 2 + 2)
                dve.tensor_tensor(t[:, s, :, 0:w], ring[:, slot, :, 0:w], psS[bslot(slot)][:, :, 0:w],
                                  ALU.add).then_inc(added, 1)

            def low_half(w, slot, n):
                s = pslot(slot)
                dve.wait_ge(exp_ready, n * 2 + 6)
                dve.wait_ge(summed, n + 1)
                dve.tensor_tensor(pl[:, s, :, 0:w], p32[:, s, :, 0:w], ph[:, s, :, 0:w], ALU.subtract).then_inc(probs_ready, 1)

            def one(b, w, next_w):
                n0 = b * NGRP

                def step(b, w, g, slot, n):
                    low_half(w, (slot - 1) % 4, n - 1)
                    add(b, w, g, slot, n)

                low_half(w, FIRST, n0)
                add(b, w, 1, 0, n0 + 1)
                for u in range(1, 4):
                    step(b, w, u + 1, u, n0 + u + 1)
                later_groups(dve, step, b, w, n0, begin=1)
                if next_w:
                    add(b + 1, next_w, 0, FIRST, n0 + NGRP)
                low_half(w, 3, n0 + NGRP - 1)

            add(0, W, 0, FIRST, 0)
            over_blocks(dve, one)

        @block.scalar
        def _(act):
            act.preload_act_table(ACT.Exp)
            act.sem_inc(exp_ready, 4)
            act.sem_inc(stored, 4)
            act.sem_inc(summed, 2)

            def exps(b, w, g, slot, n):
                s = pslot(slot)
                act.wait_ge(added, n + 6)
                act.wait_ge(summed, n + 1)
                act.wait_ge(probs_ready, n + 1)
                act.activation(p32[:, s, :, 0:w], t[:, s, :, 0:w], ACT.Exp, scale=2.0).then_inc(exp_ready, 1)
                act.activation(ph[:, s, :, 0:w], t[:, s, :, 0:w], ACT.Exp, scale=2.0).then_inc(exp_ready, 1)

            def one(b, w, next_w):
                n0 = b * NGRP
                later_groups(act, exps, b, w, n0)
                if next_w:
                    exps(b + 1, next_w, 0, FIRST, n0 + NGRP)
                act.wait_ge(summed, n0 + NGRP + 2)
                for q in range(w // P):
                    act.copy(U[:, cols(b * 4 * width + q * width, width - 1)], acc[q][:, 0:width - 1]).then_inc(stored, 1)

            exps(0, W, 0, FIRST, 0)
            over_blocks(act, one)


class Chain:

    def __init__(self, eng, sem):
        self.eng, self.sem, self.count = eng, sem, 0

    def __call__(self, ins):
        self.count += 1
        ins.then_inc(self.sem, 1)
        self.eng.wait_ge(self.sem, self.count)


class RowProduct:

    def __init__(self, ctx, nc, m, name, src, src_width, scale, dst, plus, ps, pso):
        def sb(n, s, d=F32):
            return ctx.enter_context(nc.sbuf_tensor(f"{name}_{n}", s, d))

        def sem(n):
            return nc.alloc_semaphore(f"{name}_{n}")

        self.m, self.src, self.src_width, self.scale, self.dst, self.plus = m, src, src_width, scale, dst, plus
        self.w = sb("w", [P, 2, D])
        self.stage = sb("stage", [P, 2, D])
        self.turned = sb("turned", [P, 2, D])
        self.ps, self.pso = ps, pso
        self.staged, self.transposed, self.turned_ready, self.product_done, self.dst_done, self.biased = (
            sem("staged"), sem("transposed"), sem("turned_ready"), sem("product_done"), sem("dst_done"), sem("biased"))

    def start_vector(self, dve):
        dve.sem_inc(self.turned_ready, 2)

    def start_scalar(self, act):
        act.sem_inc(self.transposed, 2)
        act.sem_inc(self.dst_done, 2)

    def scalar(self, act, n0=0, scale0=0):
        with act.Fori(0, NT // 2) as i:
            for u in range(2):
                act.wait_ge(self.transposed, i * 2 + u + 1 + n0)
                act.activation(self.stage[:, u, :], self.src[:, cols(i * 2 * self.src_width + u * self.src_width, D)],
                               ACT.Copy, scale=self.scale[:, cols(i * 2 + u + scale0, 1)]).then_inc(self.staged, 1)

    def tensor(self, pe, n0=0):
        m, ps, pso = self.m, self.ps, self.pso
        with pe.Fori(0, NT // 2) as i:
            for u in range(2):
                pe.wait_ge(self.staged, i * 2 + u + 1 + n0)
                pe.wait_ge(self.turned_ready, i * 2 + u + 1 + n0)
                for c in range(2):
                    mm = pe.transpose(ps[u][:, c * P:(c + 1) * P], self.stage[:, u, c * P:(c + 1) * P], m.ident[:])
                mm.then_inc(self.transposed, 1)
            for u in range(2):
                pe.wait_ge(self.turned_ready, i * 2 + u + 3 + n0)
                pe.wait_ge(self.dst_done, i * 2 + u + 1 + n0)
                for c in range(2):
                    mm = pe.matmul(pso[u][:, 0:D], self.turned[:, u, c * P:(c + 1) * P], self.w[:, c, :],
                                   start=(c == 0), stop=(c == 1))
                mm.then_inc(self.product_done, 1)

    def vector(self, dve, n0=0, bias=None, share=None):
        with dve.Fori(0, NT // 2) as i:
            for u in range(2):
                dve.wait_ge(self.transposed, i * 2 + u + 3 + n0)
                dve.tensor_copy(self.turned[:, u, :], self.ps[u][:, 0:D]).then_inc(self.turned_ready, 1)
            for u in range(2):
                at = cols(i * 2 * D + u * D, D)
                if bias is not None:
                    dve.scalar_tensor_tensor(out=self.dst[:, at], in0=bias[:], scalar=share[:, cols(i * 2 + u, 1)],
                                             in1=self.dst[:, at], op0=ALU.mult, op1=ALU.add).then_inc(self.biased, 1)
                    dve.wait_ge(self.biased, i * 2 + u + 1)
                dve.wait_ge(self.product_done, i * 2 + u + 1 + n0)
                if self.plus:
                    dve.tensor_tensor(self.dst[:, at], self.dst[:, at], self.pso[u][:, 0:D], ALU.add).then_inc(self.dst_done, 1)
                else:
                    dve.tensor_copy(self.dst[:, at], self.pso[u][:, 0:D]).then_inc(self.dst_done, 1)


def project(nc, m, name, U, weight, bias, zoff):
    with ExitStack() as ctx:
        def sb(n, s, d=F32):
            return ctx.enter_context(nc.sbuf_tensor(f"{name}_{n}", s, d))

        def sem(n):
            return nc.alloc_semaphore(f"{name}_{n}")

        z = sb("z", [P, NT])
        rz = sb("rz", [P, NT])
        share = sb("share", [P, NT])
        b = sb("b", [P, D])
        ps = [ctx.enter_context(nc.psum_tensor(f"{name}_ps{k}", [P, W], F32)) for k in range(4)]
        weight_in, bias_in, z_steps = sem("weight_in"), sem("bias_in"), sem("z_steps")
        rp = RowProduct(ctx, nc, m, name, U, D + 2, rz, m.x, True, ps[0:2], ps[2:4])
        block = ctx.enter_context(nc.Block())
        Z = U[:].rearrange("p (t w) -> p t w", t=NT)[:, :, D]

        @block.sync
        def _(sp):
            sp.dma_start(rp.w[:], weight.rearrange("(c p) d -> p c d", p=P)).then_inc(weight_in, 16)
            sp.dma_start(b[:], bias.partition_broadcast(P)).then_inc(bias_in, 16)

        @block.vector
        def _(dve):
            chain = Chain(dve, z_steps)
            if zoff is not None:
                chain(dve.tensor_tensor(z[:], Z, zoff[:], ALU.add))
            else:
                chain(dve.tensor_copy(z[:], Z))
            chain(dve.reciprocal(rz[:], z[:]))
            chain(dve.tensor_tensor(share[:], Z, rz[:], ALU.mult))
            rp.start_vector(dve)
            dve.wait_ge(bias_in, 16)
            rp.vector(dve, bias=b, share=share)

        @block.scalar
        def _(act):
            act.wait_ge(z_steps, 3)
            rp.start_scalar(act)
            rp.scalar(act)

        @block.tensor
        def _(pe):
            pe.wait_ge(weight_in, 16)
            rp.tensor(pe)


def gat_vectors(nc, m, name, io, scol, dcol, d01):
    with ExitStack() as ctx:
        def sb(n, s, d=F32):
            return ctx.enter_context(nc.sbuf_tensor(f"{name}_{n}", s, d))

        def sem(n):
            return nc.alloc_semaphore(f"{name}_{n}")

        wT = sb("wT", [P, 2 * HEADS, D])
        a = sb("a", [P, HEADS, 2, 2])
        wa = sb("wa", [P, 2, 2 * HEADS])
        psw = ctx.enter_context(nc.psum_tensor(f"{name}_psw", [P, W], F32))
        psc = ctx.enter_context(nc.psum_tensor(f"{name}_psc", [P, W], F32))
        w_in, a_in, wa_done, wa_ready, cols_done, dve_steps = (
            sem("w_in"), sem("a_in"), sem("wa_done"), sem("wa_ready"), sem("cols_done"), sem("dve_steps"))
        block = ctx.enter_context(nc.Block())

        @block.sync
        def _(sp):
            sp.dma_start(wT[:], io.w["L1T"].rearrange("(k p) c -> p k c", p=P)).then_inc(w_in, 16)
            sp.dma_start(a[:], io.a).then_inc(a_in, 16)

        @block.tensor
        def _(pe):
            pe.wait_ge(w_in, 16)
            pe.wait_ge(a_in, 16)
            for c in range(2):
                for h in range(HEADS):
                    at = c * 2 * HEADS + h * 2
                    for k in range(2):
                        mm = pe.matmul(psw[:, at:at + 2], wT[:, h * 2 + k, c * P:(c + 1) * P], a[:, h, k, :],
                                       start=(k == 0), stop=(k == 1))
            mm.then_inc(wa_done, 1)
            pe.wait_ge(wa_ready, 1)
            for t in range(NT):
                for c in range(2):
                    mm = pe.matmul(psc[:, t * 8:t * 8 + 8], m.hT[:, c * NP + t * P:c * NP + (t + 1) * P], wa[:, c, :],
                                   start=(c == 0), stop=(c == 1))
            mm.then_inc(cols_done, 1)

        @block.vector
        def _(dve):
            for col in (scol, dcol):
                dve.memset(col[:, HEADS, :], 0.0).then_inc(dve_steps, 1)
            dve.wait_ge(wa_done, 1)
            dve.tensor_copy(wa[:].rearrange("p c k -> p (c k)"), psw[:, 0:4 * HEADS]).then_inc(wa_ready, 1)
            dve.wait_ge(cols_done, 1)
            both = psc[:, 0:NT * 8].rearrange("p (t h s) -> p s h t", h=HEADS, s=2)
            dve.tensor_copy(scol[:, 0:HEADS, :], both[:, 0]).then_inc(dve_steps, 1)
            dve.tensor_copy(dcol[:, 0:HEADS, :], both[:, 1]).then_inc(dve_steps, 1)
            dve.wait_ge(dve_steps, 4)
            dve.tensor_scalar(dcol[:, 0:HEADS, NT - 1], dcol[:, 0:HEADS, NT - 1], m.padneg[:, 0:1], None,
                              ALU.add).then_inc(dve_steps, 1)
            dve.wait_ge(dve_steps, 5)
            dve.tensor_scalar(d01[:], dcol[:], 0.01, None, ALU.mult).then_inc(dve_steps, 1)


def gat_tops(nc, name, adjT, dcol, top, edge):
    with ExitStack() as ctx:
        def sb(n, s, d=F32):
            return ctx.enter_context(nc.sbuf_tensor(f"{name}_{n}", s, d))

        def sem(n):
            return nc.alloc_semaphore(f"{name}_{n}")

        ring = sb("ring", [P, 5, 2, W])
        cand = sb("cand", [P, 3, 2, W], BF16)
        adj_in = [sem(f"adj_in{k}") for k in range(5)]
        cand_ready, edge_steps, top_steps, used = (
            sem("cand_ready"), sem("edge_steps"), sem("top_steps"), sem("used"))
        block = ctx.enter_context(nc.Block())
        dflat = dcol[:].rearrange("p h t -> p (h t)")

        @block.sync
        def _(sp):
            load_blocks(sp, adjT, ring, adj_in, used, 0)

        @block.scalar
        def _(act):
            def step(b, w, g, slot, n):
                s = pslot(slot)
                arrived(act, adj_in, b, g, slot)
                act.wait_ge(top_steps, n * 2 + 2)
                for u in range(2):
                    ins = act.activation(cand[:, s, u, 0:w], ring[:, slot, u, 0:w], ACT.Identity,
                                         bias=dflat[:, cols(g * 2 + u, 1)])
                ins.then_inc(cand_ready, 1)

            def one(b, w, next_w):
                step(b, w, 0, FIRST, b * NGRP)
                later_groups(act, step, b, w, b * NGRP)
            over_blocks(act, one)

        @block.vector
        def _(dve):
            dve.sem_inc(used, 5)
            dve.sem_inc(top_steps, 4)

            def step(b, w, g, slot, n, first=False):
                s = pslot(slot)
                at = cols(b * W, w)
                arrived(dve, adj_in, b, g, slot)
                if first:
                    dve.tensor_tensor(edge[:, at], ring[:, slot, 0, 0:w], ring[:, slot, 1, 0:w], ALU.max).then_inc(edge_steps, 1)
                    dve.wait_ge(cand_ready, n + 1)
                    dve.tensor_tensor(top[:, at], cand[:, s, 0, 0:w], cand[:, s, 1, 0:w], ALU.max).then_inc(top_steps, 2)
                    dve.sem_inc(edge_steps, 1)
                else:
                    dve.wait_ge(edge_steps, n * 2)
                    dve.tensor_tensor(edge[:, at], edge[:, at], ring[:, slot, 0, 0:w], ALU.max).then_inc(edge_steps, 1)
                    dve.wait_ge(cand_ready, n + 1)
                    dve.wait_ge(top_steps, n * 2 + 4)
                    dve.tensor_tensor(top[:, at], top[:, at], cand[:, s, 0, 0:w], ALU.max).then_inc(top_steps, 1)
                    dve.wait_ge(edge_steps, n * 2 + 1)
                    dve.tensor_tensor(edge[:, at], edge[:, at], ring[:, slot, 1, 0:w], ALU.max).then_inc(edge_steps, 1)
                    dve.wait_ge(top_steps, n * 2 + 5)
                    dve.tensor_tensor(top[:, at], top[:, at], cand[:, s, 1, 0:w], ALU.max).then_inc(top_steps, 1)
                dve.wait_ge(edge_steps, n * 2 + 2)
                dve.sem_inc(used, 1)

            def one(b, w, next_w):
                step(b, w, 0, FIRST, b * NGRP, True)
                later_groups(dve, step, b, w, b * NGRP)
            over_blocks(dve, one)


def gat_shifts(nc, m, name, scol, s01, dcol, top, edge, flat, A, B):
    with ExitStack() as ctx:
        def sb(n, s, d=F32):
            return ctx.enter_context(nc.sbuf_tensor(f"{name}_{n}", s, d))

        def sem(n):
            return nc.alloc_semaphore(f"{name}_{n}")

        peak = sb("peak", [P, HEADS])
        diag = sb("diag", [P, 2, W])
        topcol, edgecol, acol, bcol = (sb(n, [P, NT]) for n in ("topcol", "edgecol", "acol", "bcol"))
        dtop = sb("dtop", [P, HEADS])
        ps = [ctx.enter_context(nc.psum_tensor(f"{name}_ps{k}", [P, W], F32)) for k in range(8)]
        steps, diag_ready, rows_done, turned, reduced, stored = (
            sem("steps"), sem("diag_ready"), sem("rows_done"), sem("turned"), sem("reduced"), sem("stored"))
        block = ctx.enter_context(nc.Block())
        widths = [W] * NB + [TAIL]
        BLOCKS = NB + 1

        @block.tensor
        def _(pe):
            pe.wait_ge(diag_ready, 1)
            pe.matmul(ps[7][:], m.ones[:], diag[:, 0, :], start=True, stop=True).then_inc(rows_done, 1)
            for b, w in enumerate(widths):
                if b >= 2:
                    pe.wait_ge(reduced, 2 * b - 2)
                for q in range(w // P):
                    at = b * W + q * P
                    pe.matmul(ps[b % 2][:, q * P:(q + 1) * P], top[:, at:at + P], m.identb[:], start=True, stop=True)
                    mm = pe.matmul(ps[2 + b % 2][:, q * P:(q + 1) * P], edge[:, at:at + P], m.identb[:], start=True, stop=True)
                mm.then_inc(turned, 1)
            for b, w in enumerate(widths):
                pe.wait_ge(diag_ready, 2 + b)
                if b >= 2:
                    pe.wait_ge(stored, 2 * b - 2)
                pe.matmul(ps[4 * (b % 2)][:, 0:w], m.ones[:], diag[:, 0, 0:w], start=True, stop=True)
                pe.matmul(ps[4 * (b % 2) + 1][:, 0:w], m.ones[:], diag[:, 1, 0:w], start=True, stop=True).then_inc(rows_done, 1)

        @block.scalar
        def _(act):
            for b, w in enumerate(widths):
                act.wait_ge(rows_done, 2 + b)
                for k, row in enumerate((A, B)):
                    act.copy(row[:, b * W:b * W + w], ps[4 * (b % 2) + k][:, 0:w]).then_inc(stored, 1)

        @block.vector
        def _(dve):
            chain = Chain(dve, steps)
            chain(dve.tensor_reduce(peak[:], dcol[:, 0:HEADS, :], AX.X, ALU.max))
            for h in range(HEADS):
                ins = dve.tensor_scalar(diag[:, 0, h * P:(h + 1) * P], m.ident[:], peak[:, h:h + 1], None, ALU.mult)
            ins.then_inc(diag_ready, 1)
            for row in (A, B):
                dve.memset(row[:, NP:NQ], 0.0)
            for b, w in enumerate(widths):
                dve.wait_ge(turned, b + 1)
                for k, col in enumerate((topcol, edgecol)):
                    dve.tensor_reduce(col[:, b * 4:b * 4 + w // P],
                                      ps[2 * k + b % 2][:, 0:w].rearrange("p (q j) -> p q j", j=P),
                                      AX.X, ALU.max).then_inc(reduced, 1)
            dve.wait_ge(rows_done, 1)
            chain(dve.tensor_reduce(dtop[:], ps[7][:].rearrange("p (h j) -> p h j", j=P), AX.X, ALU.max))
            chain(dve.tensor_scalar(dtop[:], dtop[:], 0.01, None, ALU.mult))
            chain(dve.tensor_scalar(s01[:], scol[:], 0.01, None, ALU.mult))
            chain(dve.memset(flat[:, HEADS, :], 0.0))
            dve.wait_ge(reduced, 2 * BLOCKS)
            for h in range(HEADS):
                ins = dve.scalar_tensor_tensor(out=flat[:, h, :], in0=s01[:, h, :], scalar=dtop[:, h:h + 1],
                                               in1=edgecol[:], op0=ALU.add, op1=ALU.add)
            chain(ins)
            chain(dve.tensor_tensor(topcol[:], topcol[:], scol[:, 0, :], ALU.add))
            chain(dve.tensor_tensor(topcol[:], topcol[:], flat[:, 0, :], ALU.max))
            chain(dve.tensor_tensor(acol[:], scol[:, 0, :], topcol[:], ALU.subtract))
            chain(dve.tensor_tensor(bcol[:], s01[:, 0, :], topcol[:], ALU.subtract))
            for b, w in enumerate(widths):
                dve.wait_ge(rows_done, 1 + b)
                for k, col in enumerate((acol, bcol)):
                    for q in range(w // P):
                        ins = dve.tensor_scalar(diag[:, k, q * P:(q + 1) * P], m.ident[:],
                                                col[:, b * 4 + q:b * 4 + q + 1], None, ALU.mult)
                ins.then_inc(diag_ready, 1)


def gat(nc, m, name, io, scol, s01, dcol, d01, flat, top, A, B, haug):
    width = D + 2
    with ExitStack() as ctx:
        def sb(n, s, d=F32):
            return ctx.enter_context(nc.sbuf_tensor(f"{name}_{n}", s, d))

        def sem(n):
            return nc.alloc_semaphore(f"{name}_{n}")

        U = sb("U", [P, NT * width])
        weights = sb("weights", [P, (HEADS + 1) * 2 * D])
        ring = sb("ring", [P, 5, 2, W])
        slope = sb("slope", [P, 3, 2, W])
        cand = sb("cand", [P, 3, W], BF16)
        t = sb("t", [P, 3, 2, W])
        p32 = sb("p32", [P, 3, 2, W])
        stage = sb("stage", [P, 4, D])
        turned = sb("turned", [P, 4, D])
        diag = sb("diag", [P, 2, W])
        topcol, acol, bcol, rz = (sb(n, [P, 4]) for n in ("topcol", "acol", "bcol", "rz"))
        own_d, own_next, own_d01, own_candidate = (sb(n, [P, NT]) for n in ("own_d", "own_next", "own_d01", "own_candidate"))
        acc = [ctx.enter_context(nc.psum_tensor(f"{name}_acc{k}", [P, W], F32)) for k in range(4)]
        psT = [ctx.enter_context(nc.psum_tensor(f"{name}_psT{k}", [P, W], F32)) for k in range(2)]
        psO = [ctx.enter_context(nc.psum_tensor(f"{name}_psO{k}", [P, W], F32)) for k in range(2)]
        adj_in = [sem(f"adj_in{k}") for k in range(5)]
        slope_ready, cand_ready, maxed, added, half_top, released, exp_ready, summed = (
            sem("slope_ready"), sem("cand_ready"), sem("maxed"), sem("added"), sem("half_top"), sem("released"),
            sem("exp_ready"), sem("summed"))
        weights_in = [sem(f"weights_in{h}") for h in range(HEADS)]
        weights_cleared, four_ready = sem("weights_cleared"), sem("four_ready")
        stored, rz_ready, staged, transposed, turned_ready, product_done, x_done = (
            sem("stored"), sem("rz_ready"), sem("staged"), sem("transposed"), sem("turned_ready"),
            sem("product_done"), sem("x_done"))
        tops_turned, col_steps, diag_ready, rows_done, ab_ready = (
            sem("tops_turned"), sem("col_steps"), sem("diag_ready"), sem("rows_done"), sem("ab_ready"))
        vector_cols, scalar_cols, waited = sem("vector_cols"), sem("scalar_cols"), sem("waited")
        block = ctx.enter_context(nc.Block())
        BLOCKS = NB + 1
        GROUPS = BLOCKS * NGRP
        U3 = U[:].rearrange("p (t w) -> p t w", t=NT)
        flats = {k: c[:].rearrange("p h t -> p (h t)")
                 for k, c in (("s", scol), ("s01", s01), ("d", dcol), ("d01", d01), ("flat", flat))}
        COLS = 5

        class Before:

            def __init__(self, h, b, start):
                self.number = h * BLOCKS if start else h * BLOCKS + b
                self.tiles = h * NT if start else h * NT + b * 4 - 2
                self.tile = NT - 2 if start else b * 4 - 4
                self.count = 2 if start else 4
                self.column = NP - TAIL if start else b * W - W
                self.width = TAIL if start else W
                self.next_head = h if start else h + 1
                self.groups = h * GROUPS if start else h * GROUPS + b * NGRP

        def over_heads(eng, one, start=None):
            with eng.Fori(0, HEADS) as h:
                if start:
                    start(h)
                one(h, 0, W, Before(h, 0, True))
                with eng.Fori(1, NB) as b:
                    one(h, b, W, Before(h, b, False))
                one(h, NB, TAIL, Before(h, NB, False))

        last = Before(HEADS, 0, True)

        def slot_of(g):
            return FIRST if g == 0 else (g - 1) % 4

        @block.sync
        def _(sp):
            for h in range(HEADS):
                sp.dma_start(weights[:, (h + 1) * 2 * D:(h + 2) * 2 * D].rearrange("p (c d) -> p c d", c=2),
                             io.w["L1"][:, h * D:(h + 1) * D].rearrange("(c p) d -> p c d", p=P)).then_inc(weights_in[h], 16)
            with sp.Fori(0, HEADS) as h:
                load_blocks(sp, io.adjT, ring, adj_in, released, h * GROUPS)

        @block.tensor
        def _(pe):
            def sums(h, b, w, g, before):
                slot = slot_of(g)
                pe.wait_ge(exp_ready, before.groups + g + 3)
                for u in range(2):
                    row = slice((g * 2 + u) * width, (g * 2 + u) * width + width - 1)
                    for q in range(w // P):
                        if g == 0 and u == 0 and q < before.count:
                            pe.wait_ge(stored, before.tiles + q + 1)
                        mm = pe.matmul(acc[q][:, 0:width - 1], p32[:, pslot(slot), u, q * P:(q + 1) * P], haug[:, row],
                                       start=(g == 0 and u == 0), stop=(g == NGRP - 1 and u == 1))
                mm.then_inc(summed, 1)

            def turn_tops(before):
                pe.wait_ge(turned_ready, before.tiles + 1)
                pe.wait_ge(released, before.groups + 5)
                for q in range(before.count):
                    mm = pe.matmul(psT[0][:, q * P:(q + 1) * P], top[:, cols(before.column + q * P, P)], m.identb[:],
                                   start=True, stop=True)
                mm.then_inc(tops_turned, 1)

            def rows(before):
                pe.wait_ge(diag_ready, before.number + 1)
                for k in range(2):
                    mm = pe.matmul(psT[k][:, 0:before.width], m.ones[:], diag[:, k, 0:before.width], start=True, stop=True)
                mm.then_inc(rows_done, 1)

            def turn(before, q):
                pe.wait_ge(staged, before.tiles + q + 1)
                for c in range(2):
                    mm = pe.transpose(psT[q % 2][:, c * P:(c + 1) * P], stage[:, q, c * P:(c + 1) * P], m.ident[:])
                mm.then_inc(transposed, 1)

            def product(before, q):
                pe.wait_ge(turned_ready, before.tiles + q + 2)
                for c in range(2):
                    mm = pe.matmul(psO[q % 2][:, 0:D], turned[:, q, c * P:(c + 1) * P],
                                   weights[:, cols((before.next_head * 2 + c) * D, D)], start=(c == 0), stop=(c == 1))
                mm.then_inc(product_done, 1)

            def first_pair_turned(before, rows_free):
                if rows_free:
                    pe.wait_ge(ab_ready, before.number * 2 + 2)
                for q in range(2):
                    turn(before, q)

            def first_pair_products(before):
                pe.wait_ge(x_done, before.tiles + 1)
                for q in range(2):
                    product(before, q)

            def one(h, b, w, before):
                turn_tops(before)
                for g in range(NGRP):
                    sums(h, b, w, g, before)
                    if g == 1:
                        rows(before)
                    if g == 5:
                        first_pair_turned(before, True)
                    if g == 7:
                        first_pair_products(before)
                        if before.count > 2:
                            pe.wait_ge(turned_ready, before.tiles + 3)
                            for q in range(2, 4):
                                turn(before, q)
                    if g == 9 and before.count > 2:
                        pe.wait_ge(x_done, before.tiles + 3)
                        for q in range(2, 4):
                            product(before, q)

            for h in range(HEADS):
                pe.wait_ge(weights_in[h], 16)
            pe.wait_ge(weights_cleared, 1)
            pe.wait_ge(four_ready, 1)
            for q in range(2):
                mm = pe.matmul(acc[q][:, 0:width - 1], m.ones[:], haug[:, 0:width - 1], start=True, stop=True)
            mm.then_inc(summed, 1)
            over_heads(pe, one)
            first_pair_turned(last, False)
            first_pair_products(last)

        @block.vector
        def _(dve):
            dve.memset(weights[:, 0:2 * D], 0.0).then_inc(weights_cleared, 1)
            dve.memset(haug[:].rearrange("p (t w) -> p t w", t=NT)[:, :, D], float(HEADS)).then_inc(four_ready, 1)
            dve.sem_inc(released, 5)
            dve.sem_inc(maxed, 2)
            dve.sem_inc(turned_ready, 1)
            dve.sem_inc(x_done, 1)
            dve.sem_inc(tops_turned, 1)

            def step(h, b, w, g, before):
                slot = slot_of(g)
                s = pslot(slot)
                n = before.groups + g
                at = cols(b * W, w)
                dve.wait_ge(slope_ready, n + 1)
                dve.wait_ge(exp_ready, n + 1)
                for u in range(2):
                    ins = dve.scalar_tensor_tensor(out=t[:, s, u, 0:w], in0=A[:, at],
                                                   scalar=own_d[:, g * 2 + u:g * 2 + u + 1], in1=slope[:, s, u, 0:w],
                                                   op0=ALU.add, op1=ALU.max)
                ins.then_inc(maxed, 1)
                arrived(dve, adj_in, b, g, slot, h * BLOCKS)
                dve.wait_ge(maxed, n + 3)
                dve.tensor_tensor(t[:, s, :, 0:w], t[:, s, :, 0:w], ring[:, slot, :, 0:w], ALU.add).then_inc(added, 1)
                d_next = own_next[:, g * 2 + 1:g * 2 + 2]
                if g == 0:
                    dve.wait_ge(tops_turned, before.number + 1)
                    dve.tensor_scalar(top[:, at], ring[:, slot, 1, 0:w], d_next, None, ALU.add).then_inc(half_top, 1)
                else:
                    dve.wait_ge(released, n + 5)
                    dve.scalar_tensor_tensor(out=top[:, at], in0=ring[:, slot, 1, 0:w], scalar=d_next, in1=top[:, at],
                                             op0=ALU.add, op1=ALU.max).then_inc(half_top, 1)
                dve.wait_ge(cand_ready, n + 1)
                dve.wait_ge(half_top, n + 1)
                dve.tensor_tensor(top[:, at], top[:, at], cand[:, s, 0:w], ALU.max).then_inc(released, 1)

            def columns(before):
                dve.wait_ge(tops_turned, before.number + 2)
                n = before.number * COLS
                c = before.count
                at = cols(before.next_head * NT + before.tile, c)

                def done(ins, k):
                    ins.then_inc(col_steps, 1)
                    dve.wait_ge(col_steps, n + k)
                done(dve.tensor_reduce(topcol[:, 0:c], psT[0][:, 0:c * P].rearrange("p (q j) -> p q j", j=P), AX.X, ALU.max), 1)
                done(dve.tensor_tensor(topcol[:, 0:c], topcol[:, 0:c], flats["s"][:, at], ALU.add), 2)
                done(dve.tensor_tensor(topcol[:, 0:c], topcol[:, 0:c], flats["flat"][:, at], ALU.max), 3)
                dve.tensor_tensor(acol[:, 0:c], flats["s"][:, at], topcol[:, 0:c], ALU.subtract).then_inc(col_steps, 1)
                done(dve.tensor_tensor(bcol[:, 0:c], flats["s01"][:, at], topcol[:, 0:c], ALU.subtract), 5)
                for k, col in enumerate((acol, bcol)):
                    for q in range(c):
                        ins = dve.tensor_scalar(diag[:, k, q * P:(q + 1) * P], m.ident[:], col[:, q:q + 1], None, ALU.mult)
                ins.then_inc(diag_ready, 1)

            def shares(before):
                wait_apart(dve, stored, before.tiles + before.count, waited)
                dve.reciprocal(rz[:, 0:before.count], U3[:, cols(before.tile, before.count), D]).then_inc(rz_ready, 1)

            def keep_turned(before, q):
                dve.wait_ge(transposed, before.tiles + q + 1)
                dve.tensor_copy(turned[:, q, :], psT[q % 2][:, 0:D]).then_inc(turned_ready, 1)

            def into_x(before, q):
                dve.wait_ge(product_done, before.tiles + q + 1)
                at = cols((before.tile + q) * D, D)
                dve.tensor_tensor(m.x[:, at], m.x[:, at], psO[q % 2][:, 0:D], ALU.add).then_inc(x_done, 1)

            def one(h, b, w, before):
                for g in range(NGRP):
                    step(h, b, w, g, before)
                    if g == 2:
                        columns(before)
                    if g == 3:
                        shares(before)
                    if g == 8:
                        for q in range(2):
                            keep_turned(before, q)
                    if g == 10:
                        if before.count > 2:
                            for q in range(2, 4):
                                keep_turned(before, q)
                        for q in range(2):
                            into_x(before, q)
                    if g == 12 and before.count > 2:
                        for q in range(2, 4):
                            into_x(before, q)

            def start(h):
                wait_apart(dve, released, h * GROUPS + 5, waited)
                dve.tensor_copy(own_d[:], flats["d"][:, cols(h * NT, NT)]).then_inc(vector_cols, 1)
                dve.tensor_copy(own_next[:], flats["d"][:, cols(h * NT + NT, NT)]).then_inc(vector_cols, 1)
                wait_apart(dve, vector_cols, h * 2 + 2, waited)

            over_heads(dve, one, start)
            shares(last)
            for q in range(2):
                keep_turned(last, q)
            for q in range(2):
                into_x(last, q)

        @block.scalar
        def _(act):
            act.preload_act_table(ACT.Exp)
            act.sem_inc(exp_ready, 2)
            act.sem_inc(summed, 1)

            def slopes(h, b, w, g, n):
                s = pslot(slot_of(g))
                wait_apart(act, maxed, n + 1, waited)
                for u in range(2):
                    ins = act.activation(slope[:, s, u, 0:w], B[:, cols(b * W, w)], ACT.Identity,
                                         bias=flats["d01"][:, cols(h * NT + g * 2 + u, 1)] if g == 0 else
                                         own_d01[:, g * 2 + u:g * 2 + u + 1])
                ins.then_inc(slope_ready, 1)

            def candidates(h, b, w, g, n):
                slot = slot_of(g)
                arrived(act, adj_in, b, g, slot, h * BLOCKS)
                act.wait_ge(released, n + 4)
                act.activation(cand[:, pslot(slot), 0:w], ring[:, slot, 0, 0:w], ACT.Identity,
                               bias=own_candidate[:, g * 2:g * 2 + 1]).then_inc(cand_ready, 1)

            def exps(w, g, n):
                s = pslot(slot_of(g))
                act.wait_ge(added, n + 1)
                act.wait_ge(summed, n + 1)
                act.activation(p32[:, s, :, 0:w], t[:, s, :, 0:w], ACT.Exp).then_inc(exp_ready, 1)

            def keep_sums(before):
                wait_apart(act, summed, before.groups + 2, waited)
                for q in range(before.count):
                    act.copy(U3[:, cols(before.tile + q, 1), 0:width - 1].rearrange("p o w -> p (o w)"),
                             acc[q][:, 0:width - 1]).then_inc(stored, 1)

            def stages(before):
                wait_apart(act, rz_ready, before.number + 1, waited)
                for q in range(before.count):
                    act.activation(stage[:, q, :], U3[:, cols(before.tile + q, 1), 0:D].rearrange("p o w -> p (o w)"),
                                   ACT.Copy, scale=rz[:, q:q + 1]).then_inc(staged, 1)

            def keep_rows(before):
                wait_apart(act, rows_done, before.number + 1, waited)
                for k, row in enumerate((A, B)):
                    act.copy(row[:, cols(before.column, before.width)], psT[k][:, 0:before.width]).then_inc(ab_ready, 1)

            def one(h, b, w, before):
                n = before.groups
                candidates(h, b, w, 0, n)
                for g in range(NGRP):
                    if g + 1 < NGRP:
                        slopes(h, b, w, g + 1, n + g + 1)
                        candidates(h, b, w, g + 1, n + g + 1)
                    elif w == W:
                        slopes(h, b + 1, W, 0, n + NGRP)
                    else:
                        slopes(h + 1, 0, W, 0, n + NGRP)
                    exps(w, g, n + g)
                    if g == 1:
                        keep_sums(before)
                    if g == 4:
                        stages(before)
                    if g == 5:
                        keep_rows(before)

            def start(h):
                wait_apart(act, slope_ready, h * GROUPS + 1, waited)
                act.copy(own_d01[:], flats["d01"][:, cols(h * NT, NT)]).then_inc(scalar_cols, 1)
                act.copy(own_candidate[:], flats["d"][:, cols(h * NT + NT, NT)]).then_inc(scalar_cols, 1)
                wait_apart(act, scalar_cols, h * 2 + 2, waited)

            slopes(0, 0, W, 0, 0)
            over_heads(act, one, start)
            keep_sums(last)
            stages(last)


TOP = float(np.float32(1.0 - 1e-7))
EPS3 = 1e-10


def artanh_before(chain, dve, y, v, w):
    chain(dve.tensor_scalar(y, y, TOP, -TOP, ALU.min, ALU.max))
    chain(dve.tensor_scalar(w, y, -1.0, 1.0, ALU.mult, ALU.add))
    chain(dve.reciprocal(w, w))
    chain(dve.tensor_scalar(v, y, 1.0, None, ALU.add))
    chain(dve.tensor_tensor(v, v, w, ALU.mult))


def artanh_after(chain, dve, y, v, w, z):
    chain(dve.tensor_tensor(w, y, y, ALU.mult))
    chain(dve.tensor_scalar(z, w, 1.0 / 11, 1.0 / 9, ALU.mult, ALU.add))
    for k in (7, 5, 3, 1):
        chain(dve.tensor_tensor(z, z, w, ALU.mult))
        chain(dve.tensor_scalar(z, z, 1.0 / k, None, ALU.add))
    chain(dve.tensor_tensor(z, z, y, ALU.mult))
    chain(dve.scalar_tensor_tensor(out=v, in0=v, scalar=0.5, in1=z, op0=ALU.mult, op1=ALU.subtract))
    chain(dve.scalar_tensor_tensor(out=v, in0=y, scalar=0.125, in1=v, op0=ALU.is_ge, op1=ALU.mult))
    chain(dve.tensor_tensor(v, v, z, ALU.add))


def row_product(nc, m, name, src, src_width, ones, dst, weight):
    with ExitStack() as ctx:
        ps = [ctx.enter_context(nc.psum_tensor(f"{name}_ps{k}", [P, W], F32)) for k in range(4)]
        weight_in = nc.alloc_semaphore(f"{name}_weight_in")
        rp = RowProduct(ctx, nc, m, name, src, src_width, ones, dst, False, ps[0:2], ps[2:4])
        block = ctx.enter_context(nc.Block())

        @block.sync
        def _(sp):
            sp.dma_start(rp.w[:], weight.rearrange("(c p) d -> p c d", p=P)).then_inc(weight_in, 16)

        @block.vector
        def _(dve):
            rp.start_vector(dve)
            rp.vector(dve)

        @block.scalar
        def _(act):
            rp.start_scalar(act)
            rp.scalar(act)

        @block.tensor
        def _(pe):
            pe.wait_ge(weight_in, 16)
            rp.tensor(pe)


def square_sums(chain, dve, src, big, out):
    chain(dve.tensor_tensor(big, src, src, ALU.mult))
    chain(dve.tensor_reduce(out, big, AX.X, ALU.add))


def hyper_points(nc, name, haug, mx, gaug):
    with ExitStack() as ctx:
        def col(n):
            return ctx.enter_context(nc.sbuf_tensor(f"{name}_{n}", [P, NT], F32))[:]

        def sem(n):
            return nc.alloc_semaphore(f"{name}_{n}")

        hh, mm, xn, mn, live, v, w, z, f = (col(n) for n in ("hh", "mm", "xn", "mn", "live", "v", "w", "z", "f"))
        steps, sums_ready, roots_ready, log_in, log_out, tanh_in, tanh_out = (
            sem("steps"), sem("sums_ready"), sem("roots_ready"), sem("log_in"), sem("log_out"), sem("tanh_in"), sem("tanh_out"))
        h3 = haug[:].rearrange("p (t w) -> p t w", t=NT)
        g3 = gaug[:].rearrange("p (t w) -> p t w", t=NT)
        mx3 = mx[:].rearrange("p (t d) -> p t d", t=NT)
        block = ctx.enter_context(nc.Block())

        @block.vector
        def _(dve):
            chain = Chain(dve, steps)
            square_sums(chain, dve, h3[:, :, 0:D], g3[:, :, 0:D], hh)
            square_sums(chain, dve, mx3, g3[:, :, 0:D], mm)
            chain(dve.tensor_scalar(live, mm, EPS3 * EPS3, None, ALU.is_gt))
            chain(dve.tensor_scalar(hh, hh, EPS3 * EPS3, None, ALU.max))
            dve.tensor_scalar(mm, mm, EPS3 * EPS3, None, ALU.max).then_inc(sums_ready, 1)
            dve.wait_ge(roots_ready, 2)
            chain(dve.reciprocal(f, xn))
            chain(dve.tensor_tensor(f, f, mn, ALU.mult))
            artanh_before(chain, dve, xn, v, w)
            dve.sem_inc(log_in, 1)
            dve.wait_ge(log_out, 1)
            artanh_after(chain, dve, xn, v, w, z)
            chain(dve.tensor_tensor(v, v, f, ALU.mult))
            dve.sem_inc(tanh_in, 1)
            dve.wait_ge(tanh_out, 1)
            chain(dve.tensor_tensor(v, v, live, ALU.mult))
            chain(dve.tensor_tensor(w, v, v, ALU.mult))
            chain(dve.tensor_scalar(w, w, -1.0, 1.0, ALU.mult, ALU.add))
            chain(dve.reciprocal(w, w))
            chain(dve.tensor_scalar(w, w, 2.0, 1e-15, ALU.mult, ALU.max))
            chain(dve.tensor_scalar(g3[:, :, D], w, -1.0, None, ALU.add))
            chain(dve.memset(g3[:, :, D + 1], 1.0))
            chain(dve.reciprocal(f, mn))
            chain(dve.tensor_tensor(f, f, v, ALU.mult))
            chain(dve.tensor_tensor(f, f, w, ALU.mult))
            chain(dve.tensor_tensor(g3[:, :, 0:D], mx3, f.rearrange("p (t o) -> p t o", o=1).to_broadcast([P, NT, D]), ALU.mult))

        @block.scalar
        def _(act):
            act.wait_ge(sums_ready, 1)
            act.activation(xn, hh, ACT.Sqrt).then_inc(roots_ready, 1)
            act.activation(mn, mm, ACT.Sqrt).then_inc(roots_ready, 1)
            act.wait_ge(log_in, 1)
            act.activation(v, v, ACT.Ln).then_inc(log_out, 1)
            act.wait_ge(tanh_in, 1)
            act.activation(v, v, ACT.Tanh).then_inc(tanh_out, 1)


def mean_sums(nc, name, adjT, gaug, U):
    width = D + 2
    with ExitStack() as ctx:
        def sem(n):
            return nc.alloc_semaphore(f"{name}_{n}")

        ring = ctx.enter_context(nc.sbuf_tensor(f"{name}_ring", [P, 5, 2, W], F32))
        acc = [ctx.enter_context(nc.psum_tensor(f"{name}_acc{k}", [P, W], F32)) for k in range(8)]
        adj_in = [sem(f"adj_in{k}") for k in range(5)]
        summed, stored = sem("summed"), sem("stored")
        block = ctx.enter_context(nc.Block())

        @block.sync
        def _(sp):
            load_blocks(sp, adjT, ring, adj_in, summed, 0)

        @block.tensor
        def _(pe):
            def sums(b, w, g, slot, first, last):
                arrived(pe, adj_in, b, g, slot)
                for u in range(2):
                    for q in range(w // P):
                        if first and u == 0:
                            pe.wait_ge(stored, b * 4 + q + 1)
                        mm = pe.matmul(acc[q][:, 0:width], ring[:, slot, u, q * P:(q + 1) * P],
                                       gaug[:, cols(g * 2 * width + u * width, width)],
                                       start=(first and u == 0), stop=(last and u == 1))
                mm.then_inc(summed, 1)

            def one(b, w, next_w):
                sums(b, w, 0, FIRST, True, False)
                later = NGRP // 4
                with pe.Fori(0, later - 1) as i:
                    for u in range(4):
                        sums(b, w, i * 4 + u + 1, u, False, False)
                for u in range(4):
                    g = (later - 1) * 4 + u + 1
                    sums(b, w, g, u, False, g == NGRP - 1)
            over_blocks(pe, one)

        @block.vector
        def _(dve):
            dve.sem_inc(summed, 5)
            dve.sem_inc(stored, 4)

            def one(b, w, next_w):
                dve.wait_ge(summed, b * NGRP + NGRP + 5)
                for q in range(w // P):
                    dve.tensor_copy(U[:, cols(b * 4 * width + q * width, width)], acc[q][:, 0:width]).then_inc(stored, 1)
            over_blocks(dve, one)


def hyper_mean(nc, m, name, U, big):
    with ExitStack() as ctx:
        def col(n):
            return ctx.enter_context(nc.sbuf_tensor(f"{name}_{n}", [P, NT], F32))[:]

        def sem(n):
            return nc.alloc_semaphore(f"{name}_{n}")

        ss, d, k, q, y, v, w, z = (col(n) for n in ("ss", "d", "k", "q", "y", "v", "w", "z"))
        steps, root_in, root_out, log_in, log_out, tanh_in, tanh_out = (
            sem("steps"), sem("root_in"), sem("root_out"), sem("log_in"), sem("log_out"), sem("tanh_in"), sem("tanh_out"))
        U3 = U[:].rearrange("p (t w) -> p t w", t=NT)
        big3 = big[:].rearrange("p (t d) -> p t d", t=NT)
        x3 = m.x[:].rearrange("p (t d) -> p t d", t=NT)
        nom, den, alpha = U3[:, :, 0:D], U3[:, :, D], U3[:, :, D + 1]

        def wide(c):
            return c.rearrange("p (t o) -> p t o", o=1).to_broadcast([P, NT, D])
        block = ctx.enter_context(nc.Block())

        @block.vector
        def _(dve):
            chain = Chain(dve, steps)

            def norm_of(factor, squares, number):
                if factor is not None:
                    chain(dve.tensor_tensor(y, factor, factor, ALU.mult))
                    chain(dve.tensor_tensor(y, y, squares, ALU.mult))
                    chain(dve.tensor_scalar(y, y, EPS3 * EPS3, None, ALU.max))
                else:
                    chain(dve.tensor_scalar(y, squares, EPS3 * EPS3, None, ALU.max))
                dve.sem_inc(root_in, 1)
                dve.wait_ge(root_out, number)

            square_sums(chain, dve, nom, big3, ss)
            chain(dve.tensor_scalar(d, den, 0.0, 2.0, ALU.is_ge, ALU.mult))
            chain(dve.tensor_scalar(d, d, -1.0, None, ALU.add))
            chain(dve.tensor_tensor(v, d, den, ALU.mult))
            chain(dve.tensor_scalar(v, v, EPS3, None, ALU.max))
            chain(dve.tensor_tensor(d, d, v, ALU.mult))
            chain(dve.reciprocal(d, d))
            chain(dve.tensor_tensor(y, d, d, ALU.mult))
            chain(dve.tensor_tensor(y, y, ss, ALU.mult))
            chain(dve.tensor_scalar(y, y, -1.0, 1.0, ALU.mult, ALU.add))
            chain(dve.tensor_scalar(y, y, EPS3, None, ALU.max))
            dve.sem_inc(root_in, 1)
            dve.wait_ge(root_out, 1)
            chain(dve.tensor_scalar(y, y, 1.0, None, ALU.add))
            chain(dve.reciprocal(y, y))
            chain(dve.tensor_tensor(k, d, y, ALU.mult))
            norm_of(k, ss, 2)
            chain(dve.reciprocal(q, y))
            chain(dve.tensor_tensor(k, k, q, ALU.mult))
            artanh_before(chain, dve, y, v, w)
            dve.sem_inc(log_in, 1)
            dve.wait_ge(log_out, 1)
            artanh_after(chain, dve, y, v, w, z)
            chain(dve.tensor_tensor(v, v, alpha, ALU.mult))
            dve.sem_inc(tanh_in, 1)
            dve.wait_ge(tanh_out, 1)
            chain(dve.tensor_tensor(k, k, v, ALU.mult))
            norm_of(k, ss, 3)
            chain(dve.reciprocal(q, y))
            chain(dve.tensor_tensor(k, k, q, ALU.mult))
            artanh_before(chain, dve, y, v, w)
            dve.sem_inc(log_in, 1)
            dve.wait_ge(log_out, 2)
            artanh_after(chain, dve, y, v, w, z)
            chain(dve.tensor_tensor(k, k, v, ALU.mult))
            chain(dve.tensor_tensor(nom, nom, wide(k), ALU.mult))
            chain(dve.tensor_scalar(nom, nom, 0.0, None, ALU.max))
            square_sums(chain, dve, nom, big3, ss)
            norm_of(None, ss, 4)
            chain(dve.reciprocal(q, y))
            chain(dve.tensor_copy(v, y))
            dve.sem_inc(tanh_in, 1)
            dve.wait_ge(tanh_out, 2)
            chain(dve.tensor_tensor(q, q, v, ALU.mult))
            chain(dve.tensor_tensor(nom, nom, wide(q), ALU.mult))
            chain(dve.tensor_tensor(x3, x3, nom, ALU.add))

        @block.scalar
        def _(act):
            def root(n):
                act.wait_ge(root_in, n)
                act.activation(y, y, ACT.Sqrt).then_inc(root_out, 1)

            def log(n):
                act.wait_ge(log_in, n)
                act.activation(v, v, ACT.Ln).then_inc(log_out, 1)

            def tanh(n):
                act.wait_ge(tanh_in, n)
                act.activation(v, v, ACT.Tanh).then_inc(tanh_out, 1)

            root(1)
            root(2)
            log(1)
            tanh(1)
            root(3)
            log(2)
            root(4)
            tanh(2)


def store(nc, m, out):
    body_out, last_out = nc.alloc_semaphore("body_out"), nc.alloc_semaphore("last_out")
    with nc.Block() as block:
        @block.sync
        def _(sp):
            xt = m.x[:].rearrange("p (t d) -> p t d", t=NT)
            sp.dma_start(out[0:(NT - 1) * P, :].rearrange("(t p) d -> p t d", p=P), xt[:, 0:NT - 1, :]).then_inc(body_out, 16)
            sp.dma_start(out[(NT - 1) * P:N, :], xt[0:N - (NT - 1) * P, NT - 1, :]).then_inc(last_out, 16)
            sp.wait_ge(body_out, 16)
            sp.wait_ge(last_out, 16)


class Io:
    pass


def attention_layer(nc, m, io, name, graphs):
    with nc.cleanup_on_exit(), ExitStack() as layer:
        def sb(n, s, d=F32):
            return layer.enter_context(nc.sbuf_tensor(f"{name}_{n}", s, d))

        hh = sb("hh", [P, NT * (D + 2)], F16)
        hl = sb("hl", [P, NT * (D + 2)], F16)
        negm = sb("negm", [P, NT])
        zoff = sb("zoff", [P, NT]) if graphs else None
        q_parts = (sb("qh", [P, 2 * NQ], F16), sb("ql", [P, 2 * NQ], F16))
        k_parts = (sb("kh", [P, 2 * NP], F16), sb("kl", [P, 2 * NP], F16))
        augI = sb("augI", [P, NQ], BF16)
        augJ = sb("augJ", [P, NP], BF16)
        with nc.sbuf_tensor(f"{name}_hT", [P, 2 * NP], F32) as m.hT:
            norm(nc, m, f"{name}_norm", True, hh, hl)
            queries_keys(nc, m, f"{name}_qk", io.w[name + "q"], io.w[name + "k"], io.b[name + "q"],
                         io.b[name + "k"], q_parts, k_parts)
        with nc.sbuf_tensor(f"{name}_notJ", [P, NP], BF16) as notJ:
            if graphs:
                aug_graphs(nc, name, io.ptr, augI, augJ, notJ, q_parts)
            else:
                aug_plain(nc, name, augI, augJ, q_parts)
            row_max(nc, f"{name}_max", io.adj, q_parts[0], k_parts[0], graphs, augI, augJ, notJ, negm, zoff)
        shift_rows(nc, m, f"{name}_shift", negm, augI)
        U = sb("U", [P, NT * (D + 2)])
        attend(nc, f"{name}_att", io.adjT, q_parts, k_parts, augI, augJ, hh, hl, U)
        project(nc, m, f"{name}_out", U, io.w[name + "v"], io.b[name + "v"], zoff)


def gat_layer(nc, m, io):
    with nc.cleanup_on_exit(), ExitStack() as layer:
        def sb(n, s, d=F32):
            return layer.enter_context(nc.sbuf_tensor(f"L1_{n}", s, d))

        haug = sb("haug", [P, NT * (D + 2)])
        scol, s01, dcol, d01, flat = (sb(n, [P, HEADS + 1, NT]) for n in ("scol", "s01", "dcol", "d01", "flat"))
        top = sb("top", [P, NP], BF16)
        A = sb("A", [P, NQ])
        B = sb("B", [P, NQ])
        with nc.sbuf_tensor("L1_hT", [P, 2 * NP], F32) as m.hT:
            norm(nc, m, "L1_norm", False, haug, None)
            gat_vectors(nc, m, "L1_vec", io, scol, dcol, d01)
        with nc.sbuf_tensor("L1_edge", [P, NP], BF16) as edge:
            gat_tops(nc, "L1_tops", io.adjT, dcol, top, edge)
            gat_shifts(nc, m, "L1_shifts", scol, s01, dcol, top, edge, flat, A, B)
        gat(nc, m, "L1_gat", io, scol, s01, dcol, d01, flat, top, A, B, haug)


def hyper_layer(nc, m, io):
    with nc.cleanup_on_exit(), ExitStack() as layer:
        def sb(n, s, d=F32):
            return layer.enter_context(nc.sbuf_tensor(f"L3_{n}", s, d))

        gaug = sb("gaug", [P, NT * (D + 2)])
        with nc.sbuf_tensor("L3_haug", [P, NT * (D + 2)], F32) as haug, \
                nc.sbuf_tensor("L3_mx", [P, NT * D], F32) as mx:
            with nc.sbuf_tensor("L3_hT", [P, 2 * NP], F32) as m.hT:
                norm(nc, m, "L3_norm", False, haug, None)
            row_product(nc, m, "L3_mx", haug, D + 2, m.ones, mx, io.w["L3"])
            hyper_points(nc, "L3_points", haug, mx, gaug)
        U = sb("U", [P, NT * (D + 2)])
        big = sb("big", [P, NT * D])
        mean_sums(nc, "L3_mean", io.adjT, gaug, U)
        hyper_mean(nc, m, "L3_out", U, big)


def program(nc, io, layers):
    with ExitStack() as ctx:
        m = Mem()
        setup(nc, ctx, m, io)
        if "L0" in layers:
            attention_layer(nc, m, io, "L0", True)
        if "L1" in layers:
            gat_layer(nc, m, io)
        if "L2" in layers:
            attention_layer(nc, m, io, "L2", False)
        if "L3" in layers:
            hyper_layer(nc, m, io)
        store(nc, m, io.out)


LAYERS = ("L0", "L1", "L2", "L3")


def kernel(**inputs):
    import concourse.bacc as bacc
    from concourse.bass_utils import run_bass_kernel_spmd as run

    nc = bacc.Bacc("TRN2", target_bir_lowering=False, num_devices=1)
    arrays = {}

    def given(name, array):
        array = np.ascontiguousarray(array)
        arrays[name] = array
        return nc.dram_tensor(name, array.shape, mybir.dt.from_np(array.dtype), kind="ExternalInput").ap()

    adj = np.asarray(inputs["adj"])
    pad = ((0, NP - N), (0, NP - N))
    io = Io()
    io.x = given("x", inputs["x"])
    io.adj = given("adj_padded", np.pad(adj, pad))
    io.adjT = given("adj_transposed", np.pad(adj.T, pad))
    io.ptr = given("ptr", np.asarray(inputs["L0_gnn_ptr"]).reshape(NG, 1))
    io.w, io.b = {}, {}
    for layer in ("L0", "L2"):
        for k in "qkv":
            io.w[layer + k] = given(f"{layer}_W{k}_transposed", np.asarray(inputs[f"{layer}_gnn_W{k}"]).T)
            b = np.asarray(inputs[f"{layer}_gnn_b{k}"])
            io.b[layer + k] = given(f"{layer}_b{k}", b if k == "v" else b.reshape(2, P).T)
    io.w["L1"] = given("L1_W", inputs["L1_gnn_W"])
    io.w["L1T"] = given("L1_W_transposed", np.asarray(inputs["L1_gnn_W"]).T)
    io.a = given("L1_a", np.asarray(inputs["L1_gnn_a"]).reshape(HEADS, 2, 2, P).transpose(3, 0, 2, 1))
    io.w["L3"] = given("L3_W", inputs["L3_gnn_W"])
    io.out = nc.dram_tensor("out", (N, D), F32, kind="ExternalOutput").ap()
    program(nc, io, LAYERS)
    return run(nc, [arrays], core_ids=[0]).results[0]["out"]
```

```python
from contextlib import ExitStack

import numpy as np
import concourse.bass as bass
from concourse import mybir

ALU = mybir.AluOpType
ACT = mybir.ActivationFunctionType
AX = mybir.AxisListType
F32 = mybir.dt.float32
F16 = mybir.dt.float16
BF16 = mybir.dt.bfloat16
I32 = mybir.dt.int32

P = 128
N = 3327
D = 256
NT = (N + P - 1) // P
NP = NT * P
HEADS = 4
NG = 33
W = 512
NB = NP // W
TAIL = NP - NB * W
NGRP = NT // 2
QUARTER = NP // 4
BIG = float(2.0 ** 100)
EPS = 1e-5
LOG_P = float(np.log(256.0))


class Mem:
    pass


def cols(start, size):
    return bass.ds(start, size)


def chunks(total, size):
    return [(a, min(size, total - a)) for a in range(0, total, size)]


def wait_apart(eng, sem, value, waited):
    eng.wait_ge(sem, value)
    eng.sem_inc(waited, 1)


class Chain:

    def __init__(self, eng, sem):
        self.eng, self.sem, self.count = eng, sem, 0

    def __call__(self, ins):
        self.count += 1
        ins.then_inc(self.sem, 1)
        self.eng.wait_ge(self.sem, self.count)


def setup(nc, ctx, m, io):
    def sb(n, s, d=F32):
        return ctx.enter_context(nc.sbuf_tensor(n, s, d))

    m.x = sb("state", [P, NT * D])
    m.ident = sb("ident", [P, P])
    m.identb = sb("identb", [P, P], BF16)
    m.ones = sb("ones", [P, P])
    m.padneg = sb("padneg", [P, 1])
    m.rstd = sb("rstd", [P, NT])
    m.nbias = sb("nbias", [P, NT])
    x_cleared, x_body, x_last, set_steps, pool_steps = (
        nc.alloc_semaphore(n) for n in ("x_cleared", "x_body", "x_last", "set_steps", "pool_steps"))
    with nc.sbuf_tensor("pidx", [P, 1], F32) as pidx, nc.Block() as block:
        xt = m.x[:].rearrange("p (t d) -> p t d", t=NT)
        m.x_in = [x_body, x_last]

        @block.sync
        def _(sp):
            sp.dma_start(xt[:, 0:NT - 1, :],
                         io.x[0:(NT - 1) * P, :].rearrange("(t p) d -> p t d", p=P)).then_inc(x_body, 16)
            sp.wait_ge(x_cleared, 1)
            sp.dma_start(xt[0:N - (NT - 1) * P, NT - 1, :], io.x[(NT - 1) * P:N, :]).then_inc(x_last, 16)

        @block.gpsimd
        def _(pool):
            pool.iota(pidx[:], pattern=[[0, 1]], base=0, channel_multiplier=1,
                      allow_small_or_imprecise_dtypes=True).then_inc(pool_steps, 1)
            pool.memset(m.ident[:], 0.0).then_inc(pool_steps, 1)
            pool.wait_ge(pool_steps, 2)
            pool.affine_select(out=m.ident[:], in_=m.ident[:], compare_op=ALU.not_equal, fill=1.0,
                               base=0, pattern=[[-1, P]], channel_multiplier=1).then_inc(pool_steps, 1)

        @block.vector
        def _(dve):
            dve.memset(xt[:, NT - 1, :], 0.0).then_inc(x_cleared, 1)
            dve.memset(m.ones[:], 1.0).then_inc(set_steps, 1)
            dve.wait_ge(pool_steps, 3)
            dve.tensor_copy(m.identb[:], m.ident[:]).then_inc(set_steps, 1)
            dve.tensor_scalar(m.padneg[:], pidx[:], float(P - 1), -1e30, ALU.is_ge,
                              ALU.mult).then_inc(set_steps, 1)


def norm(nc, m, name, split, haug, hlow, x_in=()):
    width = D + 2
    with ExitStack() as ctx:
        def sb(n, s, d=F32):
            return ctx.enter_context(nc.sbuf_tensor(f"{name}_{n}", s, d))

        def sem(n):
            return nc.alloc_semaphore(f"{name}_{n}")

        PART = NT // 2
        stat = sb("stat", [P, PART * 6])
        mv = sb("mv", [P, PART * 2])
        mvall = sb("mvall", [P, NT, 2])
        std = sb("std", [P, NT])
        stage = sb("stage", [P, 2, D])
        psT = ctx.enter_context(nc.psum_tensor(f"{name}_psT", [P, 2, W], F32))
        stat_steps, waited = sem("stat_steps"), sem("waited")
        var_ready, std_ready, scale_ready = sem("var_ready"), sem("std_ready"), sem("scale_ready")
        row_steps = sem("row_steps")
        h_ready, transposed, h_split, hT_stored = sem("h_ready"), sem("transposed"), sem("h_split"), sem("hT_stored")
        block = ctx.enter_context(nc.Block())
        hT3 = m.hT[:].rearrange("p (c n) -> p c n", c=2)
        ha = haug[:].rearrange("p (t w) -> p t w", t=NT)

        @block.vector
        def _(dve):
            for loaded in x_in:
                dve.wait_ge(loaded, 16)
            with dve.Fori(0, 2) as i:
                for t in range(PART):
                    dve.bn_stats(stat[:, 6 * t:6 * t + 6], m.x[:, cols(i * PART * D + t * D, D)]).then_inc(stat_steps, 1)
                for t in range(PART):
                    if t % 4 == 0:
                        wait_apart(dve, stat_steps, i * 2 * PART + min(t + 4, PART), waited)
                    dve.bn_aggr(mv[:, 2 * t:2 * t + 2], stat[:, 6 * t:6 * t + 6]).then_inc(stat_steps, 1)
                dve.wait_ge(stat_steps, i * 2 * PART + 2 * PART)
                dve.tensor_copy(mvall[:].rearrange("p t k -> p (t k)")[:, cols(i * 2 * PART, 2 * PART)], mv[:]).then_inc(row_steps, 1)
                wait_apart(dve, row_steps, i + 1, waited)
            dve.wait_ge(row_steps, 2)
            dve.tensor_scalar(std[:], mvall[:, :, 1], EPS, None, ALU.add).then_inc(var_ready, 1)
            dve.wait_ge(std_ready, 1)
            dve.reciprocal(m.rstd[:], std[:]).then_inc(row_steps, 1)
            dve.wait_ge(row_steps, 3)
            dve.scalar_tensor_tensor(out=m.nbias[:], in0=mvall[:, :, 0], scalar=-1.0, in1=m.rstd[:],
                                     op0=ALU.mult, op1=ALU.mult).then_inc(scale_ready, 1)
            dve.memset(ha[:, :, D:D + 2], 1.0).then_inc(row_steps, 1)
            if split:
                dve.memset(hlow[:].rearrange("p (t w) -> p t w", t=NT)[:, :, D:D + 2], 0.0).then_inc(row_steps, 1)
            with dve.Fori(0, NT // 2) as i:
                for u in range(2):
                    dve.wait_ge(h_ready, i * 2 + u + 1)
                    dve.tensor_copy(haug[:, cols((i * 2 + u) * width, D)], stage[:, u, :]).then_inc(row_steps if split else h_split, 1)
                if split:
                    for u in range(2):
                        at = cols((i * 2 + u) * width, D)
                        dve.wait_ge(row_steps, i * 2 + u + 6)
                        dve.tensor_tensor(hlow[:, at], stage[:, u, :], haug[:, at], ALU.subtract).then_inc(h_split, 1)
                for u in range(2):
                    dve.wait_ge(transposed, i * 2 + u + 1)
                    dve.tensor_copy(hT3[:, :, cols(i * 2 * P + u * P, P)],
                                    psT[:, u, 0:2 * P].rearrange("p (c n) -> p c n", c=2)).then_inc(hT_stored, 1)

        @block.scalar
        def _(act):
            act.preload_act_table(ACT.Sqrt)
            act.wait_ge(var_ready, 1)
            act.activation(std[:], std[:], ACT.Sqrt).then_inc(std_ready, 1)
            act.preload_act_table(ACT.Exp)
            act.wait_ge(scale_ready, 1)
            for u in range(2):
                act.activation(stage[:, u, :], m.x[:, u * D:(u + 1) * D], ACT.Relu,
                               scale=m.rstd[:, u:u + 1], bias=m.nbias[:, u:u + 1]).then_inc(h_ready, 1)
            with act.Fori(1, NT // 2) as i:
                for u in range(2):
                    act.wait_ge(h_split, i * 2 + u - 1)
                    act.wait_ge(transposed, i * 2 + u - 1)
                    act.activation(stage[:, u, :], m.x[:, cols(i * 2 * D + u * D, D)], ACT.Relu,
                                   scale=m.rstd[:, cols(i * 2 + u, 1)],
                                   bias=m.nbias[:, cols(i * 2 + u, 1)]).then_inc(h_ready, 1)

        @block.tensor
        def _(pe):
            pe.wait_ge(h_ready, 1)
            for u in range(2):
                pe.wait_ge(h_ready, u + 1)
                for c in range(2):
                    mm = pe.transpose(psT[:, u, c * P:(c + 1) * P], stage[:, u, c * P:(c + 1) * P], m.ident[:])
                mm.then_inc(transposed, 1)
            with pe.Fori(1, NT // 2) as i:
                for u in range(2):
                    pe.wait_ge(h_ready, i * 2 + u + 1)
                    pe.wait_ge(hT_stored, i * 2 + u - 1)
                    for c in range(2):
                        mm = pe.transpose(psT[:, u, c * P:(c + 1) * P], stage[:, u, c * P:(c + 1) * P], m.ident[:])
                    mm.then_inc(transposed, 1)


def queries_keys(nc, m, name, io_q, io_k, bq, bk, q_parts, k_parts):
    with ExitStack() as ctx:
        def sb(n, s, d=F32):
            return ctx.enter_context(nc.sbuf_tensor(f"{name}_{n}", s, d))

        def sem(n):
            return nc.alloc_semaphore(f"{name}_{n}")

        wt = [sb(f"w{k}", [P, 2, D]) for k in "qk"]
        bias = [sb(f"b{k}", [P, 2]) for k in "qk"]
        whole = sb("whole", [P, 4, W])
        ps = ctx.enter_context(nc.psum_tensor(f"{name}_ps", [P, 4, W], F32))
        weights_in = [sem(f"weights_in{k}") for k in range(4)]
        bias_scaled = sem("bias_scaled")
        product_done, whole_ready, high_ready, low_ready = sem("product_done"), sem("whole_ready"), sem("high_ready"), sem("low_ready")
        block = ctx.enter_context(nc.Block())
        parts = [q_parts, k_parts]

        @block.sync
        def _(sp):
            for k, src in enumerate((io_q, io_k)):
                sp.dma_start(wt[k][:], src.rearrange("(c p) d -> p c d", p=P)).then_inc(weights_in[k], 16)
            for k, src in enumerate((bq, bk)):
                sp.dma_start(bias[k][:], src).then_inc(weights_in[2 + k], 16)

        def each_block(eng, body):
            with eng.Fori(0, NB) as b:
                body(b, W, b * 4)
            body(NB, TAIL, NB * 4)

        @block.tensor
        def _(pe):
            for s in weights_in[0:2]:
                pe.wait_ge(s, 16)

            def body(b, w, done):
                for k in range(4):
                    pe.wait_ge(whole_ready, done + k + 1)
                    for c in range(2):
                        mm = pe.matmul(ps[:, k, 0:w], wt[k // 2][:, c, (k % 2) * P:(k % 2 + 1) * P],
                                       m.hT[:, cols(b * W + c * NP, w)], start=(c == 0), stop=(c == 1))
                    mm.then_inc(product_done, 1)
            each_block(pe, body)

        @block.scalar
        def _(act):
            act.preload_act_table(ACT.Exp)
            for s in weights_in[2:4]:
                act.wait_ge(s, 16)
            act.mul(bias[0][:], bias[0][:], 1.0 / 32).then_inc(bias_scaled, 1)
            act.sem_inc(whole_ready, 4)
            act.wait_ge(bias_scaled, 1)

            def body(b, w, done):
                for k in range(4):
                    act.wait_ge(product_done, done + k + 1)
                    act.wait_ge(low_ready, done + k + 1)
                    act.activation(whole[:, k, 0:w], ps[:, k, 0:w], ACT.Identity, bias=bias[k // 2][:, k % 2:k % 2 + 1],
                                   scale=1.0 / 32 if k < 2 else 1.0).then_inc(whole_ready, 1)
            each_block(act, body)

        @block.vector
        def _(dve):
            dve.sem_inc(low_ready, 4)

            def body(b, w, done):
                for k in range(4):
                    high, low = parts[k // 2]
                    at = cols(b * W + (k % 2) * (NQ if k < 2 else NP), w)
                    dve.wait_ge(whole_ready, done + k + 5)
                    dve.tensor_copy(high[:, at], whole[:, k, 0:w]).then_inc(high_ready, 1)
                    dve.wait_ge(high_ready, done + k + 1)
                    dve.tensor_tensor(low[:, at], whole[:, k, 0:w], high[:, at], ALU.subtract).then_inc(low_ready, 1)
            each_block(dve, body)


NQ = (NB + 1) * W


def aug_graphs(nc, name, ptr, augI, augJ, notJ, q_parts):
    with ExitStack() as ctx:
        def sb(n, s, d=F32):
            return ctx.enter_context(nc.sbuf_tensor(f"{name}_{n}", s, d))

        def sem(n):
            return nc.alloc_semaphore(f"{name}_{n}")

        G = NG + 1
        bounds = sb("bounds", [G, 2], I32)
        edges = sb("edges", [G, 2])
        node = sb("node", [G, NP])
        hot = sb("hot", [G, NP])
        bounds_cleared, low_in, high_in, node_ready, dve_steps = (
            sem("bounds_cleared"), sem("low_in"), sem("high_in"), sem("node_ready"), sem("dve_steps"))
        block = ctx.enter_context(nc.Block())

        @block.sync
        def _(sp):
            sp.wait_ge(bounds_cleared, 1)
            sp.dma_start(bounds[1:G, 0:1], ptr).then_inc(low_in, 16)
            sp.dma_start(bounds[0:G - 1, 1:2], ptr).then_inc(high_in, 16)

        @block.gpsimd
        def _(pool):
            pool.iota(node[:], pattern=[[1, NP]], base=0, channel_multiplier=0,
                      allow_small_or_imprecise_dtypes=True).then_inc(node_ready, 1)

        @block.vector
        def _(dve):
            steps = 0

            def done(ins):
                nonlocal steps
                steps += 1
                ins.then_inc(dve_steps, 1)
                return steps

            done(dve.memset(bounds[:, 0:1], -1))
            dve.memset(bounds[:, 1:2], 1 << 30).then_inc(dve_steps, 1)
            steps += 1
            dve.wait_ge(dve_steps, 2)
            dve.memset(edges[:], 0.0).then_inc(bounds_cleared, 1)
            done(dve.memset(augI[:], 0.0))
            done(dve.memset(augJ[:], 0.0))
            done(dve.memset(notJ[:], 0.0))
            for q in q_parts:
                for c in range(2):
                    done(dve.memset(q[:, c * NQ + NP:(c + 1) * NQ], 0.0))
            dve.wait_ge(low_in, 16)
            dve.wait_ge(high_in, 16)
            dve.wait_ge(bounds_cleared, 1)
            n = done(dve.tensor_copy(edges[:], bounds[:]))
            dve.wait_ge(dve_steps, n)
            dve.wait_ge(node_ready, 1)
            n = done(dve.tensor_scalar(hot[:], node[:], edges[:, 0:1], None, ALU.is_ge))
            dve.wait_ge(dve_steps, n)
            n = done(dve.scalar_tensor_tensor(out=hot[:], in0=node[:], scalar=edges[:, 1:2], in1=hot[:],
                                              op0=ALU.is_lt, op1=ALU.mult))
            dve.wait_ge(dve_steps, n)
            done(dve.tensor_scalar(augI[0:G, 0:NP], hot[:], -BIG, None, ALU.mult))
            done(dve.tensor_scalar(augJ[0:G, :], hot[:], -1.0, 1.0, ALU.mult, ALU.add))
            n = done(dve.tensor_scalar(notJ[0:G, :], hot[:], -1.0, None, ALU.mult))
            dve.wait_ge(dve_steps, n)
            done(dve.memset(augJ[0:G, N:NP], 1.0))
            done(dve.memset(notJ[0:G, N:NP], -1.0))
            done(dve.memset(augJ[64:67, :], 1.0))


def row_max(nc, name, adj, q_parts, kh, graphs, augI, augJ, notJ, negm, zoff):
    with ExitStack() as ctx:
        def sb(n, s, d=F32):
            return ctx.enter_context(nc.sbuf_tensor(f"{name}_{n}", s, d))

        def sem(n):
            return nc.alloc_semaphore(f"{name}_{n}")

        rows = sb("rows", [P, 2, NP])
        junk = sb("junk", [P, 4, QUARTER], BF16)
        best = sb("best", [P, 2, 4])
        least = sb("least", [P, 2, 4])
        top = sb("top", [P, 2])
        low = sb("low", [P, 2])
        if graphs:
            masked = sb("masked", [P, 2, NP])
            junk2 = sb("junk2", [P, NP], BF16)
            shift = sb("shift", [P, 2])
            zt = sb("zt", [P, 2])
        ps = [ctx.enter_context(nc.psum_tensor(f"{name}_ps{k}", [P, 2 * W], F32)) for k in range(4)]
        kinds = ("scores", "graphs") if graphs else ("scores",)
        per_tile = 4 * len(kinds)
        rows_in = [sem(f"rows_in{k}") for k in range(2)]
        rows_used, products, bank_free, max_steps = sem("rows_used"), sem("products"), sem("bank_free"), sem("max_steps")
        shift_ready, sums_ready, waited, aug_steps = sem("shift_ready"), sem("sums_ready"), sem("waited"), sem("aug_steps")
        qh = q_parts[0]
        block = ctx.enter_context(nc.Block())

        @block.sync
        def _(sp):
            with sp.Fori(0, NT // 2) as i:
                for u in range(2):
                    sp.wait_ge(rows_used, i * 2 + u + 1)
                    sp.dma_start(rows[:, u, :], adj[cols(i * 2 * P + u * P, P), :]).then_inc(rows_in[u], 16)

        if not graphs:
            @block.gpsimd
            def _(pool):
                pool.memset(augI[:], 0.0).then_inc(aug_steps, 1)
                pool.memset(augJ[:], 0.0).then_inc(aug_steps, 1)
                for q in q_parts:
                    for c in range(2):
                        pool.memset(q[:, c * NQ + NP:(c + 1) * NQ], 0.0).then_inc(aug_steps, 1)
                pool.wait_ge(aug_steps, 6)
                pool.memset(augI[0:1, :], 1.0).then_inc(aug_steps, 1)
                pool.memset(augJ[0:1, N:NP], -BIG).then_inc(aug_steps, 1)

        @block.tensor
        def _(pe):
            with pe.Fori(0, NT // 2) as i:
                for u in range(2):
                    at = i * 2 * P + u * P
                    for part in range(4):
                        for kind in kinds:
                            n = len(kinds) * part + kinds.index(kind)
                            pe.wait_ge(bank_free, i * 2 * per_tile + u * per_tile + n + 1)
                            for a, w in chunks(QUARTER, W):
                                key = part * QUARTER + a
                                out = ps[n % 4][:, a:a + w]
                                if kind == "scores":
                                    for c in range(2):
                                        mm = pe.matmul(out, qh[:, cols(at + c * NQ, P)], kh[:, c * NP + key:c * NP + key + w],
                                                       start=(c == 0), stop=(c == 1 and not graphs))
                                    if graphs:
                                        mm = pe.matmul(out, augI[:, cols(at, P)], augJ[:, key:key + w],
                                                       start=False, stop=True)
                                else:
                                    mm = pe.matmul(out, augI[:, cols(at, P)], notJ[:, key:key + w], start=True, stop=True)
                            mm.then_inc(products, 1)

        @block.vector
        def _(dve):
            dve.sem_inc(bank_free, 4)
            dve.sem_inc(rows_used, 2)
            per_max = 4 if graphs else 2

            def reductions(i, u, part):
                a = part * QUARTER
                w = min(QUARTER, N - a)
                n = len(kinds) * part
                done = i * 2 * per_tile + u * per_tile + n
                wait_apart(dve, products, done + 1, waited)
                dve.tensor_tensor_reduce(junk[:, part, 0:w], rows[:, u, a:a + w], ps[n % 4][:, 0:w], 1.0, -3e38,
                                         ALU.add, ALU.max, best[:, u, part:part + 1]).then_inc(bank_free, 1)
                if graphs:
                    wait_apart(dve, products, done + 2, waited)
                    dve.tensor_tensor_reduce(masked[:, u, a:a + QUARTER], rows[:, u, a:a + QUARTER],
                                             ps[(n + 1) % 4][:, 0:QUARTER], 1.0, 3e38,
                                             ALU.add, ALU.min, least[:, u, part:part + 1]).then_inc(bank_free, 1)

            def across_parts(i, u):
                dve.wait_ge(bank_free, i * 2 * per_tile + (u + 1) * per_tile + 4)
                dve.tensor_reduce(top[:, u:u + 1], best[:, u, :], AX.X, ALU.max).then_inc(max_steps, 1)
                if graphs:
                    dve.tensor_reduce(low[:, u:u + 1], least[:, u, :], AX.X, ALU.min).then_inc(max_steps, 1)
                dve.sem_inc(rows_used, 1)

            def across_kinds(i, u):
                if graphs:
                    dve.wait_ge(max_steps, i * 2 * per_max + u * per_max + 2)
                    dve.scalar_tensor_tensor(out=top[:, u:u + 1], in0=low[:, u:u + 1], scalar=-1e6, in1=top[:, u:u + 1],
                                             op0=ALU.mult, op1=ALU.max).then_inc(max_steps, 1)

            def shifts(i, u):
                dve.wait_ge(max_steps, i * 2 * per_max + u * per_max + per_max - 1)
                if graphs:
                    dve.tensor_scalar(shift[:, u:u + 1], top[:, u:u + 1], -2.0, LOG_P, ALU.mult, ALU.add).then_inc(shift_ready, 1)
                dve.tensor_scalar(negm[:, cols(i * 2 + u, 1)], top[:, u:u + 1], -1.0, LOG_P / 2, ALU.mult,
                                  ALU.add).then_inc(max_steps, 1)

            with dve.Fori(0, NT // 2) as i:
                for u in range(2):
                    dve.wait_ge(rows_in[u], i * 16 + 16)
                    if graphs:
                        dve.wait_ge(sums_ready, i * 2 + u + 1)
                    for part in range(4):
                        reductions(i, u, part)
                        if graphs and u == 1:
                            if part == 0:
                                across_parts(i, 0)
                            if part == 1:
                                across_kinds(i, 0)
                            if part == 2:
                                shifts(i, 0)
                    if u == 1 or not graphs:
                        across_parts(i, u)
                        across_kinds(i, u)
                        shifts(i, u)

        if graphs:
            @block.scalar
            def _(act):
                act.preload_act_table(ACT.Exp)
                act.sem_inc(sums_ready, 2)
                with act.Fori(0, NT // 2) as i:
                    for u in range(2):
                        act.wait_ge(shift_ready, i * 2 + u + 1)
                        act.activation(junk2[:], masked[:, u, :], ACT.Exp, bias=shift[:, u:u + 1], scale=-2e6,
                                       accum_out=zt[:, u:u + 1]).then_inc(sums_ready, 1)
                        act.wait_ge(sums_ready, i * 2 + u + 3)
                        act.copy(zoff[:, cols(i * 2 + u, 1)], zt[:, u:u + 1])


def shift_rows(nc, name, identb, negm, rows_out, augI):
    with ExitStack() as ctx:
        def sb(n, s, d=F32):
            return ctx.enter_context(nc.sbuf_tensor(f"{name}_{n}", s, d))

        def sem(n):
            return nc.alloc_semaphore(f"{name}_{n}")

        part = sb("part", [P, 3, NT], BF16)
        rest = sb("rest", [P, 2, NT])
        tiles = sb("tiles", [NT, 3, P], BF16)
        ps = ctx.enter_context(nc.psum_tensor(f"{name}_ps", [P, W], F32))
        dve_steps, turned, tiles_ready, rows_stored, rows_in = (
            sem("dve_steps"), sem("turned"), sem("tiles_ready"), sem("rows_stored"), sem("rows_in"))
        block = ctx.enter_context(nc.Block())

        @block.vector
        def _(dve):
            chain = Chain(dve, dve_steps)
            chain(dve.tensor_copy(part[:, 0, :], negm[:]))
            for k in range(2):
                whole = negm[:] if k == 0 else rest[:, 0, :]
                chain(dve.tensor_tensor(rest[:, k, :], whole, part[:, k, :], ALU.subtract))
                chain(dve.tensor_copy(part[:, k + 1, :], rest[:, k, :]))
            dve.wait_ge(turned, 1)
            dve.tensor_copy(tiles[:].rearrange("t k p -> t (k p)"), ps[0:NT, 0:3 * P]).then_inc(tiles_ready, 1)

        @block.tensor
        def _(pe):
            pe.wait_ge(dve_steps, 5)
            for k in range(3):
                mm = pe.matmul(ps[0:NT, k * P:(k + 1) * P], part[:, k, :], identb[:], start=True, stop=True)
            mm.then_inc(turned, 1)

        @block.sync
        def _(sp):
            sp.wait_ge(tiles_ready, 1)
            sp.dma_start(rows_out.rearrange("k (t p) -> t k p", p=P), tiles[:]).then_inc(rows_stored, 16)
            sp.wait_ge(rows_stored, 16)
            sp.dma_start(augI[64:67, 0:NP], rows_out).then_inc(rows_in, 16)
            sp.wait_ge(rows_in, 16)


def shift_everywhere(nc, name, ident, negm, row_out, shift):
    with ExitStack() as ctx:
        def sem(n):
            return nc.alloc_semaphore(f"{name}_{n}")

        tiles = ctx.enter_context(nc.sbuf_tensor(f"{name}_tiles", [NT, P], F32))
        ps = ctx.enter_context(nc.psum_tensor(f"{name}_ps", [P, W], F32))
        turned, tiles_ready, row_stored, shift_in, pad_cleared = (
            sem("turned"), sem("tiles_ready"), sem("row_stored"), sem("shift_in"), sem("pad_cleared"))
        block = ctx.enter_context(nc.Block())

        @block.tensor
        def _(pe):
            pe.transpose(ps[0:NT, 0:P], negm[:], ident[:]).then_inc(turned, 1)

        @block.vector
        def _(dve):
            dve.memset(shift[:, NP:NQ], 0.0).then_inc(pad_cleared, 1)
            dve.wait_ge(turned, 1)
            dve.tensor_copy(tiles[:], ps[0:NT, 0:P]).then_inc(tiles_ready, 1)

        @block.sync
        def _(sp):
            sp.wait_ge(tiles_ready, 1)
            sp.dma_start(row_out.rearrange("(t p) -> t p", p=P), tiles[:]).then_inc(row_stored, 16)
            sp.wait_ge(row_stored, 16)
            sp.dma_start(shift[:, 0:NP], row_out.partition_broadcast(P)).then_inc(shift_in, 16)
            sp.wait_ge(shift_in, 16)


def over_blocks(eng, one):
    with eng.Fori(0, NB) as b:
        one(b, W, W)
    one(NB, TAIL, None)


def later_groups(eng, step, b, w, n0, begin=0):
    def four(i):
        for u in range(4):
            g = i * 4 + u + 1
            step(b, w, g, u, n0 + g)
    with eng.Fori(begin, NGRP // 4) as i:
        four(i)


FIRST = 4


def pslot(slot):
    return 2 if slot == FIRST else slot % 2


def bslot(slot):
    return 1 if slot == FIRST else slot % 2


def load_blocks(sp, adjT, ring, adj_in, used, n0):
    def step(b, w, g, slot, n):
        sp.wait_ge(used, n + (1 if slot == FIRST else 2))
        sp.dma_start(ring[:, slot, :, 0:w],
                     adjT[cols(g * 2 * P, 2 * P), cols(b * W, w)].rearrange("(u p) i -> p u i", p=P)
                     ).then_inc(adj_in[slot], 16)

    def one(b, w, next_w):
        n = n0 + b * NGRP
        step(b, w, 0, FIRST, n)
        later_groups(sp, step, b, w, n)
    over_blocks(sp, one)


def arrived(dve, adj_in, b, g, slot, before=0):
    if slot == FIRST:
        dve.wait_ge(adj_in[slot], (b + before) * 16 + 16)
    else:
        dve.wait_ge(adj_in[slot], (b + before) * 48 + (g - 1 - slot) * 4 + 16)


def attend(nc, name, adjT, q_parts, k_parts, augI, augJ, hh, hl, U, edge=None, shift=None):
    width = D + 2
    with ExitStack() as ctx:
        def sb(n, s, d=F32):
            return ctx.enter_context(nc.sbuf_tensor(f"{name}_{n}", s, d))

        def sem(n):
            return nc.alloc_semaphore(f"{name}_{n}")

        ring = sb("ring", [P, 5, 2, W])
        t = sb("t", [P, 3, 2, W])
        ph = sb("ph", [P, 3, 2, W], F16)
        pl = sb("pl", [P, 3, 2, W], F16)
        psS = [ctx.enter_context(nc.psum_tensor(f"{name}_psS{k}", [P, 2, W], F32)) for k in range(2)]
        acc = [ctx.enter_context(nc.psum_tensor(f"{name}_acc{k}", [P, W], F32)) for k in range(4)]
        adj_in = [sem(f"adj_in{k}") for k in range(5)]
        scores_ready, added, exp_ready, probs_ready, summed, stored = (
            sem("scores_ready"), sem("added"), sem("exp_ready"), sem("probs_ready"), sem("summed"), sem("stored"))
        edge_steps, released, shifted = sem("edge_steps"), sem("released"), sem("shifted")
        block = ctx.enter_context(nc.Block())

        @block.sync
        def _(sp):
            load_blocks(sp, adjT, ring, adj_in, added if edge is None else released, 0)

        @block.tensor
        def _(pe):
            kh, kl = k_parts
            qh, ql = q_parts

            def scores(b, w, g, slot, need, last=False):
                pe.wait_ge(added, need)
                for u in range(2):
                    key = g * 2 * P + u * P
                    out = psS[bslot(slot)][:, u, 0:w]
                    aug = shift is None or (last and u == 1)
                    if aug:
                        pe.matmul(out, augJ[:, cols(key, P)], augI[:, cols(b * W, w)], start=True, stop=False)
                    for c in range(2):
                        high = kh[:, cols(key + c * NP, P)]
                        pe.matmul(out, high, qh[:, cols(b * W + c * NQ, w)], start=(c == 0 and not aug), stop=False)
                        pe.matmul(out, high, ql[:, cols(b * W + c * NQ, w)], start=False, stop=False)
                        mm = pe.matmul(out, kl[:, cols(key + c * NP, P)], qh[:, cols(b * W + c * NQ, w)],
                                       start=False, stop=(c == 1))
                mm.then_inc(scores_ready, 1)

            def sums(b, w, g, slot, n, first, last):
                pe.wait_ge(probs_ready, n + 3)
                for u in range(2):
                    row = cols(g * 2 * width + u * width, width - 1)
                    for q in range(w // P):
                        if first and u == 0:
                            pe.wait_ge(stored, b * 4 + q + 1)
                        out = acc[q][:, 0:width - 1]
                        high = ph[:, pslot(slot), u, q * P:(q + 1) * P]
                        low = pl[:, pslot(slot), u, q * P:(q + 1) * P]
                        pe.matmul(out, high, hh[:, row], start=(first and u == 0), stop=False)
                        pe.matmul(out, high, hl[:, row], start=False, stop=False)
                        mm = pe.matmul(out, low, hh[:, row], start=False, stop=(last and u == 1))
                mm.then_inc(summed, 1)

            def one(b, w, next_w):
                n0 = b * NGRP

                def step(b, w, g, slot, n, last=False):
                    nxt = (slot + 1) % 4
                    scores(b, w, g + 1, nxt, n + 5, last)
                    sums(b, w, g, slot, n, False, False)

                scores(b, w, 1, 0, n0 + 5)
                sums(b, w, 0, FIRST, n0, True, False)
                later = NGRP // 4
                with pe.Fori(0, later - 1) as i:
                    for u in range(4):
                        step(b, w, i * 4 + u + 1, u, n0 + i * 4 + u + 1)
                for u in range(3):
                    g = (later - 1) * 4 + u + 1
                    step(b, w, g, u, n0 + g, g + 1 == NGRP - 1)
                n = n0 + NGRP - 1
                if next_w:
                    scores(b + 1, next_w, 0, FIRST, n + 6)
                sums(b, w, NGRP - 1, 3, n, False, True)

            scores(0, W, 0, FIRST, 5)
            over_blocks(pe, one)

        @block.vector
        def _(dve):
            dve.sem_inc(added, 5)
            dve.sem_inc(released, 5)
            dve.sem_inc(probs_ready, 2)

            def add(b, w, g, slot, n):
                s = pslot(slot)
                if shift is None:
                    arrived(dve, adj_in, b, g, slot)
                else:
                    dve.wait_ge(shifted, n + 1)
                dve.wait_ge(scores_ready, n + 1)
                dve.wait_ge(probs_ready, n + 1)
                dve.tensor_tensor(t[:, s, :, 0:w], ring[:, slot, :, 0:w], psS[bslot(slot)][:, :, 0:w],
                                  ALU.add).then_inc(added, 1)
                if edge is None:
                    return
                at = cols(b * W, w)
                if slot == FIRST:
                    dve.tensor_tensor(edge[:, at], ring[:, slot, 0, 0:w], ring[:, slot, 1, 0:w], ALU.max).then_inc(released, 1)
                    dve.sem_inc(edge_steps, 1)
                else:
                    dve.wait_ge(released, n + 5)
                    dve.tensor_tensor(edge[:, at], edge[:, at], ring[:, slot, 0, 0:w], ALU.max).then_inc(edge_steps, 1)
                    dve.wait_ge(edge_steps, n + 1)
                    dve.tensor_tensor(edge[:, at], edge[:, at], ring[:, slot, 1, 0:w], ALU.max).then_inc(released, 1)

            def shift_tiles(b, w, g, slot):
                if shift is None:
                    return
                arrived(dve, adj_in, b, g, slot)
                across = shift[:, cols(b * W, w)].rearrange("p (o i) -> p o i", o=1).to_broadcast([P, 2, w])
                dve.tensor_tensor(ring[:, slot, :, 0:w], ring[:, slot, :, 0:w], across, ALU.add).then_inc(shifted, 1)

            def low_half(w, slot, n):
                s = pslot(slot)
                dve.wait_ge(exp_ready, n * 2 + 6)
                dve.wait_ge(summed, n + 1)
                dve.tensor_tensor(pl[:, s, :, 0:w], t[:, s, :, 0:w], ph[:, s, :, 0:w], ALU.subtract).then_inc(probs_ready, 1)

            def one(b, w, next_w):
                n0 = b * NGRP

                def step(b, w, g, slot, n, last=False):
                    low_half(w, (slot - 1) % 4, n - 1)
                    add(b, w, g, slot, n)
                    if not last:
                        shift_tiles(b, w, g + 1, (slot + 1) % 4)

                low_half(w, FIRST, n0)
                add(b, w, 1, 0, n0 + 1)
                shift_tiles(b, w, 2, 1)
                for u in range(1, 4):
                    step(b, w, u + 1, u, n0 + u + 1)
                with dve.Fori(1, NGRP // 4 - 1) as i:
                    for u in range(4):
                        step(b, w, i * 4 + u + 1, u, n0 + i * 4 + u + 1)
                for g in range(NGRP - 4, NGRP):
                    step(b, w, g, (g - 1) % 4, n0 + g, g == NGRP - 1)
                if next_w:
                    shift_tiles(b + 1, next_w, 0, FIRST)
                low_half(w, 3, n0 + NGRP - 1)
                if next_w:
                    add(b + 1, next_w, 0, FIRST, n0 + NGRP)
                    shift_tiles(b + 1, next_w, 1, 0)

            shift_tiles(0, W, 0, FIRST)
            add(0, W, 0, FIRST, 0)
            shift_tiles(0, W, 1, 0)
            over_blocks(dve, one)

        @block.scalar
        def _(act):
            act.preload_act_table(ACT.Exp)
            act.sem_inc(exp_ready, 4)
            act.sem_inc(stored, 4)
            act.sem_inc(summed, 2)

            def exps(b, w, g, slot, n):
                s = pslot(slot)
                act.wait_ge(added, n + 6)
                act.wait_ge(summed, n + 1)
                act.activation(ph[:, s, :, 0:w], t[:, s, :, 0:w], ACT.Exp, scale=2.0).then_inc(exp_ready, 1)
                act.wait_ge(exp_ready, n * 2 + 5)
                act.activation(t[:, s, :, 0:w], t[:, s, :, 0:w], ACT.Exp, scale=2.0).then_inc(exp_ready, 1)

            def one(b, w, next_w):
                n0 = b * NGRP
                later_groups(act, exps, b, w, n0)
                if next_w:
                    exps(b + 1, next_w, 0, FIRST, n0 + NGRP)
                act.wait_ge(summed, n0 + NGRP + 2)
                for q in range(w // P):
                    act.copy(U[:, cols(b * 4 * width + q * width, width - 1)], acc[q][:, 0:width - 1]).then_inc(stored, 1)

            exps(0, W, 0, FIRST, 0)
            over_blocks(act, one)


class RowProduct:

    def __init__(self, ctx, nc, m, name, src, src_width, scale, dst, plus, ps, pso):
        def sb(n, s, d=F32):
            return ctx.enter_context(nc.sbuf_tensor(f"{name}_{n}", s, d))

        def sem(n):
            return nc.alloc_semaphore(f"{name}_{n}")

        self.m, self.src, self.src_width, self.scale, self.dst, self.plus = m, src, src_width, scale, dst, plus
        self.w = sb("w", [P, 2, D])
        self.stage = sb("stage", [P, 2, D])
        self.turned = sb("turned", [P, 2, D])
        self.ps, self.pso = ps, pso
        self.staged, self.transposed, self.turned_ready, self.product_done, self.dst_done, self.biased = (
            sem("staged"), sem("transposed"), sem("turned_ready"), sem("product_done"), sem("dst_done"), sem("biased"))
        self.waited = sem("waited")

    def start_vector(self, dve):
        dve.sem_inc(self.turned_ready, 2)

    def start_scalar(self, act):
        act.sem_inc(self.transposed, 2)
        act.sem_inc(self.dst_done, 2)

    def scalar(self, act):
        with act.Fori(0, NT // 2) as i:
            for u in range(2):
                act.wait_ge(self.transposed, i * 2 + u + 1)
                act.activation(self.stage[:, u, :], self.src[:, cols(i * 2 * self.src_width + u * self.src_width, D)],
                               ACT.Copy, scale=self.scale[:, cols(i * 2 + u, 1)]).then_inc(self.staged, 1)

    def tensor(self, pe):
        m, ps, pso = self.m, self.ps, self.pso

        def turn(i):
            for u in range(2):
                pe.wait_ge(self.staged, i * 2 + u + 1)
                pe.wait_ge(self.turned_ready, i * 2 + u + 1)
                for c in range(2):
                    mm = pe.transpose(ps[u][:, c * P:(c + 1) * P], self.stage[:, u, c * P:(c + 1) * P], m.ident[:])
                mm.then_inc(self.transposed, 1)

        def multiply(i):
            for u in range(2):
                pe.wait_ge(self.turned_ready, i * 2 + u + 3)
                pe.wait_ge(self.dst_done, i * 2 + u + 1)
                for c in range(2):
                    mm = pe.matmul(pso[u][:, 0:D], self.turned[:, u, c * P:(c + 1) * P], self.w[:, c, :],
                                   start=(c == 0), stop=(c == 1))
                mm.then_inc(self.product_done, 1)

        turn(0)
        with pe.Fori(0, NT // 2 - 1) as i:
            turn(i + 1)
            multiply(i)
        multiply(NT // 2 - 1)

    def vector(self, dve, bias=None, share=None):
        def keep(i, u, first=False):
            dve.wait_ge(self.transposed, i * 2 + u + 3)
            if not first:
                dve.wait_ge(self.product_done, i * 2 + u - 1)
            dve.tensor_copy(self.turned[:, u, :], self.ps[u][:, 0:D]).then_inc(self.turned_ready, 1)

        def finish(i, u):
            at = cols(i * 2 * D + u * D, D)
            if bias is not None:
                dve.scalar_tensor_tensor(out=self.dst[:, at], in0=bias[:], scalar=share[:, cols(i * 2 + u, 1)],
                                         in1=self.dst[:, at], op0=ALU.mult, op1=ALU.add).then_inc(self.biased, 1)
                dve.wait_ge(self.biased, i * 2 + u + 1)
            if self.plus:
                dve.wait_ge(self.product_done, i * 2 + u + 1)
                dve.tensor_tensor(self.dst[:, at], self.dst[:, at], self.pso[u][:, 0:D], ALU.add).then_inc(self.dst_done, 1)
            else:
                wait_apart(dve, self.product_done, i * 2 + u + 1, self.waited)
                dve.tensor_copy(self.dst[:, at], self.pso[u][:, 0:D]).then_inc(self.dst_done, 1)

        for u in range(2):
            keep(0, u, True)
        with dve.Fori(0, NT // 2 - 1) as i:
            for u in range(2):
                keep(i + 1, u)
                finish(i, u)
        for u in range(2):
            finish(NT // 2 - 1, u)


def project(nc, m, name, U, weight, bias, zoff):
    with ExitStack() as ctx:
        def sb(n, s, d=F32):
            return ctx.enter_context(nc.sbuf_tensor(f"{name}_{n}", s, d))

        def sem(n):
            return nc.alloc_semaphore(f"{name}_{n}")

        z = sb("z", [P, NT])
        rz = sb("rz", [P, NT])
        share = sb("share", [P, NT])
        b = sb("b", [P, D])
        ps = [ctx.enter_context(nc.psum_tensor(f"{name}_ps{k}", [P, W], F32)) for k in range(4)]
        weight_in, bias_in, z_steps = sem("weight_in"), sem("bias_in"), sem("z_steps")
        rp = RowProduct(ctx, nc, m, name, U, D + 2, rz, m.x, True, ps[0:2], ps[2:4])
        block = ctx.enter_context(nc.Block())
        Z = U[:].rearrange("p (t w) -> p t w", t=NT)[:, :, D]

        @block.sync
        def _(sp):
            sp.dma_start(rp.w[:], weight.rearrange("(c p) d -> p c d", p=P)).then_inc(weight_in, 16)
            sp.dma_start(b[:], bias.partition_broadcast(P)).then_inc(bias_in, 16)

        @block.vector
        def _(dve):
            chain = Chain(dve, z_steps)
            if zoff is not None:
                chain(dve.tensor_tensor(z[:], Z, zoff[:], ALU.add))
            else:
                chain(dve.tensor_copy(z[:], Z))
            chain(dve.reciprocal(rz[:], z[:]))
            chain(dve.tensor_tensor(share[:], Z, rz[:], ALU.mult))
            rp.start_vector(dve)
            dve.wait_ge(bias_in, 16)
            rp.vector(dve, bias=b, share=share)

        @block.scalar
        def _(act):
            act.wait_ge(z_steps, 3)
            rp.start_scalar(act)
            rp.scalar(act)

        @block.tensor
        def _(pe):
            pe.wait_ge(weight_in, 16)
            rp.tensor(pe)


def gat_vectors(nc, m, name, io, scol, dcol, d01):
    with ExitStack() as ctx:
        def sb(n, s, d=F32):
            return ctx.enter_context(nc.sbuf_tensor(f"{name}_{n}", s, d))

        def sem(n):
            return nc.alloc_semaphore(f"{name}_{n}")

        wT = sb("wT", [P, 2 * HEADS, D])
        a = sb("a", [P, HEADS, 2, 2])
        wa = sb("wa", [P, 2, 2 * HEADS])
        psw = ctx.enter_context(nc.psum_tensor(f"{name}_psw", [P, W], F32))
        psc = ctx.enter_context(nc.psum_tensor(f"{name}_psc", [P, W], F32))
        w_in, a_in, wa_done, wa_ready, cols_done, dve_steps = (
            sem("w_in"), sem("a_in"), sem("wa_done"), sem("wa_ready"), sem("cols_done"), sem("dve_steps"))
        block = ctx.enter_context(nc.Block())

        @block.sync
        def _(sp):
            sp.dma_start(wT[:], io.w["L1T"].rearrange("(k p) c -> p k c", p=P)).then_inc(w_in, 16)
            sp.dma_start(a[:], io.a).then_inc(a_in, 16)

        @block.tensor
        def _(pe):
            pe.wait_ge(w_in, 16)
            pe.wait_ge(a_in, 16)
            for c in range(2):
                for h in range(HEADS):
                    at = c * 2 * HEADS + h * 2
                    for k in range(2):
                        mm = pe.matmul(psw[:, at:at + 2], wT[:, h * 2 + k, c * P:(c + 1) * P], a[:, h, k, :],
                                       start=(k == 0), stop=(k == 1))
            mm.then_inc(wa_done, 1)
            pe.wait_ge(wa_ready, 1)
            for t in range(NT):
                for c in range(2):
                    mm = pe.matmul(psc[:, t * 8:t * 8 + 8], m.hT[:, c * NP + t * P:c * NP + (t + 1) * P], wa[:, c, :],
                                   start=(c == 0), stop=(c == 1))
            mm.then_inc(cols_done, 1)

        @block.vector
        def _(dve):
            for col in (scol, dcol):
                dve.memset(col[:, HEADS, :], 0.0).then_inc(dve_steps, 1)
            dve.wait_ge(wa_done, 1)
            dve.tensor_copy(wa[:].rearrange("p c k -> p (c k)"), psw[:, 0:4 * HEADS]).then_inc(wa_ready, 1)
            dve.wait_ge(cols_done, 1)
            both = psc[:, 0:NT * 8].rearrange("p (t h s) -> p s h t", h=HEADS, s=2)
            dve.tensor_copy(scol[:, 0:HEADS, :], both[:, 0]).then_inc(dve_steps, 1)
            dve.tensor_copy(dcol[:, 0:HEADS, :], both[:, 1]).then_inc(dve_steps, 1)
            dve.wait_ge(dve_steps, 4)
            dve.tensor_scalar(dcol[:, 0:HEADS, NT - 1], dcol[:, 0:HEADS, NT - 1], m.padneg[:, 0:1], None,
                              ALU.add).then_inc(dve_steps, 1)
            dve.wait_ge(dve_steps, 5)
            dve.tensor_scalar(d01[:], dcol[:], 0.01, None, ALU.mult).then_inc(dve_steps, 1)


def gat_tops(nc, name, adjT, dcol, top):
    with ExitStack() as ctx:
        def sb(n, s, d=F32):
            return ctx.enter_context(nc.sbuf_tensor(f"{name}_{n}", s, d))

        def sem(n):
            return nc.alloc_semaphore(f"{name}_{n}")

        ring = sb("ring", [P, 5, 2, W])
        cand = sb("cand", [P, 3, 2, W], BF16)
        adj_in = [sem(f"adj_in{k}") for k in range(5)]
        cand_ready, top_steps = sem("cand_ready"), sem("top_steps")
        block = ctx.enter_context(nc.Block())
        dflat = dcol[:].rearrange("p h t -> p (h t)")

        @block.sync
        def _(sp):
            load_blocks(sp, adjT, ring, adj_in, cand_ready, 0)

        @block.scalar
        def _(act):
            act.sem_inc(cand_ready, 5)

            def step(b, w, g, slot, n):
                s = pslot(slot)
                arrived(act, adj_in, b, g, slot)
                act.wait_ge(top_steps, n * 2 + 2)
                for u in range(2):
                    ins = act.activation(cand[:, s, u, 0:w], ring[:, slot, u, 0:w], ACT.Identity,
                                         bias=dflat[:, cols(g * 2 + u, 1)])
                ins.then_inc(cand_ready, 1)

            def one(b, w, next_w):
                step(b, w, 0, FIRST, b * NGRP)
                later_groups(act, step, b, w, b * NGRP)
            over_blocks(act, one)

        @block.vector
        def _(dve):
            dve.sem_inc(top_steps, 4)

            def step(b, w, g, slot, n, first=False):
                s = pslot(slot)
                at = cols(b * W, w)
                dve.wait_ge(cand_ready, n + 6)
                if first:
                    dve.tensor_tensor(top[:, at], cand[:, s, 0, 0:w], cand[:, s, 1, 0:w], ALU.max).then_inc(top_steps, 2)
                else:
                    for u in range(2):
                        dve.wait_ge(top_steps, n * 2 + 4 + u)
                        dve.tensor_tensor(top[:, at], top[:, at], cand[:, s, u, 0:w], ALU.max).then_inc(top_steps, 1)

            def one(b, w, next_w):
                step(b, w, 0, FIRST, b * NGRP, True)
                later_groups(dve, step, b, w, b * NGRP)
            over_blocks(dve, one)


def gat_shifts(nc, m, name, scol, s01, dcol, top, edge, flat, A, B):
    with ExitStack() as ctx:
        def sb(n, s, d=F32):
            return ctx.enter_context(nc.sbuf_tensor(f"{name}_{n}", s, d))

        def sem(n):
            return nc.alloc_semaphore(f"{name}_{n}")

        peak = sb("peak", [P, HEADS])
        diag = sb("diag", [P, 2, W])
        topcol, edgecol, acol, bcol = (sb(n, [P, NT]) for n in ("topcol", "edgecol", "acol", "bcol"))
        dtop = sb("dtop", [P, HEADS])
        ps = [ctx.enter_context(nc.psum_tensor(f"{name}_ps{k}", [P, W], F32)) for k in range(8)]
        steps, diag_ready, rows_done, turned, reduced, stored = (
            sem("steps"), sem("diag_ready"), sem("rows_done"), sem("turned"), sem("reduced"), sem("stored"))
        block = ctx.enter_context(nc.Block())
        widths = [W] * NB + [TAIL]
        BLOCKS = NB + 1

        @block.tensor
        def _(pe):
            pe.wait_ge(diag_ready, 1)
            pe.matmul(ps[7][:], m.ones[:], diag[:, 0, :], start=True, stop=True).then_inc(rows_done, 1)
            for b, w in enumerate(widths):
                if b >= 2:
                    pe.wait_ge(reduced, 2 * b - 2)
                for q in range(w // P):
                    at = b * W + q * P
                    pe.matmul(ps[b % 2][:, q * P:(q + 1) * P], top[:, at:at + P], m.identb[:], start=True, stop=True)
                    mm = pe.matmul(ps[2 + b % 2][:, q * P:(q + 1) * P], edge[:, at:at + P], m.identb[:], start=True, stop=True)
                mm.then_inc(turned, 1)
            for b, w in enumerate(widths):
                pe.wait_ge(diag_ready, 2 + b)
                if b >= 2:
                    pe.wait_ge(stored, 2 * b - 2)
                pe.matmul(ps[4 * (b % 2)][:, 0:w], m.ones[:], diag[:, 0, 0:w], start=True, stop=True)
                pe.matmul(ps[4 * (b % 2) + 1][:, 0:w], m.ones[:], diag[:, 1, 0:w], start=True, stop=True).then_inc(rows_done, 1)

        @block.scalar
        def _(act):
            for b, w in enumerate(widths):
                act.wait_ge(rows_done, 2 + b)
                for k, row in enumerate((A, B)):
                    act.copy(row[:, b * W:b * W + w], ps[4 * (b % 2) + k][:, 0:w]).then_inc(stored, 1)

        @block.vector
        def _(dve):
            chain = Chain(dve, steps)
            chain(dve.tensor_reduce(peak[:], dcol[:, 0:HEADS, :], AX.X, ALU.max))
            for h in range(HEADS):
                ins = dve.tensor_scalar(diag[:, 0, h * P:(h + 1) * P], m.ident[:], peak[:, h:h + 1], None, ALU.mult)
            ins.then_inc(diag_ready, 1)
            for row in (A, B):
                dve.memset(row[:, NP:NQ], 0.0)
            for b, w in enumerate(widths):
                dve.wait_ge(turned, b + 1)
                for k, col in enumerate((topcol, edgecol)):
                    dve.tensor_reduce(col[:, b * 4:b * 4 + w // P],
                                      ps[2 * k + b % 2][:, 0:w].rearrange("p (q j) -> p q j", j=P),
                                      AX.X, ALU.max).then_inc(reduced, 1)
            dve.wait_ge(rows_done, 1)
            chain(dve.tensor_reduce(dtop[:], ps[7][:].rearrange("p (h j) -> p h j", j=P), AX.X, ALU.max))
            chain(dve.tensor_scalar(dtop[:], dtop[:], 0.01, None, ALU.mult))
            chain(dve.tensor_scalar(s01[:], scol[:], 0.01, None, ALU.mult))
            chain(dve.memset(flat[:, HEADS, :], 0.0))
            dve.wait_ge(reduced, 2 * BLOCKS)
            for h in range(HEADS):
                ins = dve.scalar_tensor_tensor(out=flat[:, h, :], in0=s01[:, h, :], scalar=dtop[:, h:h + 1],
                                               in1=edgecol[:], op0=ALU.add, op1=ALU.add)
            chain(ins)
            chain(dve.tensor_tensor(topcol[:], topcol[:], scol[:, 0, :], ALU.add))
            chain(dve.tensor_tensor(topcol[:], topcol[:], flat[:, 0, :], ALU.max))
            chain(dve.tensor_tensor(acol[:], scol[:, 0, :], topcol[:], ALU.subtract))
            chain(dve.tensor_tensor(bcol[:], s01[:, 0, :], topcol[:], ALU.subtract))
            for b, w in enumerate(widths):
                dve.wait_ge(rows_done, 1 + b)
                for k, col in enumerate((acol, bcol)):
                    for q in range(w // P):
                        ins = dve.tensor_scalar(diag[:, k, q * P:(q + 1) * P], m.ident[:],
                                                col[:, b * 4 + q:b * 4 + q + 1], None, ALU.mult)
                ins.then_inc(diag_ready, 1)


def gat(nc, m, name, io, scol, s01, dcol, d01, flat, top, A, B, haug):
    width = D + 2
    with ExitStack() as ctx:
        def sb(n, s, d=F32):
            return ctx.enter_context(nc.sbuf_tensor(f"{name}_{n}", s, d))

        def sem(n):
            return nc.alloc_semaphore(f"{name}_{n}")

        U = sb("U", [P, NT * width])
        weights = sb("weights", [P, (HEADS + 1) * 2 * D])
        ring = sb("ring", [P, 5, 2, W])
        slope = sb("slope", [P, 3, 2, W])
        cand = sb("cand", [P, 3, W], BF16)
        t = sb("t", [P, 3, 2, W])
        p32 = sb("p32", [P, 3, 2, W])
        stage = sb("stage", [P, 4, D])
        turned = sb("turned", [P, 4, D])
        diag = sb("diag", [P, 2, W])
        topcol, acol, bcol, rz = (sb(n, [P, 4]) for n in ("topcol", "acol", "bcol", "rz"))
        own_d, own_next, own_d01, own_candidate = (sb(n, [P, NT]) for n in ("own_d", "own_next", "own_d01", "own_candidate"))
        acc = [ctx.enter_context(nc.psum_tensor(f"{name}_acc{k}", [P, W], F32)) for k in range(4)]
        psT = [ctx.enter_context(nc.psum_tensor(f"{name}_psT{k}", [P, W], F32)) for k in range(2)]
        psO = [ctx.enter_context(nc.psum_tensor(f"{name}_psO{k}", [P, W], F32)) for k in range(2)]
        adj_in = [sem(f"adj_in{k}") for k in range(5)]
        slope_ready, cand_ready, maxed, added, half_top, released, exp_ready, summed = (
            sem("slope_ready"), sem("cand_ready"), sem("maxed"), sem("added"), sem("half_top"), sem("released"),
            sem("exp_ready"), sem("summed"))
        weights_in = [sem(f"weights_in{h}") for h in range(HEADS)]
        weights_cleared, four_ready = sem("weights_cleared"), sem("four_ready")
        stored, rz_ready, staged, transposed, turned_ready, product_done, x_done = (
            sem("stored"), sem("rz_ready"), sem("staged"), sem("transposed"), sem("turned_ready"),
            sem("product_done"), sem("x_done"))
        tops_turned, col_steps, diag_ready, rows_done, ab_ready = (
            sem("tops_turned"), sem("col_steps"), sem("diag_ready"), sem("rows_done"), sem("ab_ready"))
        vector_cols, scalar_cols, waited = sem("vector_cols"), sem("scalar_cols"), sem("waited")
        block = ctx.enter_context(nc.Block())
        BLOCKS = NB + 1
        GROUPS = BLOCKS * NGRP
        U3 = U[:].rearrange("p (t w) -> p t w", t=NT)
        flats = {k: c[:].rearrange("p h t -> p (h t)")
                 for k, c in (("s", scol), ("s01", s01), ("d", dcol), ("d01", d01), ("flat", flat))}
        COLS = 5

        class Before:

            def __init__(self, h, b, start):
                self.number = h * BLOCKS if start else h * BLOCKS + b
                self.tiles = h * NT if start else h * NT + b * 4 - 2
                self.tile = NT - 2 if start else b * 4 - 4
                self.count = 2 if start else 4
                self.column = NP - TAIL if start else b * W - W
                self.width = TAIL if start else W
                self.next_head = h if start else h + 1
                self.groups = h * GROUPS if start else h * GROUPS + b * NGRP

        def over_heads(eng, one, start=None):
            with eng.Fori(0, HEADS) as h:
                if start:
                    start(h)
                one(h, 0, W, Before(h, 0, True))
                with eng.Fori(1, NB) as b:
                    one(h, b, W, Before(h, b, False))
                one(h, NB, TAIL, Before(h, NB, False))

        last = Before(HEADS, 0, True)

        def slot_of(g):
            return FIRST if g == 0 else (g - 1) % 4

        @block.sync
        def _(sp):
            for h in range(HEADS):
                sp.dma_start(weights[:, (h + 1) * 2 * D:(h + 2) * 2 * D].rearrange("p (c d) -> p c d", c=2),
                             io.w["L1"][:, h * D:(h + 1) * D].rearrange("(c p) d -> p c d", p=P)).then_inc(weights_in[h], 16)
            with sp.Fori(0, HEADS) as h:
                load_blocks(sp, io.adjT, ring, adj_in, released, h * GROUPS)

        @block.tensor
        def _(pe):
            def sums(w, g, before):
                slot = slot_of(g)
                pe.wait_ge(exp_ready, before.groups + g + 3)
                for u in range(2):
                    row = slice((g * 2 + u) * width, (g * 2 + u) * width + width - 1)
                    for q in range(w // P):
                        if g == 0 and u == 0 and q < before.count:
                            pe.wait_ge(stored, before.tiles + q + 1)
                        mm = pe.matmul(acc[q][:, 0:width - 1], p32[:, pslot(slot), u, q * P:(q + 1) * P], haug[:, row],
                                       start=(g == 0 and u == 0), stop=(g == NGRP - 1 and u == 1))
                mm.then_inc(summed, 1)

            def turn_tops(before):
                pe.wait_ge(turned_ready, before.tiles + 1)
                pe.wait_ge(released, before.groups + 5)
                for q in range(before.count):
                    mm = pe.matmul(psT[0][:, q * P:(q + 1) * P], top[:, cols(before.column + q * P, P)], m.identb[:],
                                   start=True, stop=True)
                mm.then_inc(tops_turned, 1)

            def rows(before):
                pe.wait_ge(diag_ready, before.number + 1)
                for k in range(2):
                    mm = pe.matmul(psT[k][:, 0:before.width], m.ones[:], diag[:, k, 0:before.width], start=True, stop=True)
                mm.then_inc(rows_done, 1)

            def turn(before, q):
                pe.wait_ge(staged, before.tiles + q + 1)
                for c in range(2):
                    mm = pe.transpose(psT[q % 2][:, c * P:(c + 1) * P], stage[:, q, c * P:(c + 1) * P], m.ident[:])
                mm.then_inc(transposed, 1)

            def product(before, q):
                pe.wait_ge(turned_ready, before.tiles + q + 2)
                for c in range(2):
                    mm = pe.matmul(psO[q % 2][:, 0:D], turned[:, q, c * P:(c + 1) * P],
                                   weights[:, cols((before.next_head * 2 + c) * D, D)], start=(c == 0), stop=(c == 1))
                mm.then_inc(product_done, 1)

            def first_pair_turned(before, rows_free):
                if rows_free:
                    pe.wait_ge(ab_ready, before.number * 2 + 2)
                for q in range(2):
                    turn(before, q)

            def first_pair_products(before):
                pe.wait_ge(x_done, before.tiles + 1)
                for q in range(2):
                    product(before, q)

            def one(h, b, w, before):
                turn_tops(before)
                for g in range(NGRP):
                    sums(w, g, before)
                    if g == 1:
                        rows(before)
                    if g == 5:
                        first_pair_turned(before, True)
                    if g == 7:
                        first_pair_products(before)
                        if before.count > 2:
                            pe.wait_ge(turned_ready, before.tiles + 3)
                            for q in range(2, 4):
                                turn(before, q)
                    if g == 9 and before.count > 2:
                        pe.wait_ge(x_done, before.tiles + 3)
                        for q in range(2, 4):
                            product(before, q)

            for h in range(HEADS):
                pe.wait_ge(weights_in[h], 16)
            pe.wait_ge(weights_cleared, 1)
            pe.wait_ge(four_ready, 1)
            for q in range(2):
                mm = pe.matmul(acc[q][:, 0:width - 1], m.ones[:], haug[:, 0:width - 1], start=True, stop=True)
            mm.then_inc(summed, 1)
            over_heads(pe, one)
            first_pair_turned(last, False)
            first_pair_products(last)

        @block.vector
        def _(dve):
            dve.memset(weights[:, 0:2 * D], 0.0).then_inc(weights_cleared, 1)
            dve.memset(haug[:].rearrange("p (t w) -> p t w", t=NT)[:, :, D], float(HEADS)).then_inc(four_ready, 1)
            dve.sem_inc(released, 5)
            dve.sem_inc(maxed, 2)
            dve.sem_inc(turned_ready, 1)
            dve.sem_inc(x_done, 1)
            dve.sem_inc(tops_turned, 1)

            def step(h, b, w, g, before):
                slot = slot_of(g)
                s = pslot(slot)
                n = before.groups + g
                at = cols(b * W, w)
                dve.wait_ge(slope_ready, n + 1)
                dve.wait_ge(exp_ready, n + 1)
                for u in range(2):
                    ins = dve.scalar_tensor_tensor(out=t[:, s, u, 0:w], in0=A[:, at],
                                                   scalar=own_d[:, g * 2 + u:g * 2 + u + 1], in1=slope[:, s, u, 0:w],
                                                   op0=ALU.add, op1=ALU.max)
                ins.then_inc(maxed, 1)
                if g > 0:
                    join(b, w, g - 1, n - 1)
                arrived(dve, adj_in, b, g, slot, h * BLOCKS)
                dve.wait_ge(maxed, n + 3)
                dve.tensor_tensor(t[:, s, :, 0:w], t[:, s, :, 0:w], ring[:, slot, :, 0:w], ALU.add).then_inc(added, 1)
                d_next = own_next[:, g * 2 + 1:g * 2 + 2]
                if g == 0:
                    dve.wait_ge(tops_turned, before.number + 1)
                    dve.tensor_scalar(top[:, at], ring[:, slot, 1, 0:w], d_next, None, ALU.add).then_inc(half_top, 1)
                else:
                    dve.wait_ge(released, n + 5)
                    dve.scalar_tensor_tensor(out=top[:, at], in0=ring[:, slot, 1, 0:w], scalar=d_next, in1=top[:, at],
                                             op0=ALU.add, op1=ALU.max).then_inc(half_top, 1)

            def join(b, w, g, n):
                at = cols(b * W, w)
                dve.wait_ge(cand_ready, n + 1)
                dve.wait_ge(half_top, n + 1)
                dve.tensor_tensor(top[:, at], top[:, at], cand[:, pslot(slot_of(g)), 0:w], ALU.max).then_inc(released, 1)

            def columns(before):
                dve.wait_ge(tops_turned, before.number + 2)
                n = before.number * COLS
                c = before.count
                at = cols(before.next_head * NT + before.tile, c)

                def done(ins, k):
                    ins.then_inc(col_steps, 1)
                    dve.wait_ge(col_steps, n + k)
                done(dve.tensor_reduce(topcol[:, 0:c], psT[0][:, 0:c * P].rearrange("p (q j) -> p q j", j=P), AX.X, ALU.max), 1)
                done(dve.tensor_tensor(topcol[:, 0:c], topcol[:, 0:c], flats["s"][:, at], ALU.add), 2)
                done(dve.tensor_tensor(topcol[:, 0:c], topcol[:, 0:c], flats["flat"][:, at], ALU.max), 3)
                dve.tensor_tensor(acol[:, 0:c], flats["s"][:, at], topcol[:, 0:c], ALU.subtract).then_inc(col_steps, 1)
                done(dve.tensor_tensor(bcol[:, 0:c], flats["s01"][:, at], topcol[:, 0:c], ALU.subtract), 5)
                for k, col in enumerate((acol, bcol)):
                    for q in range(c):
                        ins = dve.tensor_scalar(diag[:, k, q * P:(q + 1) * P], m.ident[:], col[:, q:q + 1], None, ALU.mult)
                ins.then_inc(diag_ready, 1)

            def shares(before):
                wait_apart(dve, stored, before.tiles + before.count, waited)
                dve.reciprocal(rz[:, 0:before.count], U3[:, cols(before.tile, before.count), D]).then_inc(rz_ready, 1)

            def keep_turned(before, q):
                dve.wait_ge(transposed, before.tiles + q + 1)
                dve.tensor_copy(turned[:, q, :], psT[q % 2][:, 0:D]).then_inc(turned_ready, 1)

            def into_x(before, q):
                dve.wait_ge(product_done, before.tiles + q + 1)
                at = cols((before.tile + q) * D, D)
                dve.tensor_tensor(m.x[:, at], m.x[:, at], psO[q % 2][:, 0:D], ALU.add).then_inc(x_done, 1)

            def one(h, b, w, before):
                for g in range(NGRP):
                    step(h, b, w, g, before)
                    if g == NGRP - 1:
                        join(b, w, g, before.groups + g)
                    if g == 2:
                        columns(before)
                    if g == 3:
                        shares(before)
                    if g == 8:
                        for q in range(2):
                            keep_turned(before, q)
                    if g == 10:
                        if before.count > 2:
                            for q in range(2, 4):
                                keep_turned(before, q)
                        for q in range(2):
                            into_x(before, q)
                    if g == 12 and before.count > 2:
                        for q in range(2, 4):
                            into_x(before, q)

            def start(h):
                wait_apart(dve, released, h * GROUPS + 5, waited)
                dve.tensor_copy(own_d[:], flats["d"][:, cols(h * NT, NT)]).then_inc(vector_cols, 1)
                dve.tensor_copy(own_next[:], flats["d"][:, cols(h * NT + NT, NT)]).then_inc(vector_cols, 1)
                wait_apart(dve, vector_cols, h * 2 + 2, waited)

            over_heads(dve, one, start)
            shares(last)
            for q in range(2):
                keep_turned(last, q)
            for q in range(2):
                into_x(last, q)

        @block.scalar
        def _(act):
            act.preload_act_table(ACT.Exp)
            act.sem_inc(exp_ready, 2)
            act.sem_inc(summed, 1)

            def slopes(h, b, w, g, n):
                s = pslot(slot_of(g))
                wait_apart(act, maxed, n + 1, waited)
                for u in range(2):
                    ins = act.activation(slope[:, s, u, 0:w], B[:, cols(b * W, w)], ACT.Identity,
                                         bias=flats["d01"][:, cols(h * NT + g * 2 + u, 1)] if g == 0 else
                                         own_d01[:, g * 2 + u:g * 2 + u + 1])
                ins.then_inc(slope_ready, 1)

            def candidates(h, b, w, g, n):
                slot = slot_of(g)
                arrived(act, adj_in, b, g, slot, h * BLOCKS)
                act.wait_ge(released, n + 4)
                act.activation(cand[:, pslot(slot), 0:w], ring[:, slot, 0, 0:w], ACT.Identity,
                               bias=own_candidate[:, g * 2:g * 2 + 1]).then_inc(cand_ready, 1)

            def exps(w, g, n):
                s = pslot(slot_of(g))
                act.wait_ge(added, n + 1)
                act.wait_ge(summed, n + 1)
                act.activation(p32[:, s, :, 0:w], t[:, s, :, 0:w], ACT.Exp).then_inc(exp_ready, 1)

            def keep_sums(before):
                wait_apart(act, summed, before.groups + 2, waited)
                for q in range(before.count):
                    act.copy(U3[:, cols(before.tile + q, 1), 0:width - 1].rearrange("p o w -> p (o w)"),
                             acc[q][:, 0:width - 1]).then_inc(stored, 1)

            def stages(before):
                wait_apart(act, rz_ready, before.number + 1, waited)
                for q in range(before.count):
                    act.activation(stage[:, q, :], U3[:, cols(before.tile + q, 1), 0:D].rearrange("p o w -> p (o w)"),
                                   ACT.Copy, scale=rz[:, q:q + 1]).then_inc(staged, 1)

            def keep_rows(before):
                wait_apart(act, rows_done, before.number + 1, waited)
                for k, row in enumerate((A, B)):
                    act.copy(row[:, cols(before.column, before.width)], psT[k][:, 0:before.width]).then_inc(ab_ready, 1)

            def one(h, b, w, before):
                n = before.groups
                candidates(h, b, w, 0, n)
                for g in range(NGRP):
                    if g + 1 < NGRP:
                        slopes(h, b, w, g + 1, n + g + 1)
                        candidates(h, b, w, g + 1, n + g + 1)
                    elif w == W:
                        slopes(h, b + 1, W, 0, n + NGRP)
                    else:
                        slopes(h + 1, 0, W, 0, n + NGRP)
                    if g == 1:
                        keep_sums(before)
                    exps(w, g, n + g)
                    if g == 4:
                        stages(before)
                    if g == 5:
                        keep_rows(before)

            def start(h):
                wait_apart(act, slope_ready, h * GROUPS + 1, waited)
                act.copy(own_d01[:], flats["d01"][:, cols(h * NT, NT)]).then_inc(scalar_cols, 1)
                act.copy(own_candidate[:], flats["d"][:, cols(h * NT + NT, NT)]).then_inc(scalar_cols, 1)
                wait_apart(act, scalar_cols, h * 2 + 2, waited)

            slopes(0, 0, W, 0, 0)
            over_heads(act, one, start)
            keep_sums(last)
            stages(last)


TOP = float(np.float32(1.0 - 1e-7))
EPS3 = 1e-10


def artanh_before(chain, dve, y, v, w):
    chain(dve.tensor_scalar(y, y, TOP, -TOP, ALU.min, ALU.max))
    chain(dve.tensor_scalar(w, y, -1.0, 1.0, ALU.mult, ALU.add))
    chain(dve.reciprocal(w, w))
    chain(dve.tensor_scalar(v, y, 1.0, None, ALU.add))
    chain(dve.tensor_tensor(v, v, w, ALU.mult))


def artanh_after(chain, dve, y, v, w, z):
    chain(dve.tensor_tensor(w, y, y, ALU.mult))
    chain(dve.tensor_scalar(z, w, 1.0 / 11, 1.0 / 9, ALU.mult, ALU.add))
    for k in (7, 5, 3, 1):
        chain(dve.tensor_tensor(z, z, w, ALU.mult))
        chain(dve.tensor_scalar(z, z, 1.0 / k, None, ALU.add))
    chain(dve.tensor_tensor(z, z, y, ALU.mult))
    chain(dve.scalar_tensor_tensor(out=v, in0=v, scalar=0.5, in1=z, op0=ALU.mult, op1=ALU.subtract))
    chain(dve.scalar_tensor_tensor(out=v, in0=y, scalar=0.125, in1=v, op0=ALU.is_ge, op1=ALU.mult))
    chain(dve.tensor_tensor(v, v, z, ALU.add))


def row_product(nc, m, name, src, src_width, ones, dst, weight):
    with ExitStack() as ctx:
        ps = [ctx.enter_context(nc.psum_tensor(f"{name}_ps{k}", [P, W], F32)) for k in range(4)]
        weight_in = nc.alloc_semaphore(f"{name}_weight_in")
        rp = RowProduct(ctx, nc, m, name, src, src_width, ones, dst, False, ps[0:2], ps[2:4])
        block = ctx.enter_context(nc.Block())

        @block.sync
        def _(sp):
            sp.dma_start(rp.w[:], weight.rearrange("(c p) d -> p c d", p=P)).then_inc(weight_in, 16)

        @block.vector
        def _(dve):
            rp.start_vector(dve)
            rp.vector(dve)

        @block.scalar
        def _(act):
            rp.start_scalar(act)
            rp.scalar(act)

        @block.tensor
        def _(pe):
            pe.wait_ge(weight_in, 16)
            rp.tensor(pe)


def square_sums(chain, dve, src, big, out):
    chain(dve.tensor_tensor(big, src, src, ALU.mult))
    chain(dve.tensor_reduce(out, big, AX.X, ALU.add))


def hyper_points(nc, name, haug, mx, gaug):
    with ExitStack() as ctx:
        def col(n):
            return ctx.enter_context(nc.sbuf_tensor(f"{name}_{n}", [P, NT], F32))[:]

        def sem(n):
            return nc.alloc_semaphore(f"{name}_{n}")

        hh, mm, xn, mn, live, v, w, z, f = (col(n) for n in ("hh", "mm", "xn", "mn", "live", "v", "w", "z", "f"))
        steps, sums_ready, roots_ready, log_in, log_out, tanh_in, tanh_out = (
            sem("steps"), sem("sums_ready"), sem("roots_ready"), sem("log_in"), sem("log_out"), sem("tanh_in"), sem("tanh_out"))
        h3 = haug[:].rearrange("p (t w) -> p t w", t=NT)
        g3 = gaug[:].rearrange("p (t w) -> p t w", t=NT)
        mx3 = mx[:].rearrange("p (t d) -> p t d", t=NT)
        block = ctx.enter_context(nc.Block())

        @block.vector
        def _(dve):
            chain = Chain(dve, steps)
            square_sums(chain, dve, h3[:, :, 0:D], g3[:, :, 0:D], hh)
            square_sums(chain, dve, mx3, g3[:, :, 0:D], mm)
            chain(dve.tensor_scalar(live, mm, EPS3 * EPS3, None, ALU.is_gt))
            chain(dve.tensor_scalar(hh, hh, EPS3 * EPS3, None, ALU.max))
            dve.tensor_scalar(mm, mm, EPS3 * EPS3, None, ALU.max).then_inc(sums_ready, 1)
            dve.wait_ge(roots_ready, 2)
            chain(dve.reciprocal(f, xn))
            chain(dve.tensor_tensor(f, f, mn, ALU.mult))
            artanh_before(chain, dve, xn, v, w)
            dve.sem_inc(log_in, 1)
            dve.wait_ge(log_out, 1)
            artanh_after(chain, dve, xn, v, w, z)
            chain(dve.tensor_tensor(v, v, f, ALU.mult))
            dve.sem_inc(tanh_in, 1)
            dve.wait_ge(tanh_out, 1)
            chain(dve.tensor_tensor(v, v, live, ALU.mult))
            chain(dve.tensor_tensor(w, v, v, ALU.mult))
            chain(dve.tensor_scalar(w, w, -1.0, 1.0, ALU.mult, ALU.add))
            chain(dve.reciprocal(w, w))
            chain(dve.tensor_scalar(w, w, 2.0, 1e-15, ALU.mult, ALU.max))
            chain(dve.tensor_scalar(g3[:, :, D], w, -1.0, None, ALU.add))
            chain(dve.memset(g3[:, :, D + 1], 1.0))
            chain(dve.reciprocal(f, mn))
            chain(dve.tensor_tensor(f, f, v, ALU.mult))
            chain(dve.tensor_tensor(f, f, w, ALU.mult))
            chain(dve.tensor_tensor(g3[:, :, 0:D], mx3, f.rearrange("p (t o) -> p t o", o=1).to_broadcast([P, NT, D]), ALU.mult))

        @block.scalar
        def _(act):
            act.wait_ge(sums_ready, 1)
            act.activation(xn, hh, ACT.Sqrt).then_inc(roots_ready, 1)
            act.activation(mn, mm, ACT.Sqrt).then_inc(roots_ready, 1)
            act.wait_ge(log_in, 1)
            act.activation(v, v, ACT.Ln).then_inc(log_out, 1)
            act.wait_ge(tanh_in, 1)
            act.activation(v, v, ACT.Tanh).then_inc(tanh_out, 1)


def mean_sums(nc, name, adjT, gaug, U):
    width = D + 2
    with ExitStack() as ctx:
        def sem(n):
            return nc.alloc_semaphore(f"{name}_{n}")

        ring = ctx.enter_context(nc.sbuf_tensor(f"{name}_ring", [P, 5, 2, W], F32))
        acc = [ctx.enter_context(nc.psum_tensor(f"{name}_acc{k}", [P, W], F32)) for k in range(8)]
        adj_in = [sem(f"adj_in{k}") for k in range(5)]
        summed, stored = sem("summed"), sem("stored")
        block = ctx.enter_context(nc.Block())

        @block.sync
        def _(sp):
            load_blocks(sp, adjT, ring, adj_in, summed, 0)

        @block.tensor
        def _(pe):
            def sums(b, w, g, slot, first, last):
                arrived(pe, adj_in, b, g, slot)
                for u in range(2):
                    for q in range(w // P):
                        if first and u == 0:
                            pe.wait_ge(stored, b * 4 + q + 1)
                        mm = pe.matmul(acc[q][:, 0:width], ring[:, slot, u, q * P:(q + 1) * P],
                                       gaug[:, cols(g * 2 * width + u * width, width)],
                                       start=(first and u == 0), stop=(last and u == 1))
                mm.then_inc(summed, 1)

            def one(b, w, next_w):
                sums(b, w, 0, FIRST, True, False)
                later = NGRP // 4
                with pe.Fori(0, later - 1) as i:
                    for u in range(4):
                        sums(b, w, i * 4 + u + 1, u, False, False)
                for u in range(4):
                    g = (later - 1) * 4 + u + 1
                    sums(b, w, g, u, False, g == NGRP - 1)
            over_blocks(pe, one)

        @block.vector
        def _(dve):
            dve.sem_inc(summed, 5)
            dve.sem_inc(stored, 4)

            def one(b, w, next_w):
                dve.wait_ge(summed, b * NGRP + NGRP + 5)
                for q in range(w // P):
                    dve.tensor_copy(U[:, cols(b * 4 * width + q * width, width)], acc[q][:, 0:width]).then_inc(stored, 1)
            over_blocks(dve, one)


def hyper_mean(nc, m, name, U, big):
    with ExitStack() as ctx:
        def col(n):
            return ctx.enter_context(nc.sbuf_tensor(f"{name}_{n}", [P, NT], F32))[:]

        def sem(n):
            return nc.alloc_semaphore(f"{name}_{n}")

        ss, d, k, q, y, v, w, z = (col(n) for n in ("ss", "d", "k", "q", "y", "v", "w", "z"))
        steps, root_in, root_out, log_in, log_out, tanh_in, tanh_out = (
            sem("steps"), sem("root_in"), sem("root_out"), sem("log_in"), sem("log_out"), sem("tanh_in"), sem("tanh_out"))
        U3 = U[:].rearrange("p (t w) -> p t w", t=NT)
        big3 = big[:].rearrange("p (t d) -> p t d", t=NT)
        x3 = m.x[:].rearrange("p (t d) -> p t d", t=NT)
        nom, den, alpha = U3[:, :, 0:D], U3[:, :, D], U3[:, :, D + 1]

        def wide(c):
            return c.rearrange("p (t o) -> p t o", o=1).to_broadcast([P, NT, D])
        block = ctx.enter_context(nc.Block())

        @block.vector
        def _(dve):
            chain = Chain(dve, steps)

            def norm_of(factor, squares, number):
                if factor is not None:
                    chain(dve.tensor_tensor(y, factor, factor, ALU.mult))
                    chain(dve.tensor_tensor(y, y, squares, ALU.mult))
                    chain(dve.tensor_scalar(y, y, EPS3 * EPS3, None, ALU.max))
                else:
                    chain(dve.tensor_scalar(y, squares, EPS3 * EPS3, None, ALU.max))
                dve.sem_inc(root_in, 1)
                dve.wait_ge(root_out, number)

            square_sums(chain, dve, nom, big3, ss)
            chain(dve.tensor_scalar(d, den, 0.0, 2.0, ALU.is_ge, ALU.mult))
            chain(dve.tensor_scalar(d, d, -1.0, None, ALU.add))
            chain(dve.tensor_tensor(v, d, den, ALU.mult))
            chain(dve.tensor_scalar(v, v, EPS3, None, ALU.max))
            chain(dve.tensor_tensor(d, d, v, ALU.mult))
            chain(dve.reciprocal(d, d))
            chain(dve.tensor_tensor(y, d, d, ALU.mult))
            chain(dve.tensor_tensor(y, y, ss, ALU.mult))
            chain(dve.tensor_scalar(y, y, -1.0, 1.0, ALU.mult, ALU.add))
            chain(dve.tensor_scalar(y, y, EPS3, None, ALU.max))
            dve.sem_inc(root_in, 1)
            dve.wait_ge(root_out, 1)
            chain(dve.tensor_scalar(y, y, 1.0, None, ALU.add))
            chain(dve.reciprocal(y, y))
            chain(dve.tensor_tensor(k, d, y, ALU.mult))
            norm_of(k, ss, 2)
            chain(dve.reciprocal(q, y))
            chain(dve.tensor_tensor(k, k, q, ALU.mult))
            artanh_before(chain, dve, y, v, w)
            dve.sem_inc(log_in, 1)
            dve.wait_ge(log_out, 1)
            artanh_after(chain, dve, y, v, w, z)
            chain(dve.tensor_tensor(v, v, alpha, ALU.mult))
            dve.sem_inc(tanh_in, 1)
            dve.wait_ge(tanh_out, 1)
            chain(dve.tensor_tensor(k, k, v, ALU.mult))
            norm_of(k, ss, 3)
            chain(dve.reciprocal(q, y))
            chain(dve.tensor_tensor(k, k, q, ALU.mult))
            artanh_before(chain, dve, y, v, w)
            dve.sem_inc(log_in, 1)
            dve.wait_ge(log_out, 2)
            artanh_after(chain, dve, y, v, w, z)
            chain(dve.tensor_tensor(k, k, v, ALU.mult))
            chain(dve.tensor_tensor(nom, nom, wide(k), ALU.mult))
            chain(dve.tensor_scalar(nom, nom, 0.0, None, ALU.max))
            square_sums(chain, dve, nom, big3, ss)
            norm_of(None, ss, 4)
            chain(dve.reciprocal(q, y))
            chain(dve.tensor_copy(v, y))
            dve.sem_inc(tanh_in, 1)
            dve.wait_ge(tanh_out, 2)
            chain(dve.tensor_tensor(q, q, v, ALU.mult))
            chain(dve.tensor_tensor(nom, nom, wide(q), ALU.mult))
            chain(dve.tensor_tensor(x3, x3, nom, ALU.add))

        @block.scalar
        def _(act):
            def root(n):
                act.wait_ge(root_in, n)
                act.activation(y, y, ACT.Sqrt).then_inc(root_out, 1)

            def log(n):
                act.wait_ge(log_in, n)
                act.activation(v, v, ACT.Ln).then_inc(log_out, 1)

            def tanh(n):
                act.wait_ge(tanh_in, n)
                act.activation(v, v, ACT.Tanh).then_inc(tanh_out, 1)

            root(1)
            root(2)
            log(1)
            tanh(1)
            root(3)
            log(2)
            root(4)
            tanh(2)


def store(nc, m, out):
    body_out, last_out = nc.alloc_semaphore("body_out"), nc.alloc_semaphore("last_out")
    with nc.Block() as block:
        @block.sync
        def _(sp):
            xt = m.x[:].rearrange("p (t d) -> p t d", t=NT)
            sp.dma_start(out[0:(NT - 1) * P, :].rearrange("(t p) d -> p t d", p=P), xt[:, 0:NT - 1, :]).then_inc(body_out, 16)
            sp.dma_start(out[(NT - 1) * P:N, :], xt[0:N - (NT - 1) * P, NT - 1, :]).then_inc(last_out, 16)
            sp.wait_ge(body_out, 16)
            sp.wait_ge(last_out, 16)


class Io:
    pass


def attention_layer(nc, m, io, name, graphs, edge=None):
    with nc.cleanup_on_exit(), ExitStack() as layer:
        def sb(n, s, d=F32):
            return layer.enter_context(nc.sbuf_tensor(f"{name}_{n}", s, d))

        hh = sb("hh", [P, NT * (D + 2)], F16)
        hl = sb("hl", [P, NT * (D + 2)], F16)
        negm = sb("negm", [P, NT])
        zoff = sb("zoff", [P, NT]) if graphs else None
        q_parts = (sb("qh", [P, 2 * NQ], F16), sb("ql", [P, 2 * NQ], F16))
        k_parts = (sb("kh", [P, 2 * NP], F16), sb("kl", [P, 2 * NP], F16))
        augI = sb("augI", [P, NQ], BF16)
        augJ = sb("augJ", [P, NP], BF16)
        with nc.sbuf_tensor(f"{name}_notJ", [P, NP], BF16) as notJ:
            if graphs:
                aug_graphs(nc, name, io.ptr, augI, augJ, notJ, q_parts)
            with nc.sbuf_tensor(f"{name}_hT", [P, 2 * NP], F32) as m.hT:
                norm(nc, m, f"{name}_norm", True, hh, hl, m.x_in if graphs else ())
                queries_keys(nc, m, f"{name}_qk", io.w[name + "q"], io.w[name + "k"], io.b[name + "q"],
                             io.b[name + "k"], q_parts, k_parts)
            row_max(nc, f"{name}_max", io.adj, q_parts, k_parts[0], graphs, augI, augJ, notJ, negm, zoff)
        shift = None
        if graphs:
            shift_rows(nc, f"{name}_shift", m.identb, negm, io.shift_rows, augI)
        else:
            shift = sb("shift", [P, NQ])
            shift_everywhere(nc, f"{name}_shift", m.ident, negm, io.shift_row, shift)
        U = sb("U", [P, NT * (D + 2)])
        attend(nc, f"{name}_att", io.adjT, q_parts, k_parts, augI, augJ, hh, hl, U, edge, shift)
        project(nc, m, f"{name}_out", U, io.w[name + "v"], io.b[name + "v"], zoff)


def gat_layer(nc, m, io, edge):
    with nc.cleanup_on_exit(), ExitStack() as layer:
        def sb(n, s, d=F32):
            return layer.enter_context(nc.sbuf_tensor(f"L1_{n}", s, d))

        haug = sb("haug", [P, NT * (D + 2)])
        scol, s01, dcol, d01, flat = (sb(n, [P, HEADS + 1, NT]) for n in ("scol", "s01", "dcol", "d01", "flat"))
        top = sb("top", [P, NP], BF16)
        A = sb("A", [P, NQ])
        B = sb("B", [P, NQ])
        with nc.sbuf_tensor("L1_hT", [P, 2 * NP], F32) as m.hT:
            norm(nc, m, "L1_norm", False, haug, None)
            gat_vectors(nc, m, "L1_vec", io, scol, dcol, d01)
        gat_tops(nc, "L1_tops", io.adjT, dcol, top)
        gat_shifts(nc, m, "L1_shifts", scol, s01, dcol, top, edge, flat, A, B)
        gat(nc, m, "L1_gat", io, scol, s01, dcol, d01, flat, top, A, B, haug)


def hyper_layer(nc, m, io):
    with nc.cleanup_on_exit(), ExitStack() as layer:
        def sb(n, s, d=F32):
            return layer.enter_context(nc.sbuf_tensor(f"L3_{n}", s, d))

        gaug = sb("gaug", [P, NT * (D + 2)])
        with nc.sbuf_tensor("L3_haug", [P, NT * (D + 2)], F32) as haug, \
                nc.sbuf_tensor("L3_mx", [P, NT * D], F32) as mx:
            with nc.sbuf_tensor("L3_hT", [P, 2 * NP], F32) as m.hT:
                norm(nc, m, "L3_norm", False, haug, None)
            row_product(nc, m, "L3_mx", haug, D + 2, m.ones, mx, io.w["L3"])
            hyper_points(nc, "L3_points", haug, mx, gaug)
        U = sb("U", [P, NT * (D + 2)])
        big = sb("big", [P, NT * D])
        mean_sums(nc, "L3_mean", io.adjT, gaug, U)
        hyper_mean(nc, m, "L3_out", U, big)


def program(nc, io):
    with ExitStack() as ctx:
        m = Mem()
        setup(nc, ctx, m, io)
        with nc.sbuf_tensor("edge", [P, NQ], BF16) as edge:
            attention_layer(nc, m, io, "L0", True, edge)
            gat_layer(nc, m, io, edge)
        attention_layer(nc, m, io, "L2", False)
        hyper_layer(nc, m, io)
        store(nc, m, io.out)


def kernel(**inputs):
    import concourse.bacc as bacc
    from concourse.bass_utils import run_bass_kernel_spmd as run

    nc = bacc.Bacc("TRN2", target_bir_lowering=False, num_devices=1)
    arrays = {}

    def given(name, array):
        array = np.ascontiguousarray(array)
        arrays[name] = array
        return nc.dram_tensor(name, array.shape, mybir.dt.from_np(array.dtype), kind="ExternalInput").ap()

    adj = np.asarray(inputs["adj"])
    pad = ((0, NP - N), (0, NP - N))
    io = Io()
    io.x = given("x", inputs["x"])
    io.adj = given("adj_padded", np.pad(adj, pad))
    io.adjT = given("adj_transposed", np.pad(adj.T, pad))
    io.ptr = given("ptr", np.asarray(inputs["L0_gnn_ptr"]).reshape(NG, 1))
    io.w, io.b = {}, {}
    for layer in ("L0", "L2"):
        for k in "qkv":
            io.w[layer + k] = given(f"{layer}_W{k}_transposed", np.asarray(inputs[f"{layer}_gnn_W{k}"]).T)
            b = np.asarray(inputs[f"{layer}_gnn_b{k}"])
            io.b[layer + k] = given(f"{layer}_b{k}", b if k == "v" else b.reshape(2, P).T)
    io.w["L1"] = given("L1_W", inputs["L1_gnn_W"])
    io.w["L1T"] = given("L1_W_transposed", np.asarray(inputs["L1_gnn_W"]).T)
    io.a = given("L1_a", np.asarray(inputs["L1_gnn_a"]).reshape(HEADS, 2, 2, P).transpose(3, 0, 2, 1))
    io.w["L3"] = given("L3_W", inputs["L3_gnn_W"])
    io.out = nc.dram_tensor("out", (N, D), F32, kind="ExternalOutput").ap()
    io.shift_rows = nc.dram_tensor("shift_rows", (3, NP), BF16, kind="Internal").ap()
    io.shift_row = nc.dram_tensor("shift_row", (NP,), F32, kind="Internal").ap()
    program(nc, io)
    return run(nc, [arrays], core_ids=[0]).results[0]["out"]
```
